# Optimizing a Trainium2 kernel written in Bass

```python
import numpy as np
import jax
import jax.numpy as jnp

def _softmax(x, axis=-1):
    return jax.nn.softmax(x, axis=axis)

def _gelu(x):
    return jax.nn.gelu(x, approximate=True)

def _silu(x):
    return jax.nn.silu(x)

def _sigmoid(x):
    return jax.nn.sigmoid(x)

def _layernorm(x, axis=-1, eps=1e-05):
    m = jnp.mean(x, axis=axis, keepdims=True)
    v = jnp.var(x, axis=axis, keepdims=True)
    return (x - m) / jnp.sqrt(v + eps)

def _scatter_add(tgt, idx, src, axis=0):
    return tgt.at[idx].add(src)

def _segment_sum(src, seg, n):
    return jax.ops.segment_sum(src, seg, n)
kernel_name = 'mk_adj_resnorm_d4_adj_r2_cc016d'

def setup_inputs(seed: int=0):
    np.random.seed(seed)
    _w = jnp.asarray

    def _rec_inputs():
        import jax
        import jax.numpy as jnp
        _gk = jax.random.key(seed)
        x = 7.34e-05 + 1 * jax.random.normal(jax.random.fold_in(_gk, 1), (64, 128, 256), jnp.float32)
        _a = jax.random.bernoulli(jax.random.fold_in(_gk, 2), 0.015625, (128, 128))
        _a = jnp.logical_or(_a, jnp.swapaxes(_a, -1, -2))
        _a = jnp.logical_or(_a, jnp.eye(128, dtype=bool))
        _af = _a.astype(jnp.float32)
        adj = _af
        return (x, adj)
    x, adj = _rec_inputs()

    def _L0_gnn_setup():
        import jax, jax.numpy as jnp
        import numpy as np
        B, N, D, H = (16, 1025, 256, 8)
        LN_EPS = 1e-05

        def _make_mask(key, n):
            n_proto = n - 1
            adj = jax.random.bernoulli(key, 0.03, (n_proto, n_proto)).astype(jnp.float32)
            adj = jnp.clip(adj + adj.T + jnp.eye(n_proto, dtype=jnp.float32), 0.0, 1.0)
            mask = jnp.zeros((n, n), dtype=jnp.float32)
            mask = mask.at[0, :].set(1.0).at[:, 0].set(1.0)
            mask = mask.at[1:, 1:].set(adj)
            return mask
        key = jax.random.key(seed)
        ks = jax.random.split(key, 7)
        s = 1.0 / np.sqrt(D)
        return {'x': jax.random.normal(ks[0], (B, N, D), dtype=jnp.float32), 'w_qkv': jax.random.uniform(ks[1], (D, 3 * D), dtype=jnp.float32, minval=-s, maxval=s), 'w_proj': jax.random.uniform(ks[2], (D, D), dtype=jnp.float32, minval=-s, maxval=s), 'b_proj': jnp.zeros((D,), dtype=jnp.float32), 'ln_gamma': jnp.ones((D,), dtype=jnp.float32), 'ln_beta': jnp.zeros((D,), dtype=jnp.float32), 'attn_mask': _make_mask(ks[3], N)}
    _L0_gnn_all = _L0_gnn_setup()
    _L0_gnn_in = {k: v for k, v in _L0_gnn_all.items() if k in ('w_qkv', 'w_proj', 'b_proj', 'ln_gamma', 'ln_beta')}
    del _L0_gnn_all

    def _L1_gnn_setup():
        import jax, jax.numpy as jnp
        import numpy as np
        B, N, D, T = (64, 128, 256, 3)

        def _lin(v, W, b):
            return jnp.einsum('...i,oi->...o', v, W) + b
        key = jax.random.key(seed)
        ks = jax.random.split(key, 12)
        s2 = 1.0 / np.sqrt(2 * D)
        s1 = 1.0 / np.sqrt(D)
        return {'x': jax.random.normal(ks[0], (B, N, D), jnp.float32), 'in_mat': jax.random.uniform(ks[1], (N, N), jnp.float32) / N, 'out_mat': jax.random.uniform(ks[2], (N, N), jnp.float32) / N, 'w3_w': jax.random.normal(ks[3], (D, 2 * D), jnp.float32) * s2, 'w3_b': jnp.zeros((D,), jnp.float32), 'u3_w': jax.random.normal(ks[4], (D, D), jnp.float32) * s1, 'u3_b': jnp.zeros((D,), jnp.float32), 'w4_w': jax.random.normal(ks[5], (D, 2 * D), jnp.float32) * s2, 'w4_b': jnp.zeros((D,), jnp.float32), 'w5_w': jax.random.normal(ks[6], (D, 2 * D), jnp.float32) * s2, 'w5_b': jnp.zeros((D,), jnp.float32), 'u5_w': jax.random.normal(ks[7], (D, D), jnp.float32) * s1, 'u5_b': jnp.zeros((D,), jnp.float32)}
    _L1_gnn_all = _L1_gnn_setup()
    _L1_gnn_in = {k: v for k, v in _L1_gnn_all.items() if k in ('w3_w', 'w3_b', 'u3_w', 'u3_b', 'w4_w', 'w4_b', 'w5_w', 'w5_b', 'u5_w', 'u5_b')}
    del _L1_gnn_all

    def _L2_gnn_setup():
        import jax, jax.numpy as jnp
        import numpy as np
        ALPHA = 0.2
        key = jax.random.key(seed)
        k0, k1, k2, k3 = jax.random.split(key, 4)
        B, N, C, F = (64, 512, 256, 256)
        x = jax.random.normal(k0, (B, N, C), dtype=jnp.float32)
        W = jax.random.normal(k1, (C, F), dtype=jnp.float32) * (1.414 / np.sqrt(C + F))
        a = jax.random.normal(k2, (2 * F, 1), dtype=jnp.float32) * (1.414 / np.sqrt(2 * F + 1))
        beta = jnp.ones((1,), dtype=jnp.float32)
        mask = (jax.random.uniform(k3, (N, N)) < 0.3).astype(jnp.float32)
        return {'x': x, 'W': W, 'a': a, 'beta': beta, 'mask': mask}
    _L2_gnn_all = _L2_gnn_setup()
    _L2_gnn_in = {k: v for k, v in _L2_gnn_all.items() if k in ('W', 'a', 'beta')}
    del _L2_gnn_all

    def _L3_gnn_setup():
        import jax, jax.numpy as jnp
        import numpy as np
        B, N, D = (8, 1024, 256)
        key = jax.random.key(seed)
        k1, k2, k3, k4, k5 = jax.random.split(key, 5)
        neuron_states = jax.random.normal(k1, (B, N, D), dtype=jnp.float32)
        adjacency = jax.random.randint(k2, (N, N), 0, 2).astype(jnp.float32)
        scale = 1.0 / np.sqrt(D)
        Wq = jax.random.normal(k3, (D, D), dtype=jnp.float32) * scale
        Wk = jax.random.normal(k4, (D, D), dtype=jnp.float32) * scale
        Wv = jax.random.normal(k5, (D, D), dtype=jnp.float32) * scale
        return {'neuron_states': neuron_states, 'adjacency': adjacency, 'Wq': Wq, 'Wk': Wk, 'Wv': Wv}
    _L3_gnn_all = _L3_gnn_setup()
    _L3_gnn_in = {k: v for k, v in _L3_gnn_all.items() if k in ('Wq', 'Wk', 'Wv')}
    del _L3_gnn_all
    return {'x': x, 'adj': adj, 'L0_gnn_w_qkv': _L0_gnn_in['w_qkv'], 'L0_gnn_w_proj': _L0_gnn_in['w_proj'], 'L0_gnn_b_proj': _L0_gnn_in['b_proj'], 'L0_gnn_ln_gamma': _L0_gnn_in['ln_gamma'], 'L0_gnn_ln_beta': _L0_gnn_in['ln_beta'], 'L1_gnn_w3_w': _L1_gnn_in['w3_w'], 'L1_gnn_w3_b': _L1_gnn_in['w3_b'], 'L1_gnn_u3_w': _L1_gnn_in['u3_w'], 'L1_gnn_u3_b': _L1_gnn_in['u3_b'], 'L1_gnn_w4_w': _L1_gnn_in['w4_w'], 'L1_gnn_w4_b': _L1_gnn_in['w4_b'], 'L1_gnn_w5_w': _L1_gnn_in['w5_w'], 'L1_gnn_w5_b': _L1_gnn_in['w5_b'], 'L1_gnn_u5_w': _L1_gnn_in['u5_w'], 'L1_gnn_u5_b': _L1_gnn_in['u5_b'], 'L2_gnn_W': _L2_gnn_in['W'], 'L2_gnn_a': _L2_gnn_in['a'], 'L2_gnn_beta': _L2_gnn_in['beta'], 'L3_gnn_Wq': _L3_gnn_in['Wq'], 'L3_gnn_Wk': _L3_gnn_in['Wk'], 'L3_gnn_Wv': _L3_gnn_in['Wv']}

def reference(x, adj, L0_gnn_w_qkv, L0_gnn_w_proj, L0_gnn_b_proj, L0_gnn_ln_gamma, L0_gnn_ln_beta, L1_gnn_w3_w, L1_gnn_w3_b, L1_gnn_u3_w, L1_gnn_u3_b, L1_gnn_w4_w, L1_gnn_w4_b, L1_gnn_w5_w, L1_gnn_w5_b, L1_gnn_u5_w, L1_gnn_u5_b, L2_gnn_W, L2_gnn_a, L2_gnn_beta, L3_gnn_Wq, L3_gnn_Wk, L3_gnn_Wv):
    import jax
    import jax.numpy as jnp

    def _L0_gnn_ref(x, w_qkv, w_proj, b_proj, ln_gamma, ln_beta, attn_mask):
        import jax, jax.numpy as jnp
        import numpy as np
        B, N, D, H = (16, 1025, 256, 8)
        LN_EPS = 1e-05

        def _make_mask(key, n):
            n_proto = n - 1
            adj = jax.random.bernoulli(key, 0.03, (n_proto, n_proto)).astype(jnp.float32)
            adj = jnp.clip(adj + adj.T + jnp.eye(n_proto, dtype=jnp.float32), 0.0, 1.0)
            mask = jnp.zeros((n, n), dtype=jnp.float32)
            mask = mask.at[0, :].set(1.0).at[:, 0].set(1.0)
            mask = mask.at[1:, 1:].set(adj)
            return mask
        b, n, d = x.shape
        hd = d // H
        scale = hd ** (-0.5)
        qkv = (x @ w_qkv).reshape(b, n, 3, H, hd).transpose(2, 0, 3, 1, 4)
        q, k, v = (qkv[0], qkv[1], qkv[2])
        attn = jnp.einsum('bhnd,bhmd->bhnm', q, k) * scale
        attn = jnp.where(attn_mask[None, None] == 0, -jnp.inf, attn)
        attn = jax.nn.softmax(attn, axis=-1)
        o = jnp.einsum('bhnm,bhmd->bhnd', attn, v).transpose(0, 2, 1, 3).reshape(b, n, d)
        o = o @ w_proj + b_proj
        mu = jnp.mean(o, axis=-1, keepdims=True)
        var = jnp.mean(jnp.square(o - mu), axis=-1, keepdims=True)
        ln = (o - mu) * jax.lax.rsqrt(var + LN_EPS) * ln_gamma + ln_beta
        return o + ln

    def _L1_gnn_ref(x, in_mat, out_mat, w3_w, w3_b, u3_w, u3_b, w4_w, w4_b, w5_w, w5_b, u5_w, u5_b):
        import jax, jax.numpy as jnp
        import numpy as np
        B, N, D, T = (64, 128, 256, 3)

        def _lin(v, W, b):
            return jnp.einsum('...i,oi->...o', v, W) + b
        h = x
        for _ in range(T):
            a_in = jnp.einsum('nm,bmd->bnd', in_mat, h)
            a_out = jnp.einsum('nm,bmd->bnd', out_mat, h)
            av = jnp.concatenate([a_in, a_out], axis=-1)
            z = jax.nn.sigmoid(_lin(av, w3_w, w3_b) + _lin(h, u3_w, u3_b))
            r = jax.nn.sigmoid(_lin(av, w4_w, w4_b) + _lin(h, u3_w, u3_b))
            hv = jnp.tanh(_lin(av, w5_w, w5_b) + _lin(r * h, u5_w, u5_b))
            h = (1.0 - z) * h + z * hv
        return h

    def _L2_gnn_ref(x, W, a, beta, mask):
        import jax, jax.numpy as jnp
        import numpy as np
        ALPHA = 0.2
        F_ = W.shape[1]
        h = jnp.einsum('bnc,cf->bnf', x, W)
        a1, a2 = (a[:F_, 0], a[F_:, 0])
        s1 = jnp.einsum('bnf,f->bn', h, a1)
        s2 = jnp.einsum('bnf,f->bn', h, a2)
        e = jax.nn.leaky_relu(s1[:, :, None] + s2[:, None, :], negative_slope=ALPHA)
        e = e * mask[None, :, :]
        att = jax.nn.softmax(e, axis=2)
        h_prime = jnp.einsum('bij,bjf->bif', att, h)
        return jax.nn.elu(h_prime + beta * h)

    def _L3_gnn_ref(neuron_states, adjacency, Wq, Wk, Wv):
        import jax, jax.numpy as jnp
        import numpy as np
        B, N, D = (8, 1024, 256)
        q = jnp.einsum('bnd,ed->bne', neuron_states, Wq)
        k = jnp.einsum('bnd,ed->bne', neuron_states, Wk)
        v = jnp.einsum('bnd,ed->bne', neuron_states, Wv)
        rel = jnp.einsum('bnd,bmd->bnm', q, k)
        rel = adjacency.T[None, :, :] * rel
        rel = rel / jnp.linalg.norm(rel, axis=2, keepdims=True)
        return jnp.einsum('bnm,bmd->bnd', rel, v)
    x = _layernorm(x + _L0_gnn_ref(x, L0_gnn_w_qkv, L0_gnn_w_proj, L0_gnn_b_proj, L0_gnn_ln_gamma, L0_gnn_ln_beta, adj), axis=-1)
    x = _layernorm(x + _L1_gnn_ref(x, adj, adj, L1_gnn_w3_w, L1_gnn_w3_b, L1_gnn_u3_w, L1_gnn_u3_b, L1_gnn_w4_w, L1_gnn_w4_b, L1_gnn_w5_w, L1_gnn_w5_b, L1_gnn_u5_w, L1_gnn_u5_b), axis=-1)
    x = _layernorm(x + _L2_gnn_ref(x, L2_gnn_W, L2_gnn_a, L2_gnn_beta, adj), axis=-1)
    x = _layernorm(x + _L3_gnn_ref(x, adj, L3_gnn_Wq, L3_gnn_Wk, L3_gnn_Wv), axis=-1)
    return x

_drawn_inputs = setup_inputs


def setup_inputs(seed=0):
    import zlib

    import numpy as np

    out = dict(_drawn_inputs(seed))
    spreads = {'L0_gnn_b_proj': (0.0, 0.1),
     'L0_gnn_ln_gamma': (1.0, 0.2),
     'L0_gnn_ln_beta': (0.0, 0.1),
     'L1_gnn_w3_b': (0.0, 0.1),
     'L1_gnn_u3_b': (0.0, 0.1),
     'L1_gnn_w4_b': (0.0, 0.8),
     'L1_gnn_w5_b': (0.0, 0.1),
     'L1_gnn_u5_b': (0.0, 0.1)}
    factors = {}
    for name, (base, spread) in spreads.items():
        noise = np.random.default_rng([zlib.crc32(name.encode()), seed]).standard_normal(out[name].shape)
        drawn = base * np.exp(spread * noise) if base else spread * noise
        out[name] = jnp.asarray(drawn.astype(out[name].dtype))
    for name, factor in factors.items():
        out[name] = (out[name] * factor).astype(out[name].dtype)
    return out
```

```python
from contextlib import ExitStack

import concourse.bass as bass
from concourse import mybir

F32 = mybir.dt.float32
F32R = mybir.dt.float32r
F16 = mybir.dt.float16
ALU = mybir.AluOpType
ACT = mybir.ActivationFunctionType
AX_X = mybir.AxisListType.X

P = 128
HEADS = 8
LN_EPS = 1e-5
ALPHA = 0.2
STEPS = 3
GR = 4
GROUPS = (0, 1)
FAR = -30000.0

W3, W4, W5, U3, U5, WM, WV = range(7)


class Signal:

    def __init__(self, ctx, nc, name, per_trip, credit):
        self.sems = [ctx.enter_context(nc.semaphore(f"{name}_{g}")) for g in GROUPS]
        self.per_trip, self.credit = per_trip, credit

    def __getitem__(self, g):
        return self.sems[g]

    def at(self, trip, k):
        return trip * self.per_trip + (k + self.credit)


def gnn_stack_kernel(nc, x, adj, w_qkv, w_proj, b_proj, ln_gamma, ln_beta, w3_w, w3_b, u3_w, u3_b, w4_w, w4_b,
                     w5_w, w5_b, u5_w, u5_b, gat_w, gat_a, gat_beta, wq, wk, wv, out):
    B, N, D = x.shape
    HD = D // HEADS
    SCALE = float(HD) ** -0.5
    KC = D // P
    TRIPS = B // (GR * len(GROUPS))
    COLS = GR * N
    HW = HD + 1
    assert N == P and COLS == 512 and KC == 2 and B % (GR * len(GROUPS)) == 0

    with ExitStack() as ctx:
        def sb(name, shape, dt):
            return ctx.enter_context(nc.sbuf_tensor(name, shape, dt))

        def sem(name):
            return ctx.enter_context(nc.semaphore(name))

        def sig(name, per_trip, credit=0):
            return Signal(ctx, nc, name, per_trip, credit)

        def per_group(name, shape, dt):
            return [sb(f"{name}_{g}", shape, dt) for g in GROUPS]

        ps = ctx.enter_context(nc.psum_tensor("ps", [P, 8, 512], F32))

        def bank(g, b):
            return ps[:, 4 * g + b, :]

        def banks(g, b, n):
            return ps[:, 4 * g + b:4 * g + b + n, :]

        ident = sb("ident", [P, P], F32)
        ident16 = sb("ident16", [P, P], F16)
        ones = sb("ones", [P, 2], F32)
        gate_cell = sb("gate_cell", [P, 1], F32)
        credit_cell = sb("credit_cell", [P, len(GROUPS), 5], F32)
        neg_half = sb("neg_half", [P, GR], F32)
        adj_sb = sb("adj_sb", [P, N], F32)
        adjT16 = sb("adjT16", [P, N], F16)
        far_id = sb("far_id", [P, P], F16)
        far16 = sb("far16", [P, 2, N], F16)
        qkv_hi = sb("qkv_hi", [P, KC, 3 * D], F32R)
        qkv_lo = sb("qkv_lo", [P, KC, 3 * D], F32R)
        proj_hi = sb("proj_hi", [P, KC, D], F32R)
        proj_lo = sb("proj_lo", [P, KC, D], F32R)
        wt_hi = sb("wt_hi", [P, 6, KC, D], F32R)
        wt_lo = sb("wt_lo", [P, 6, KC, D], F32R)
        gat_hi = sb("gat_hi", [P, KC, D + 2], F32R)
        gat_lo = sb("gat_lo", [P, KC, D + 2], F32R)
        wa2_hi = sb("wa2_hi", [P, KC, P], F32R)
        wa2_lo = sb("wa2_lo", [P, KC, P], F32R)
        beta_col = sb("beta_col", [P, 1], F32)
        bproj_row = sb("bproj_row", [P, D], F32)
        gamma_row = sb("gamma_row", [P, D], F32)
        lnbeta_row = sb("lnbeta_row", [P, D], F32)
        bias_raw = sb("bias_raw", [P, 5, KC], F32)
        bias_sum = sb("bias_sum", [P, 3, KC], F32)
        bias_act = sb("bias_act", [P, 3, KC], F32)

        x_in = per_group("x_in", [P, GR, D], F32)
        fT_hi = per_group("fT_hi", [P, KC, COLS], F32R)
        fT_lo = per_group("fT_lo", [P, KC, COLS], F32R)
        q_hi = per_group("q_hi", [P, KC, COLS], F16)
        q_lo = per_group("q_lo", [P, KC, COLS], F16)
        v_hi = per_group("v_hi", [P, GR, HEADS, HW], F16)
        v_lo = per_group("v_lo", [P, GR, HEADS, HW], F16)
        row_max = per_group("row_max", [P, HEADS], F32)
        neg_max = per_group("neg_max", [P, HEADS], F32)
        inv_sum = per_group("inv_sum", [P, HEADS], F32)
        feat = per_group("feat", [P, GR, D], F32)
        resid = per_group("resid", [P, GR, D], F32)
        stats = per_group("stats", [P, GR, 6], F32)
        mean_var = per_group("mean_var", [P, GR, 2], F32)
        var_eps = per_group("var_eps", [P, GR], F32)
        rstd = per_group("rstd", [P, GR], F32)
        neg_mr = per_group("neg_mr", [P, GR], F32)
        hT = per_group("hT", [P, KC, COLS], F32)
        aT_hi = per_group("aT_hi", [P, KC, COLS], F32R)
        aT_lo = per_group("aT_lo", [P, KC, COLS], F32R)
        tz = per_group("tz", [P, KC, COLS], F32)
        tr = per_group("tr", [P, KC, COLS], F32)
        rh = per_group("rh", [P, KC, COLS], F32)
        rh_hi = per_group("rh_hi", [P, KC, COLS], F32R)
        rh_lo = per_group("rh_lo", [P, KC, COLS], F32R)
        s1 = per_group("s1", [P, GR], F32)
        e_max = per_group("e_max", [P, GR], F32)
        e_sum = per_group("e_sum", [P, GR], F32)
        e_inv = per_group("e_inv", [P, GR], F32)
        sq_sum = per_group("sq_sum", [P, GR], F32)
        rel_norm = per_group("rel_norm", [P, GR], F32)
        mov_hi = per_group("mov_hi", [P, KC, 2, 4, P], F32R)
        mov_lo = per_group("mov_lo", [P, KC, 2, 4, P], F32R)

        def rows_of(t, first=0, size=GR * D):
            return t[:, :, :].rearrange("p a b -> p (a b)")[:, first:first + size]

        def as_rows(t):
            return rows_of(t).rearrange("p (i d) -> p i d", d=D)

        prob = [rows_of(t).rearrange("p (s n) -> p s n", n=N) for t in tz]
        out_sb = [as_rows(t) for t in tz]
        temp = [as_rows(t) for t in hT]
        temp2 = [as_rows(t) for t in tr]
        k_hi, k_lo = ([t[:, 2 * n:2 * n + 2, :].bitcast(F16) for t in resid] for n in range(2))
        pT_hi, pT_lo = ([t[:, n, :].bitcast(F16).rearrange("p (s m) -> p s m", m=N) for t in rh] for n in range(2))
        h16_hi = [as_rows(t) for t in q_hi]
        h16_lo = [as_rows(t) for t in q_lo]
        g_hi = [as_rows(t) for t in aT_hi]
        g_lo = [as_rows(t) for t in aT_lo]
        edge = [t[:, 0, :].rearrange("p (i n) -> p i n", n=N) for t in rh]
        edge2 = [t[:, 1, :].rearrange("p (i n) -> p i n", n=N) for t in rh]
        eT_hi = [t[:, 0, :].rearrange("p (i n) -> p i n", n=N) for t in rh_hi]
        eT_lo = [t[:, 0, :].rearrange("p (i n) -> p i n", n=N) for t in rh_lo]
        pair_raw = [tz[0], tz[1], rh[0]]
        square_raw = [rows_of(t, n, KC * D).rearrange("p (c d) -> p c d", c=KC)
                      for t in (rh[1], hT[0], hT[1]) for n in (0, KC * D)]
        proj_raw = square_raw[5]
        summed = [rows_of(t, n, KC * D).rearrange("p (c d) -> p c d", c=KC)
                  for t in (tr[0], tr[1]) for n in (0, KC * D)]
        qkv_raw = [rows_of(t, 0, 3 * D) for t in feat]
        wv_hi, wv_lo = (rows_of(t[0], 0, KC * D).rearrange("p (c d) -> p c d", c=KC) for t in (aT_hi, aT_lo))
        a_row = rows_of(resid[0], 0, 2 * D)
        a_junk = rows_of(resid[0], 2 * D, D)
        gat_raw = rows_of(resid[1], 0, KC * (D + 2)).rearrange("p (c d) -> p c d", c=KC)

        ld_weights = sem("ld_weights")
        ident_made = sem("ident_made")
        prep_v = sem("prep_v")
        prep_pe = sem("prep_pe")
        prep_done = sem("prep_done")

        x_loaded = sig("x_loaded", 16)
        t_ps = sig("t_ps", 2 * 5)
        t_hi = sig("t_hi", 2 * 5)
        t_lo = sig("t_lo", 2 * 5)
        qkv_ps, qkv_hid, qkv_lod = sig("qkv_ps", 6), sig("qkv_hid", 6), sig("qkv_lod", 6)
        score_ps = sig("score_ps", GR)
        max_step = sig("max_step", 2 * GR)
        prob_done = sig("prob_done", GR)
        pT_ps = sig("pT_ps", 2 * GR)
        pT_hid, pT_lod = sig("pT_hid", 2 * GR), sig("pT_lod", 2 * GR)
        pv_ps = sig("pv_ps", GR)
        o_step = sig("o_step", 2 * GR)
        proj_ps = sig("proj_ps", 2)
        proj_done = sig("proj_done", 2)
        xo_done = sig("xo_done", 1, credit=1)
        xob_done = sig("xob_done", 1)
        scaled_done = sig("scaled_done", 1)
        resid_done = sig("resid_done", 4, credit=1)
        moment = sig("moment", 3 * 5)
        rstd_done = sig("rstd_done", 5)
        nmr_done = sig("nmr_done", 5)
        norm_done = sig("norm_done", 5)
        hT_done = sig("hT_done", 2)
        h16_hid = sig("h16_hid", 1 + 2 * (STEPS - 1))
        h16_lod = sig("h16_lod", 1 + 2 * (STEPS - 1))
        a_ps, a_hid, a_lod = sig("a_ps", 2 * STEPS), sig("a_hid", 2 * STEPS), sig("a_lod", 2 * STEPS)
        z_ps, z_done = sig("z_ps", 2 * STEPS), sig("z_done", 2 * STEPS)
        r_ps, r_done = sig("r_ps", 2 * STEPS), sig("r_done", 2 * STEPS)
        rh_step = sig("rh_step", 6 * STEPS)
        hv_ps, hv_done = sig("hv_ps", 2 * STEPS), sig("hv_done", 2 * STEPS)
        h_step = sig("h_step", 6 * STEPS)
        hs_hid, hs_lod = sig("hs_hid", 2 * (STEPS - 1)), sig("hs_lod", 2 * (STEPS - 1))
        hn_ps = sig("hn_ps", 2 * STEPS)
        gat_ps = sig("gat_ps", 1)
        s1_done, gh_done, gb_done, gl_done = sig("s1_done", 1), sig("gh_done", 1), sig("gb_done", 1), sig("gl_done", 1)
        s2_ps = sig("s2_ps", 1)
        s12_done = sig("s12_done", 1)
        edge_step = sig("edge_step", 4)
        eexp_done = sig("eexp_done", 1)
        einv_done = sig("einv_done", 1)
        eT_ps, eT_hid, eT_lod = sig("eT_ps", 1), sig("eT_hid", 1), sig("eT_lod", 1, credit=1)
        gp_ps = sig("gp_ps", 2)
        gp_done = sig("gp_done", 2)
        clip_done = sig("clip_done", 1)
        elu_exp = sig("elu_exp", 1)
        elu_done = sig("elu_done", 1)
        tq_ps, tq_hid, tq_lod = sig("tq_ps", 2), sig("tq_hid", 2), sig("tq_lod", 2)
        rv_ps = sig("rv_ps", 2)
        vv_hid, vv_lod = sig("vv_hid", 1), sig("vv_lod", 1)
        rel_done = sig("rel_done", 1)
        sq_done = sig("sq_done", 1)
        rel_hid, rel_lod = sig("rel_hid", 1), sig("rel_lod", 1)
        ss_ps = sig("ss_ps", 1)
        ss_done = sig("ss_done", 1, credit=1)
        rn_done = sig("rn_done", 1)
        ov_ps = sig("ov_ps", 2)
        out_stored = sig("out_stored", 16, credit=1)

        INNER, AFTER0, AFTER1, AFTER2, AFTER3 = range(5)

        x_rows = x.rearrange("b n d -> n b d")
        out_rows = out.rearrange("b n d -> n b d")

        def row_of(v):
            return v.rearrange("(a d) -> a d", a=1)

        def adj_rows(n):
            return adj_sb[:, :].unsqueeze(1).to_broadcast([P, n, N])

        loads = [
            (adj_sb[:, :], adj),
            (qkv_raw[0], w_qkv[0:P, :]),
            (qkv_raw[1], w_qkv[P:2 * P, :]),
            (proj_raw, w_proj.rearrange("(c p) o -> p c o", p=P)),
            (pair_raw[0][:, :, :], w3_w.rearrange("(c p) i -> p c i", p=P)),
            (pair_raw[1][:, :, :], w4_w.rearrange("(c p) i -> p c i", p=P)),
            (pair_raw[2][:, :, :], w5_w.rearrange("(c p) i -> p c i", p=P)),
            (square_raw[0], u3_w.rearrange("(c p) i -> p c i", p=P)),
            (square_raw[1], u5_w.rearrange("(c p) i -> p c i", p=P)),
            (square_raw[2], wv.rearrange("(c p) i -> p c i", p=P)),
            (square_raw[3], wq.rearrange("(c p) i -> p c i", p=P)),
            (square_raw[4], wk.rearrange("(c p) i -> p c i", p=P)),
            (gat_raw[:, :, 0:D], gat_w.rearrange("(c p) o -> p c o", p=P)),
            (a_row, gat_a.rearrange("k a -> a k").to_broadcast([P, 2 * D])),
            (beta_col[:, :], row_of(gat_beta).to_broadcast([P, 1])),
            (bproj_row[:, :], row_of(b_proj).to_broadcast([P, D])),
            (gamma_row[:, :], row_of(ln_gamma).to_broadcast([P, D])),
            (lnbeta_row[:, :], row_of(ln_beta).to_broadcast([P, D])),
        ] + [
            (bias_raw[:, n, c:c + 1], v[c * P:(c + 1) * P].rearrange("(p a) -> p a", a=1))
            for n, v in enumerate((w3_b, w4_b, w5_b, u3_b, u5_b)) for c in range(KC)
        ]

        block = ctx.enter_context(nc.Block())

        @block.sync
        def _(sp):
            for dst, src in loads:
                sp.dma_start(dst, src).then_inc(ld_weights, 16)
            with sp.Fori(0, TRIPS) as trip:
                for g in GROUPS:
                    sp.wait_ge(xo_done[g], xo_done.at(trip, 0))
                    sp.dma_start(x_in[g][:, :, :], x_rows[:, bass.ds(trip * (2 * GR) + g * GR, GR), :]) \
                        .then_inc(x_loaded[g], 16)

        @block.gpsimd
        def _(pool):
            nc.gpsimd.memset(ident[:, :], 0.0).then_inc(ident_made, 1)
            pool.wait_ge(ident_made, 1)
            nc.gpsimd.affine_select(out=ident[:, :], in_=ident[:, :], compare_op=ALU.not_equal, fill=1.0, base=0,
                                    pattern=[[-1, P]], channel_multiplier=1).then_inc(ident_made, 1)
            nc.gpsimd.memset(neg_half[:, :], -0.5).then_inc(ident_made, 1)
            nc.gpsimd.memset(ones[:, :], 1.0).then_inc(ident_made, 1)
            for g in GROUPS:
                nc.gpsimd.memset(v_hi[g][:, :, :, HD:HW], 1.0).then_inc(ident_made, 1)
                nc.gpsimd.memset(v_lo[g][:, :, :, HD:HW], 0.0).then_inc(ident_made, 1)
            for g in GROUPS:
                for n, credited in enumerate((xo_done, ss_done, eT_lod, resid_done, out_stored)):
                    nc.gpsimd.memset(credit_cell[:, g, n:n + 1], 0.0).then_inc(credited[g], 1)

            def rsqrt_of(g, n, trip):
                pool.wait_ge(moment[g], moment.at(trip, 3 * n + 3))
                nc.gpsimd.tensor_tensor(rstd[g][:, :], var_eps[g][:, :], neg_half[:, :], ALU.pow) \
                    .then_inc(rstd_done[g], 1)

            with pool.Fori(0, TRIPS) as trip:
                for g in GROUPS:
                    pool.wait_ge(proj_done[g], proj_done.at(trip, 2))
                    nc.gpsimd.tensor_tensor(temp2[g][:, :, :], x_in[g][:, :, :], resid[g][:, :, :], ALU.add) \
                        .then_inc(xo_done[g], 1)
                    pool.wait_ge(xo_done[g], xo_done.at(trip, 1))
                    nc.gpsimd.tensor_tensor(temp2[g][:, :, :], temp2[g][:, :, :],
                                            lnbeta_row[:, :].unsqueeze(1).to_broadcast([P, GR, D]), ALU.add) \
                        .then_inc(xob_done[g], 1)
                    rsqrt_of(g, INNER, trip)
                for n in (AFTER0, AFTER1, AFTER2):
                    for g in GROUPS:
                        rsqrt_of(g, n, trip)
                for g in GROUPS:
                    pool.wait_ge(ss_done[g], ss_done.at(trip, 1))
                    nc.gpsimd.tensor_tensor(rel_norm[g][:, :], sq_sum[g][:, :], neg_half[:, :], ALU.pow) \
                        .then_inc(rn_done[g], 1)
                for g in GROUPS:
                    rsqrt_of(g, AFTER3, trip)

        @block.tensor
        def _(pe):
            def split_mm(dst, w_hi, w_lo, m_hi, m_lo, start=True, stop=True):
                n = 0
                for c in range(KC):
                    for a, b in ((w_hi, m_hi), (w_hi, m_lo), (w_lo, m_hi)):
                        last = nc.tensor.matmul(dst, a(c), b(c), start=start and n == 0,
                                                stop=stop and n == 3 * KC - 1, skip_group_check=not (start and stop))
                        n += 1
                return last

            def transposed(g, s, src, trip):
                for c in range(KC):
                    for i in range(GR):
                        last = nc.tensor.transpose(bank(g, c)[:, i * P:(i + 1) * P],
                                                   src[g][:, i, c * P:(c + 1) * P], ident[:, :])
                    last.then_inc(t_ps[g], 1)

            pe.wait_ge(ident_made, 8)
            pe.wait_ge(prep_v, 4)
            srcs = [summed[0], summed[1], summed[2], square_raw[0], summed[3], square_raw[2]]
            for n, src in zip((W3, W4, W5, U3, U5, WV), srcs):
                for oc in range(KC):
                    for dc in range(KC):
                        nc.tensor.transpose(ps[:, n, dc * D + oc * P:dc * D + (oc + 1) * P],
                                            src[:, oc, dc * P:(dc + 1) * P], ident[:, :]).then_inc(prep_pe, 1)
            for dc in range(KC):
                for c in range(KC):
                    nc.tensor.matmul(ps[:, WM, dc * D:(dc + 1) * D], square_raw[3][:, c, dc * P:(dc + 1) * P],
                                     square_raw[4][:, c, :], start=(c == 0), stop=(c == KC - 1)).then_inc(prep_pe, 1)
            nc.tensor.transpose(ps[:, 7, 0:P], adj_sb[:, :], ident[:, :]).then_inc(prep_pe, 1)
            pe.wait_ge(prep_done, 1)

            with pe.Fori(0, TRIPS) as trip:
                for g in GROUPS:
                    pe.wait_ge(x_loaded[g], x_loaded.at(trip, 16))
                    pe.wait_ge(ss_done[g], ss_done.at(trip, 0))
                    pe.wait_ge(eT_lod[g], eT_lod.at(trip, 0))
                    transposed(g, 0, x_in, trip)
                for g in GROUPS:
                    pe.wait_ge(resid_done[g], resid_done.at(trip, 0))
                    pe.wait_ge(t_lo[g], t_lo.at(trip, 2))
                    for c in range(KC):
                        split_mm(bank(g, 2 + c),
                                 lambda k: qkv_hi[:, k, c * P:(c + 1) * P], lambda k: qkv_lo[:, k, c * P:(c + 1) * P],
                                 lambda k: fT_hi[g][:, k, :], lambda k: fT_lo[g][:, k, :]).then_inc(qkv_ps[g], 1)
                    for c in range(KC):
                        split_mm(bank(g, c),
                                 lambda k: qkv_hi[:, k, D + c * P:D + (c + 1) * P],
                                 lambda k: qkv_lo[:, k, D + c * P:D + (c + 1) * P],
                                 lambda k: fT_hi[g][:, k, :], lambda k: fT_lo[g][:, k, :]).then_inc(qkv_ps[g], 1)
                for g in GROUPS:
                    for b in range(2):
                        pe.wait_ge(qkv_lod[g], qkv_lod.at(trip, b + 1))
                        for j in range(2):
                            i = 2 * b + j
                            last = split_mm(bank(g, 2 + b)[:, j * D:(j + 1) * D],
                                            lambda k: fT_hi[g][:, k, i * P:(i + 1) * P],
                                            lambda k: fT_lo[g][:, k, i * P:(i + 1) * P],
                                            lambda k: qkv_hi[:, k, 2 * D:3 * D], lambda k: qkv_lo[:, k, 2 * D:3 * D])
                        last.then_inc(qkv_ps[g], 1)

                for i in range(GR):
                    at = slice(i * N, (i + 1) * N)
                    for g in GROUPS:
                        if i == 0:
                            pe.wait_ge(qkv_lod[g], qkv_lod.at(trip, 4 + 2))
                        else:
                            pe.wait_ge(o_step[g], o_step.at(trip, 2 * i))
                        for j in range(4):
                            nc.tensor.matmul(bank(g, j)[:, 0:2 * N], far_id[:, :], far16[:, :, :], start=True,
                                             stop=False, skip_group_check=True)
                        for c in range(KC):
                            for n, (a, b) in enumerate(((q_hi, k_hi), (q_hi, k_lo), (q_lo, k_hi))):
                                for j in range(4):
                                    rows = slice(HD * j, HD * (j + 1))
                                    last = nc.tensor.matmul(bank(g, j)[:, c * N:(c + 1) * N], a[g][rows, c, at],
                                                            b[g][rows, c, at], start=False, stop=(n == 2),
                                                            skip_group_check=True)
                        last.then_inc(score_ps[g], 1)
                    for g in GROUPS:
                        pe.wait_ge(prob_done[g], prob_done.at(trip, i + 1))
                        for b in range(2):
                            for s in range(4):
                                last = nc.tensor.transpose(bank(g, b)[:, s * N:(s + 1) * N],
                                                           prob[g][:, 4 * b + s, :], ident[:, :])
                            last.then_inc(pT_ps[g], 1)
                    for g in GROUPS:
                        for s in range(HEADS):
                            if s % 4 == 0:
                                pe.wait_ge(pT_lod[g], pT_lod.at(trip, 2 * i + s // 4 + 1))
                            h = s // 2 + 4 * (s % 2)
                            dst = bank(g, 2)[:, s * HW:(s + 1) * HW]
                            for n, (a, b) in enumerate(((pT_hi, v_hi), (pT_hi, v_lo), (pT_lo, v_hi))):
                                last = nc.tensor.matmul(dst, a[g][:, s, :], b[g][:, i, h, :],
                                                        start=(n == 0), stop=(n == 2))
                        last.then_inc(pv_ps[g], 1)
                for g in GROUPS:
                    pe.wait_ge(o_step[g], o_step.at(trip, 2 * GR))
                    transposed(g, 1, feat, trip)
                for g in GROUPS:
                    pe.wait_ge(t_lo[g], t_lo.at(trip, 4))
                    for b in range(2):
                        for j in range(2):
                            i = 2 * b + j
                            last = split_mm(bank(g, 2 + b)[:, j * D:(j + 1) * D],
                                            lambda k: fT_hi[g][:, k, i * P:(i + 1) * P],
                                            lambda k: fT_lo[g][:, k, i * P:(i + 1) * P],
                                            lambda k: proj_hi[:, k, :], lambda k: proj_lo[:, k, :])
                        last.then_inc(proj_ps[g], 1)

                for g in GROUPS:
                    pe.wait_ge(norm_done[g], norm_done.at(trip, AFTER0 + 1))
                    transposed(g, 2, feat, trip)

                def gate(g, b, c, w, f_hi, f_lo, start, stop):
                    return split_mm(bank(g, b + c),
                                    lambda k: wt_hi[:, w, k, c * P:(c + 1) * P],
                                    lambda k: wt_lo[:, w, k, c * P:(c + 1) * P],
                                    lambda k: f_hi[g][:, k, :], lambda k: f_lo[g][:, k, :], start, stop)

                for t in range(STEPS):
                    for g in GROUPS:
                        if t == 0:
                            pe.wait_ge(proj_done[g], proj_done.at(trip, 2))
                            pe.wait_ge(t_lo[g], t_lo.at(trip, 6))
                        else:
                            pe.wait_ge(hv_done[g], hv_done.at(trip, 2 * t))
                            pe.wait_ge(hs_lod[g], hs_lod.at(trip, 2 * t))
                        for c in range(KC):
                            gate(g, 2, c, U3, fT_hi, fT_lo, True, False)
                    for g in GROUPS:
                        if t == 0:
                            pe.wait_ge(hT_done[g], hT_done.at(trip, 2))
                        pe.wait_ge(h16_lod[g], h16_lod.at(trip, 2 * t + 1))
                        for c in range(KC):
                            for i in range(GR):
                                for n, a in enumerate((h16_hi, h16_lo)):
                                    last = nc.tensor.matmul(bank(g, c)[:, i * N:(i + 1) * N],
                                                            a[g][:, i, c * P:(c + 1) * P], adjT16[:, :],
                                                            start=(n == 0), stop=(n == 1))
                            last.then_inc(a_ps[g], 1)
                    for g in GROUPS:
                        pe.wait_ge(a_lod[g], a_lod.at(trip, 2 * t + 2))
                        for c in range(KC):
                            gate(g, 2, c, W3, aT_hi, aT_lo, False, True).then_inc(z_ps[g], 1)
                        for c in range(KC):
                            gate(g, 0, c, U3, fT_hi, fT_lo, True, False)
                            gate(g, 0, c, W4, aT_hi, aT_lo, False, True).then_inc(r_ps[g], 1)
                    for g in GROUPS:
                        pe.wait_ge(z_done[g], z_done.at(trip, 2 * t + 2))
                        for c in range(KC):
                            gate(g, 2, c, W5, aT_hi, aT_lo, True, False)
                            if c == 0:
                                pe.wait_ge(rh_step[g], rh_step.at(trip, 6 * t + 4 + 2))
                            gate(g, 2, c, U5, rh_hi, rh_lo, False, True).then_inc(hv_ps[g], 1)
                    for g in GROUPS:
                        pe.wait_ge(h_step[g], h_step.at(trip, 6 * t + 4 + 2))
                        for b in range(2):
                            for j in range(2):
                                i = 2 * b + j
                                for c in range(KC):
                                    last = nc.tensor.transpose(bank(g, b)[:, j * D + c * P:j * D + (c + 1) * P],
                                                               hT[g][:, c, i * N:(i + 1) * N], ident[:, :])
                            last.then_inc(hn_ps[g], 1)

                for g in GROUPS:
                    pe.wait_ge(norm_done[g], norm_done.at(trip, AFTER1 + 1))
                    transposed(g, 3, feat, trip)
                for g in GROUPS:
                    pe.wait_ge(t_lo[g], t_lo.at(trip, 8))
                    for i in range(GR):
                        last = split_mm(bank(g, i)[:, 0:D + 2],
                                        lambda k: fT_hi[g][:, k, i * P:(i + 1) * P],
                                        lambda k: fT_lo[g][:, k, i * P:(i + 1) * P],
                                        lambda k: gat_hi[:, k, :], lambda k: gat_lo[:, k, :])
                    last.then_inc(gat_ps[g], 1)
                for g in GROUPS:
                    pe.wait_ge(gl_done[g], gl_done.at(trip, 1))
                    pe.wait_ge(gb_done[g], gb_done.at(trip, 1))
                    split_mm(bank(g, 0), lambda k: wa2_hi[:, k, :], lambda k: wa2_lo[:, k, :],
                             lambda k: fT_hi[g][:, k, :], lambda k: fT_lo[g][:, k, :]).then_inc(s2_ps[g], 1)
                for g in GROUPS:
                    pe.wait_ge(eexp_done[g], eexp_done.at(trip, 1))
                    for i in range(GR):
                        last = nc.tensor.transpose(bank(g, 1)[:, i * N:(i + 1) * N], edge2[g][:, i, :], ident[:, :])
                    last.then_inc(eT_ps[g], 1)
                for g in GROUPS:
                    pe.wait_ge(eT_lod[g], eT_lod.at(trip, 1))
                    for b in range(2):
                        for j in range(2):
                            i = 2 * b + j
                            for n, (a, m) in enumerate(((eT_hi, g_hi), (eT_hi, g_lo), (eT_lo, g_hi))):
                                last = nc.tensor.matmul(bank(g, 2 + b)[:, j * D:(j + 1) * D], a[g][:, i, :],
                                                        m[g][:, i, :], start=(n == 0), stop=(n == 2))
                        last.then_inc(gp_ps[g], 1)

                for g in GROUPS:
                    pe.wait_ge(norm_done[g], norm_done.at(trip, AFTER2 + 1))
                    transposed(g, 4, feat, trip)
                for g in GROUPS:
                    pe.wait_ge(t_lo[g], t_lo.at(trip, 10))
                    for c in range(KC):
                        gate(g, 2, c, WM, fT_hi, fT_lo, True, True).then_inc(tq_ps[g], 1)
                for g in GROUPS:
                    pe.wait_ge(tq_lod[g], tq_lod.at(trip, 2))
                    for i in range(GR):
                        a, odd = i // 2, i % 2
                        last = split_mm(bank(g, i)[:, 0:3 * P],
                                        lambda k: fT_hi[g][:, k, i * P:(i + 1) * P],
                                        lambda k: fT_lo[g][:, k, i * P:(i + 1) * P],
                                        lambda k: mov_hi[g][:, k, a, odd:odd + 3, :],
                                        lambda k: mov_lo[g][:, k, a, odd:odd + 3, :])
                        if odd:
                            last.then_inc(rv_ps[g], 1)
                for g in GROUPS:
                    pe.wait_ge(sq_done[g], sq_done.at(trip, 1))
                    pe.wait_ge(vv_lod[g], vv_lod.at(trip, 1))
                    for i in range(GR):
                        last = nc.tensor.matmul(bank(g, 0)[:, 2 * i:2 * i + 2], edge2[g][:, i, :], ones[:, :],
                                                start=True, stop=True)
                    last.then_inc(ss_ps[g], 1)
                for g in GROUPS:
                    pe.wait_ge(rel_lod[g], rel_lod.at(trip, 1))
                    for b in range(2):
                        for j in range(2):
                            i = 2 * b + j
                            for n, (a, m) in enumerate(((eT_hi, g_hi), (eT_hi, g_lo), (eT_lo, g_hi))):
                                last = nc.tensor.matmul(bank(g, 2 + b)[:, j * D:(j + 1) * D], a[g][:, i, :],
                                                        m[g][:, i, :], start=(n == 0), stop=(n == 2))
                        last.then_inc(ov_ps[g], 1)

        @block.scalar
        def _(act):
            def high_part(g, dst, s, trip):
                for c in range(KC):
                    act.wait_ge(t_ps[g], t_ps.at(trip, 2 * s + c + 1))
                    nc.scalar.activation(dst[g][:, c, :], bank(g, c), ACT.Copy).then_inc(t_hi[g], 1)

            def normalised(g, n, dst, trip):
                act.wait_ge(nmr_done[g], nmr_done.at(trip, n + 1))
                for i in range(GR):
                    last = nc.scalar.activation(dst[g][:, i, :], resid[g][:, i, :], ACT.Identity,
                                                scale=rstd[g][:, i:i + 1], bias=neg_mr[g][:, i:i + 1])
                last.then_inc(norm_done[g], 1)

            act.wait_ge(prep_done, 1)
            with act.Fori(0, TRIPS) as trip:
                for g in GROUPS:
                    high_part(g, fT_hi, 0, trip)
                for g in GROUPS:
                    for c in range(KC):
                        act.wait_ge(qkv_ps[g], qkv_ps.at(trip, c + 1))
                        nc.scalar.activation(q_hi[g][:, c, :], bank(g, 2 + c), ACT.Copy).then_inc(qkv_hid[g], 1)
                    for c in range(KC):
                        act.wait_ge(qkv_ps[g], qkv_ps.at(trip, 2 + c + 1))
                        nc.scalar.activation(k_hi[g][:, c, :], bank(g, c), ACT.Copy).then_inc(qkv_hid[g], 1)
                for g in GROUPS:
                    for b in range(2):
                        act.wait_ge(qkv_ps[g], qkv_ps.at(trip, 4 + b + 1))
                        nc.scalar.activation(v_hi[g][:, 2 * b:2 * b + 2, :, 0:HD],
                                             bank(g, 2 + b).rearrange("p (i h d) -> p i h d", i=2, h=HEADS),
                                             ACT.Copy).then_inc(qkv_hid[g], 1)
                for i in range(GR):
                    for g in GROUPS:
                        act.wait_ge(max_step[g], max_step.at(trip, 2 * i + 2))
                        if i == 0:
                            act.wait_ge(out_stored[g], out_stored.at(trip, 0))
                        for s in range(HEADS):
                            last = nc.scalar.activation(prob[g][:, s, :],
                                                        bank(g, s // 2)[:, (s % 2) * N:(s % 2 + 1) * N], ACT.Exp,
                                                        bias=neg_max[g][:, s:s + 1], scale=SCALE)
                        last.then_inc(prob_done[g], 1)
                    for g in GROUPS:
                        for b in range(2):
                            act.wait_ge(pT_ps[g], pT_ps.at(trip, 2 * i + b + 1))
                            nc.scalar.activation(pT_hi[g][:, 4 * b:4 * b + 4, :], bank(g, b), ACT.Copy) \
                                .then_inc(pT_hid[g], 1)
                for g in GROUPS:
                    high_part(g, fT_hi, 1, trip)
                for g in GROUPS:
                    normalised(g, INNER, temp, trip)
                for g in GROUPS:
                    normalised(g, AFTER0, feat, trip)
                for g in GROUPS:
                    for c in range(KC):
                        act.wait_ge(t_ps[g], t_ps.at(trip, 4 + c + 1))
                        nc.scalar.activation(fT_hi[g][:, c, :], bank(g, c), ACT.Copy).then_inc(t_hi[g], 1)
                        nc.scalar.activation(hT[g][:, c, :], bank(g, c), ACT.Copy).then_inc(hT_done[g], 1)
                for t in range(STEPS):
                    for g in GROUPS:
                        for c in range(KC):
                            act.wait_ge(a_ps[g], a_ps.at(trip, 2 * t + c + 1))
                            nc.scalar.activation(aT_hi[g][:, c, :], bank(g, c), ACT.Copy).then_inc(a_hid[g], 1)
                    for g in GROUPS:
                        for c in range(KC):
                            act.wait_ge(z_ps[g], z_ps.at(trip, 2 * t + c + 1))
                            nc.scalar.activation(tz[g][:, c, :], bank(g, 2 + c), ACT.Tanh,
                                                 bias=bias_act[:, 0, c:c + 1], scale=0.5).then_inc(z_done[g], 1)
                        for c in range(KC):
                            act.wait_ge(r_ps[g], r_ps.at(trip, 2 * t + c + 1))
                            nc.scalar.activation(tr[g][:, c, :], bank(g, c), ACT.Tanh,
                                                 bias=bias_act[:, 1, c:c + 1], scale=0.5).then_inc(r_done[g], 1)
                    for g in GROUPS:
                        for c in range(KC):
                            act.wait_ge(hv_ps[g], hv_ps.at(trip, 2 * t + c + 1))
                            nc.scalar.activation(rh[g][:, c, :], bank(g, 2 + c), ACT.Tanh,
                                                 bias=bias_act[:, 2, c:c + 1], scale=1.0).then_inc(hv_done[g], 1)
                    if t < STEPS - 1:
                        for g in GROUPS:
                            for b in range(2):
                                act.wait_ge(hn_ps[g], hn_ps.at(trip, 2 * t + b + 1))
                                nc.scalar.activation(h16_hi[g][:, 2 * b:2 * b + 2, :], bank(g, b), ACT.Copy) \
                                    .then_inc(h16_hid[g], 1)
                for g in GROUPS:
                    normalised(g, AFTER1, feat, trip)
                for g in GROUPS:
                    high_part(g, fT_hi, 3, trip)
                for g in GROUPS:
                    act.wait_ge(gat_ps[g], gat_ps.at(trip, 1))
                    nc.scalar.activation(g_hi[g][:, :, :], banks(g, 0, 4)[:, :, 0:D], ACT.Copy).then_inc(gh_done[g], 1)
                    act.wait_ge(s1_done[g], s1_done.at(trip, 1))
                    nc.scalar.activation(temp[g][:, :, :], banks(g, 0, 4)[:, :, 0:D], ACT.Copy,
                                         scale=beta_col[:, 0:1]).then_inc(gb_done[g], 1)
                for g in GROUPS:
                    act.wait_ge(s2_ps[g], s2_ps.at(trip, 1))
                    for i in range(GR):
                        last = nc.scalar.activation(edge[g][:, i, :], bank(g, 0)[:, i * N:(i + 1) * N],
                                                    ACT.Identity, bias=s1[g][:, i:i + 1], scale=1.0)
                    last.then_inc(s12_done[g], 1)
                for g in GROUPS:
                    act.wait_ge(edge_step[g], edge_step.at(trip, 4))
                    for i in range(GR):
                        last = nc.scalar.activation(edge2[g][:, i, :], edge2[g][:, i, :], ACT.Exp,
                                                    bias=e_max[g][:, i:i + 1], scale=1.0, accum_out=e_sum[g][:, i:i + 1])
                    last.then_inc(eexp_done[g], 1)
                for g in GROUPS:
                    act.wait_ge(eT_ps[g], eT_ps.at(trip, 1))
                    nc.scalar.activation(eT_hi[g][:, :, :], bank(g, 1), ACT.Copy).then_inc(eT_hid[g], 1)
                for g in GROUPS:
                    act.wait_ge(clip_done[g], clip_done.at(trip, 1))
                    nc.scalar.activation(temp2[g][:, :, :], temp2[g][:, :, :], ACT.Exp).then_inc(elu_exp[g], 1)
                for g in GROUPS:
                    normalised(g, AFTER2, feat, trip)
                for g in GROUPS:
                    high_part(g, fT_hi, 4, trip)
                for g in GROUPS:
                    for c in range(KC):
                        act.wait_ge(tq_ps[g], tq_ps.at(trip, c + 1))
                        nc.scalar.activation(mov_hi[g][:, c, :, 0:4:3, :],
                                             bank(g, 2 + c).rearrange("p (a q n) -> p a q n", a=2, q=2), ACT.Copy) \
                            .then_inc(tq_hid[g], 1)
                for g in GROUPS:
                    act.wait_ge(rv_ps[g], rv_ps.at(trip, 2))
                    for odd in range(2):
                        src = banks(g, 0, 4)[:, odd:4:2, P - odd * P:P - odd * P + D]
                        last = nc.scalar.activation(g_hi[g][:, odd:GR:2, :], src, ACT.Copy)
                    last.then_inc(vv_hid[g], 1)
                for g in GROUPS:
                    act.wait_ge(rel_done[g], rel_done.at(trip, 1))
                    nc.scalar.activation(edge2[g][:, :, :], edge[g][:, :, :], ACT.Square).then_inc(sq_done[g], 1)
                for g in GROUPS:
                    act.wait_ge(nmr_done[g], nmr_done.at(trip, AFTER3 + 1))
                    for i in range(GR):
                        last = nc.scalar.activation(out_sb[g][:, i, :], resid[g][:, i, :], ACT.Identity,
                                                    scale=rstd[g][:, i:i + 1], bias=neg_mr[g][:, i:i + 1])
                    last.then_inc(norm_done[g], 1)
                    act.wait_ge(norm_done[g], norm_done.at(trip, AFTER3 + 1))
                    act.dma_start(out_rows[:, bass.ds(trip * (2 * GR) + g * GR, GR), :], out_sb[g][:, :, :]) \
                        .then_inc(out_stored[g], 16)
            for g in GROUPS:
                act.wait_ge(out_stored[g], out_stored.at(TRIPS, 0))

        @block.vector
        def _(dve):
            v = nc.vector

            def f32(t):
                return t.bitcast(F32)

            dve.wait_ge(ld_weights, 16 * len(loads))
            dve.wait_ge(ident_made, 8)
            for n in range(3):
                v.tensor_tensor(summed[n], pair_raw[n][:, :, 0:D], pair_raw[n][:, :, D:2 * D], ALU.add) \
                    .then_inc(prep_v, 1)
            v.tensor_scalar(summed[3], square_raw[1], 0.5, None, ALU.mult).then_inc(prep_v, 1)
            for c in range(KC):
                for n in range(2):
                    v.tensor_tensor_reduce(out=a_junk, in0=gat_raw[:, c, 0:D], in1=a_row[:, n * D:(n + 1) * D],
                                           scale=1.0, scalar=0.0, op0=ALU.mult, op1=ALU.add,
                                           accum_out=gat_raw[:, c, D + n:D + n + 1]).then_inc(prep_v, 1)
                    dve.wait_ge(prep_v, 4 + 2 * c + n + 1)
            v.tensor_tensor(bias_sum[:, 0:2, :], bias_raw[:, 0:2, :],
                            bias_raw[:, 3:4, :].to_broadcast([P, 2, KC]), ALU.add).then_inc(prep_v, 1)
            v.tensor_tensor(bias_sum[:, 2, :], bias_raw[:, 2, :], bias_raw[:, 4, :], ALU.add).then_inc(prep_v, 1)
            v.tensor_scalar(far_id[:, :], ident[:, :], FAR, None, ALU.mult).then_inc(prep_v, 1)
            v.tensor_scalar(far16[:, :, :], adj_rows(2), 0.0, -FAR, ALU.is_equal, ALU.mult).then_inc(prep_v, 1)
            for c in range(KC):
                v.tensor_copy(qkv_hi[:, c, :], qkv_raw[c]).then_inc(prep_v, 1)
            v.tensor_copy(proj_hi[:, :, :], proj_raw).then_inc(prep_v, 1)
            v.tensor_copy(gat_hi[:, :, :], gat_raw[:, :, :]).then_inc(prep_v, 1)
            dve.wait_ge(prep_v, 16)
            v.tensor_scalar(bias_act[:, 0:2, :], bias_sum[:, 0:2, :], 0.5, None, ALU.mult).then_inc(prep_v, 1)
            v.tensor_copy(bias_act[:, 2, :], bias_sum[:, 2, :]).then_inc(prep_v, 1)
            for c in range(KC):
                v.tensor_tensor(qkv_lo[:, c, :], qkv_raw[c], f32(qkv_hi[:, c, :]), ALU.subtract).then_inc(prep_v, 1)
            v.tensor_tensor(proj_lo[:, :, :], proj_raw, f32(proj_hi[:, :, :]), ALU.subtract) \
                .then_inc(prep_v, 1)
            v.tensor_tensor(gat_lo[:, :, :], gat_raw[:, :, :], f32(gat_hi[:, :, :]), ALU.subtract).then_inc(prep_v, 1)
            dve.wait_ge(prep_v, 22)
            for c in range(KC):
                v.tensor_copy(wa2_hi[:, c, :], f32(gat_hi[:, c, D + 1:D + 2]).to_broadcast([P, P])).then_inc(prep_v, 1)
                v.tensor_copy(wa2_lo[:, c, :], f32(gat_lo[:, c, D + 1:D + 2]).to_broadcast([P, P])).then_inc(prep_v, 1)
            dve.wait_ge(prep_pe, 29)
            for n in range(7):
                src = ps[:, n, :].rearrange("p (c o) -> p c o", c=KC)
                hi, lo = (wv_hi, wv_lo) if n == WV else (wt_hi[:, n], wt_lo[:, n])
                v.tensor_copy(hi, src).then_inc(prep_v, 1)
                dve.wait_ge(prep_v, 26 + 2 * n + 1)
                v.tensor_tensor(lo, src, f32(hi), ALU.subtract).then_inc(prep_v, 1)
            v.tensor_copy(adjT16[:, :], ps[:, 7, 0:P]).then_inc(prep_v, 1)
            dve.wait_ge(prep_v, 41)
            for g in GROUPS:
                for c in range(KC):
                    for a in range(2):
                        v.tensor_copy(mov_hi[g][:, c, a, 1:3, :].rearrange("p q n -> p (q n)"),
                                      f32(wv_hi[:, c, :])).then_inc(prep_v, 1)
                        v.tensor_copy(mov_lo[g][:, c, a, 1:3, :].rearrange("p q n -> p (q n)"),
                                      f32(wv_lo[:, c, :])).then_inc(prep_v, 1)
            dve.wait_ge(prep_v, 41 + 16)
            v.memset(a_junk[:, 0:1], 0.0).then_inc(prep_done, 1)

            def low_part(g, s, trip):
                for c in range(KC):
                    dve.wait_ge(t_hi[g], t_hi.at(trip, 2 * s + c + 1))
                    v.tensor_tensor(fT_lo[g][:, c, :], bank(g, c), f32(fT_hi[g][:, c, :]), ALU.subtract) \
                        .then_inc(t_lo[g], 1)

            def moments(g, n, trip):
                for i in range(GR):
                    last = v.bn_stats(stats[g][:, i, :], resid[g][:, i, :])
                last.then_inc(moment[g], 1)
                dve.wait_ge(moment[g], moment.at(trip, 3 * n + 1))
                v.memset(gate_cell[:, :], 0.0)
                for i in range(GR):
                    last = v.bn_aggr(mean_var[g][:, i, :], stats[g][:, i, :])
                last.then_inc(moment[g], 1)
                dve.wait_ge(moment[g], moment.at(trip, 3 * n + 2))
                v.tensor_scalar(var_eps[g][:, :], mean_var[g][:, :, 1], LN_EPS, None, ALU.add).then_inc(moment[g], 1)

            def shift(g, n, trip):
                dve.wait_ge(rstd_done[g], rstd_done.at(trip, n + 1))
                v.scalar_tensor_tensor(neg_mr[g][:, :], mean_var[g][:, :, 0], -1.0, rstd[g][:, :], ALU.mult, ALU.mult) \
                    .then_inc(nmr_done[g], 1)

            with dve.Fori(0, TRIPS) as trip:
                for g in GROUPS:
                    low_part(g, 0, trip)
                for g in GROUPS:
                    for c in range(KC):
                        dve.wait_ge(qkv_hid[g], qkv_hid.at(trip, c + 1))
                        v.tensor_tensor(q_lo[g][:, c, :], bank(g, 2 + c), q_hi[g][:, c, :], ALU.subtract) \
                            .then_inc(qkv_lod[g], 1)
                    for c in range(KC):
                        dve.wait_ge(qkv_hid[g], qkv_hid.at(trip, 2 + c + 1))
                        v.tensor_tensor(k_lo[g][:, c, :], bank(g, c), k_hi[g][:, c, :], ALU.subtract) \
                            .then_inc(qkv_lod[g], 1)
                for g in GROUPS:
                    for b in range(2):
                        dve.wait_ge(qkv_hid[g], qkv_hid.at(trip, 4 + b + 1))
                        v.tensor_tensor(v_lo[g][:, 2 * b:2 * b + 2, :, 0:HD],
                                        bank(g, 2 + b).rearrange("p (i h d) -> p i h d", i=2, h=HEADS),
                                        v_hi[g][:, 2 * b:2 * b + 2, :, 0:HD], ALU.subtract).then_inc(qkv_lod[g], 1)
                for i in range(GR):
                    for g in GROUPS:
                        dve.wait_ge(score_ps[g], score_ps.at(trip, i + 1))
                        v.tensor_reduce(row_max[g][:, :],
                                        banks(g, 0, 4)[:, :, 0:2 * N].rearrange("p j (c m) -> p j c m", c=KC),
                                        AX_X, ALU.max).then_inc(max_step[g], 1)
                        dve.wait_ge(max_step[g], max_step.at(trip, 2 * i + 1))
                        v.tensor_scalar(neg_max[g][:, :], row_max[g][:, :], -SCALE, None, ALU.mult) \
                            .then_inc(max_step[g], 1)
                    for g in GROUPS:
                        for b in range(2):
                            dve.wait_ge(pT_hid[g], pT_hid.at(trip, 2 * i + b + 1))
                            v.tensor_tensor(pT_lo[g][:, 4 * b:4 * b + 4, :], bank(g, b), pT_hi[g][:, 4 * b:4 * b + 4, :],
                                            ALU.subtract).then_inc(pT_lod[g], 1)
                    for g in GROUPS:
                        pv = bank(g, 2)[:, 0:HEADS * HW].rearrange("p (j c d) -> p j c d", j=4, c=KC)
                        dve.wait_ge(pv_ps[g], pv_ps.at(trip, i + 1))
                        v.reciprocal(inv_sum[g][:, :].rearrange("p (j c) -> p j c", c=KC), pv[:, :, :, HD]) \
                            .then_inc(o_step[g], 1)
                        dve.wait_ge(o_step[g], o_step.at(trip, 2 * i + 1))
                        v.tensor_tensor(feat[g][:, i, :].rearrange("p (c j d) -> p j c d", c=KC, j=4), pv[:, :, :, 0:HD],
                                        inv_sum[g][:, :].rearrange("p (j c) -> p j c", c=KC).unsqueeze(3)
                                        .to_broadcast([P, 4, KC, HD]), ALU.mult).then_inc(o_step[g], 1)
                for g in GROUPS:
                    low_part(g, 1, trip)
                for g in GROUPS:
                    for b in range(2):
                        dve.wait_ge(proj_ps[g], proj_ps.at(trip, b + 1))
                        v.tensor_tensor(resid[g][:, 2 * b:2 * b + 2, :], bank(g, 2 + b).rearrange("p (i d) -> p i d", i=2),
                                        bproj_row[:, :].unsqueeze(1).to_broadcast([P, 2, D]), ALU.add) \
                            .then_inc(proj_done[g], 1)
                    dve.wait_ge(proj_done[g], proj_done.at(trip, 2))
                    moments(g, INNER, trip)
                for g in GROUPS:
                    shift(g, INNER, trip)
                for g in GROUPS:
                    dve.wait_ge(norm_done[g], norm_done.at(trip, INNER + 1))
                    v.tensor_tensor(temp[g][:, :, :], temp[g][:, :, :],
                                    gamma_row[:, :].unsqueeze(1).to_broadcast([P, GR, D]), ALU.mult) \
                        .then_inc(scaled_done[g], 1)
                    dve.wait_ge(scaled_done[g], scaled_done.at(trip, 1))
                    dve.wait_ge(xob_done[g], xob_done.at(trip, 1))
                    v.tensor_tensor(resid[g][:, :, :], temp[g][:, :, :], temp2[g][:, :, :], ALU.add) \
                        .then_inc(resid_done[g], 1)
                    dve.wait_ge(resid_done[g], resid_done.at(trip, 1))
                    moments(g, AFTER0, trip)
                for g in GROUPS:
                    shift(g, AFTER0, trip)

                for g in GROUPS:
                    dve.wait_ge(norm_done[g], norm_done.at(trip, AFTER0 + 1))
                    v.tensor_copy(h16_hi[g][:, :, :], feat[g][:, :, :]).then_inc(h16_hid[g], 1)
                    dve.wait_ge(h16_hid[g], h16_hid.at(trip, 1))
                    v.tensor_tensor(h16_lo[g][:, :, :], feat[g][:, :, :], h16_hi[g][:, :, :], ALU.subtract) \
                        .then_inc(h16_lod[g], 1)
                for g in GROUPS:
                    for c in range(KC):
                        dve.wait_ge(hT_done[g], hT_done.at(trip, c + 1))
                        v.tensor_tensor(fT_lo[g][:, c, :], hT[g][:, c, :], f32(fT_hi[g][:, c, :]), ALU.subtract) \
                            .then_inc(t_lo[g], 1)
                for t in range(STEPS):
                    for g in GROUPS:
                        for c in range(KC):
                            dve.wait_ge(a_hid[g], a_hid.at(trip, 2 * t + c + 1))
                            v.tensor_tensor(aT_lo[g][:, c, :], bank(g, c), f32(aT_hi[g][:, c, :]), ALU.subtract) \
                                .then_inc(a_lod[g], 1)
                    for g in GROUPS:
                        for c in range(KC):
                            dve.wait_ge(r_done[g], r_done.at(trip, 2 * t + c + 1))
                            v.scalar_tensor_tensor(rh[g][:, c, :], tr[g][:, c, :], 1.0, hT[g][:, c, :], ALU.add,
                                                   ALU.mult).then_inc(rh_step[g], 1)
                        for c in range(KC):
                            dve.wait_ge(rh_step[g], rh_step.at(trip, 6 * t + c + 1))
                            v.tensor_copy(rh_hi[g][:, c, :], rh[g][:, c, :]).then_inc(rh_step[g], 1)
                        for c in range(KC):
                            dve.wait_ge(rh_step[g], rh_step.at(trip, 6 * t + 2 + c + 1))
                            v.tensor_tensor(rh_lo[g][:, c, :], rh[g][:, c, :], f32(rh_hi[g][:, c, :]), ALU.subtract) \
                                .then_inc(rh_step[g], 1)
                    for g in GROUPS:
                        for c in range(KC):
                            dve.wait_ge(hv_done[g], hv_done.at(trip, 2 * t + c + 1))
                            v.tensor_tensor(tr[g][:, c, :], rh[g][:, c, :], hT[g][:, c, :], ALU.subtract) \
                                .then_inc(h_step[g], 1)
                        for c in range(KC):
                            dve.wait_ge(h_step[g], h_step.at(trip, 6 * t + c + 1))
                            v.scalar_tensor_tensor(tr[g][:, c, :], tz[g][:, c, :], 1.0, tr[g][:, c, :], ALU.add,
                                                   ALU.mult).then_inc(h_step[g], 1)
                        for c in range(KC):
                            dve.wait_ge(h_step[g], h_step.at(trip, 6 * t + 2 + c + 1))
                            v.scalar_tensor_tensor(hT[g][:, c, :], tr[g][:, c, :], 0.5, hT[g][:, c, :], ALU.mult,
                                                   ALU.add).then_inc(h_step[g], 1)
                        if t < STEPS - 1:
                            for c in range(KC):
                                dve.wait_ge(h_step[g], h_step.at(trip, 6 * t + 4 + c + 1))
                                v.tensor_copy(fT_hi[g][:, c, :], hT[g][:, c, :]).then_inc(hs_hid[g], 1)
                            for c in range(KC):
                                dve.wait_ge(hs_hid[g], hs_hid.at(trip, 2 * t + c + 1))
                                v.tensor_tensor(fT_lo[g][:, c, :], hT[g][:, c, :], f32(fT_hi[g][:, c, :]),
                                                ALU.subtract).then_inc(hs_lod[g], 1)
                    for g in GROUPS:
                        if t < STEPS - 1:
                            for b in range(2):
                                dve.wait_ge(h16_hid[g], h16_hid.at(trip, 1 + 2 * t + b + 1))
                                v.tensor_tensor(h16_lo[g][:, 2 * b:2 * b + 2, :],
                                                bank(g, b).rearrange("p (i d) -> p i d", i=2),
                                                h16_hi[g][:, 2 * b:2 * b + 2, :], ALU.subtract).then_inc(h16_lod[g], 1)
                        else:
                            dve.wait_ge(hn_ps[g], hn_ps.at(trip, 2 * STEPS))
                            v.tensor_tensor(resid[g][:, :, :].rearrange("p i d -> p (i d)"),
                                            banks(g, 0, 2).rearrange("p b d -> p (b d)"),
                                            feat[g][:, :, :].rearrange("p i d -> p (i d)"), ALU.add) \
                                .then_inc(resid_done[g], 1)
                            dve.wait_ge(resid_done[g], resid_done.at(trip, 2))
                            moments(g, AFTER1, trip)
                for g in GROUPS:
                    shift(g, AFTER1, trip)

                for g in GROUPS:
                    low_part(g, 3, trip)
                for g in GROUPS:
                    dve.wait_ge(gh_done[g], gh_done.at(trip, 1))
                    v.tensor_copy(s1[g][:, :], banks(g, 0, 4)[:, :, D]).then_inc(s1_done[g], 1)
                    dve.wait_ge(gb_done[g], gb_done.at(trip, 1))
                    v.tensor_tensor(g_lo[g][:, :, :], banks(g, 0, 4)[:, :, 0:D], f32(g_hi[g][:, :, :]), ALU.subtract) \
                        .then_inc(gl_done[g], 1)
                for g in GROUPS:
                    dve.wait_ge(s12_done[g], s12_done.at(trip, 1))
                    v.scalar_tensor_tensor(edge2[g][:, :, :], edge[g][:, :, :], ALPHA, edge[g][:, :, :], ALU.mult,
                                           ALU.max).then_inc(edge_step[g], 1)
                    dve.wait_ge(edge_step[g], edge_step.at(trip, 1))
                    v.tensor_tensor(edge2[g][:, :, :], edge2[g][:, :, :], adj_rows(GR), ALU.mult) \
                        .then_inc(edge_step[g], 1)
                    dve.wait_ge(edge_step[g], edge_step.at(trip, 2))
                    v.tensor_reduce(e_inv[g][:, :], edge2[g][:, :, :], AX_X, ALU.max).then_inc(edge_step[g], 1)
                    dve.wait_ge(edge_step[g], edge_step.at(trip, 3))
                    v.tensor_scalar(e_max[g][:, :], e_inv[g][:, :], -1.0, None, ALU.mult).then_inc(edge_step[g], 1)
                for g in GROUPS:
                    dve.wait_ge(eexp_done[g], eexp_done.at(trip, 1))
                    v.reciprocal(e_inv[g][:, :], e_sum[g][:, :]).then_inc(einv_done[g], 1)
                    dve.wait_ge(eT_hid[g], eT_hid.at(trip, 1))
                    v.tensor_tensor(eT_lo[g][:, :, :], bank(g, 1).rearrange("p (i n) -> p i n", i=GR),
                                    f32(eT_hi[g][:, :, :]), ALU.subtract).then_inc(eT_lod[g], 1)
                for g in GROUPS:
                    dve.wait_ge(einv_done[g], einv_done.at(trip, 1))
                    for b in range(2):
                        dve.wait_ge(gp_ps[g], gp_ps.at(trip, b + 1))
                        for j in range(2):
                            i = 2 * b + j
                            last = v.scalar_tensor_tensor(temp[g][:, i, :], bank(g, 2 + b)[:, j * D:(j + 1) * D],
                                                          e_inv[g][:, i:i + 1], temp[g][:, i, :], ALU.mult, ALU.add)
                        last.then_inc(gp_done[g], 1)
                    dve.wait_ge(gp_done[g], gp_done.at(trip, 2))
                    v.tensor_scalar(temp2[g][:, :, :], temp[g][:, :, :], 0.0, None, ALU.min).then_inc(clip_done[g], 1)
                for g in GROUPS:
                    dve.wait_ge(elu_exp[g], elu_exp.at(trip, 1))
                    v.scalar_tensor_tensor(temp[g][:, :, :], temp[g][:, :, :], 0.0, temp2[g][:, :, :], ALU.max, ALU.add) \
                        .then_inc(elu_done[g], 1)
                    dve.wait_ge(elu_done[g], elu_done.at(trip, 1))
                    v.scalar_tensor_tensor(resid[g][:, :, :], temp[g][:, :, :], -1.0, feat[g][:, :, :], ALU.add, ALU.add) \
                        .then_inc(resid_done[g], 1)
                    dve.wait_ge(resid_done[g], resid_done.at(trip, 3))
                    moments(g, AFTER2, trip)
                for g in GROUPS:
                    shift(g, AFTER2, trip)

                for g in GROUPS:
                    low_part(g, 4, trip)
                for g in GROUPS:
                    for c in range(KC):
                        dve.wait_ge(tq_hid[g], tq_hid.at(trip, c + 1))
                        v.tensor_tensor(mov_lo[g][:, c, :, 0:4:3, :],
                                        bank(g, 2 + c).rearrange("p (a q n) -> p a q n", a=2, q=2),
                                        f32(mov_hi[g][:, c, :, 0:4:3, :]), ALU.subtract).then_inc(tq_lod[g], 1)
                for g in GROUPS:
                    dve.wait_ge(vv_hid[g], vv_hid.at(trip, 1))
                    for odd in range(2):
                        at = 2 * P * odd
                        last = v.tensor_tensor(edge[g][:, odd:GR:2, :], banks(g, 0, 4)[:, odd:4:2, at:at + P],
                                               adj_rows(2), ALU.mult)
                    last.then_inc(rel_done[g], 1)
                    for odd in range(2):
                        src = banks(g, 0, 4)[:, odd:4:2, P - odd * P:P - odd * P + D]
                        last = v.tensor_tensor(g_lo[g][:, odd:GR:2, :], src, f32(g_hi[g][:, odd:GR:2, :]), ALU.subtract)
                    last.then_inc(vv_lod[g], 1)
                    dve.wait_ge(rel_done[g], rel_done.at(trip, 1))
                    v.tensor_copy(eT_hi[g][:, :, :], edge[g][:, :, :]).then_inc(rel_hid[g], 1)
                    dve.wait_ge(rel_hid[g], rel_hid.at(trip, 1))
                    v.tensor_tensor(eT_lo[g][:, :, :], edge[g][:, :, :], f32(eT_hi[g][:, :, :]), ALU.subtract) \
                        .then_inc(rel_lod[g], 1)
                for g in GROUPS:
                    dve.wait_ge(ss_ps[g], ss_ps.at(trip, 1))
                    v.tensor_copy(sq_sum[g][:, :], bank(g, 0)[:, 0:2 * GR:2]).then_inc(ss_done[g], 1)
                for g in GROUPS:
                    dve.wait_ge(rn_done[g], rn_done.at(trip, 1))
                    for b in range(2):
                        dve.wait_ge(ov_ps[g], ov_ps.at(trip, b + 1))
                        for j in range(2):
                            i = 2 * b + j
                            last = v.scalar_tensor_tensor(resid[g][:, i, :], bank(g, 2 + b)[:, j * D:(j + 1) * D],
                                                          rel_norm[g][:, i:i + 1], feat[g][:, i, :], ALU.mult, ALU.add)
                    last.then_inc(resid_done[g], 1)
                    dve.wait_ge(resid_done[g], resid_done.at(trip, 4))
                    moments(g, AFTER3, trip)
                for g in GROUPS:
                    shift(g, AFTER3, trip)


_INS = ['x', 'adj', 'L0_gnn_w_qkv', 'L0_gnn_w_proj', 'L0_gnn_b_proj', 'L0_gnn_ln_gamma', 'L0_gnn_ln_beta',
        'L1_gnn_w3_w', 'L1_gnn_w3_b', 'L1_gnn_u3_w', 'L1_gnn_u3_b', 'L1_gnn_w4_w', 'L1_gnn_w4_b', 'L1_gnn_w5_w',
        'L1_gnn_w5_b', 'L1_gnn_u5_w', 'L1_gnn_u5_b', 'L2_gnn_W', 'L2_gnn_a', 'L2_gnn_beta', 'L3_gnn_Wq', 'L3_gnn_Wk',
        'L3_gnn_Wv']
_OUTS = [((64, 128, 256), 'float32')]


def kernel(**inputs):
    import numpy as _np
    import concourse.bacc as _bacc
    from concourse import mybir as _mybir
    from concourse.bass_utils import run_bass_kernel_spmd as _run

    nc = _bacc.Bacc("TRN2", target_bir_lowering=False, num_devices=1)
    arrays, args = {}, []
    for name in _INS:
        a = _np.ascontiguousarray(inputs[name])
        arrays[f"in_{name}_dram"] = a
        args.append(nc.dram_tensor(f"in_{name}_dram", a.shape, _mybir.dt.from_np(a.dtype), kind="ExternalInput").ap())
    for i, (shape, dtype) in enumerate(_OUTS):
        dt = _mybir.dt.from_np(_np.dtype(dtype))
        args.append(nc.dram_tensor(f"out_{i}_dram", shape, dt, kind="ExternalOutput").ap())
    gnn_stack_kernel(nc, *args)
    r = _run(nc, [arrays], core_ids=[0])
    got = tuple(r.results[0][f"out_{i}_dram"] for i in range(len(_OUTS)))
    return got[0]
```

```python
from contextlib import ExitStack

import concourse.bass as bass
from concourse import mybir

F32 = mybir.dt.float32
F32R = mybir.dt.float32r
F16 = mybir.dt.float16
ALU = mybir.AluOpType
ACT = mybir.ActivationFunctionType
AX_X = mybir.AxisListType.X

P = 128
HEADS = 8
LN_EPS = 1e-5
ALPHA = 0.2
STEPS = 3
GR = 2
GROUPS = range(4)
FAR = -30000.0

W34, W4, W5, U3, U5, WM, WV = range(7)


TRIP = [
    ("x_transpose", 0, 39), ("queries", 0, 27), ("keys", 0, 0), ("values", 0, 37), ("scores", 0, 34),
    ("weights", 0, 49), ("mix", 0, 20), ("scores", 1, 17), ("weights", 1, 16), ("mix", 1, 31),
    ("o_transpose", 0, 51), ("project", 0, 28), ("inner_norm", 0, 30), ("rescale", 0, 24), ("add_norm", 0, 33),
    ("norm0", 0, 26), ("state_transpose", 0, 31), ("state_part", 0, 5), ("neighbours", 0, 22),
    ("reset_gate", 0, 8), ("value_sums", 0, 5), ("reset_parts", 0, 0), ("update_gate", 0, 43),
    ("new_value", 0, 19), ("blend", 0, 4), ("state_parts", 0, 14), ("state_rows", 0, 28),
    ("state_part", 1, 49), ("neighbours", 1, 10), ("reset_gate", 1, 16), ("value_sums", 1, 6),
    ("reset_parts", 1, 22), ("update_gate", 1, 29), ("new_value", 1, 44), ("blend", 1, 19),
    ("state_parts", 1, 18), ("state_rows", 1, 7), ("state_part", 2, 24), ("neighbours", 2, 14),
    ("reset_gate", 2, 37), ("value_sums", 2, 17), ("reset_parts", 2, 25), ("update_gate", 2, 0),
    ("new_value", 2, 31), ("blend", 2, 23), ("state_parts", 2, 8), ("state_rows", 2, 33), ("norm1", 0, 10),
    ("load_next", 0, 2), ("f2_transpose", 0, 33), ("features", 0, 42), ("edges", 0, 20), ("edge_exp", 0, 31),
    ("edge_transpose", 0, 35), ("edge_mix", 0, 28), ("elu", 0, 45), ("norm2", 0, 18), ("f3_transpose", 0, 14),
    ("fold", 0, 18), ("relate", 0, 34), ("squares", 0, 80), ("relation_mix", 0, 23), ("norm3", 0, 5)]
SHIFTS = (0.0, 2.0, 1.0, 3.0)


def window():
    whole = sum(w for _, _, w in TRIP)
    entries = []
    for g in GROUPS:
        at = SHIFTS[g] * whole / len(GROUPS)
        for name, n, w in TRIP:
            entries.append((at % whole, g, name, n, int(at >= whole)))
            at += w
    return [(name, n, g, behind) for _, g, name, n, behind in sorted(entries, key=lambda e: e[:2])]


def rises_of(events):
    return [name for name, n in events for _ in range(n)]


IN_BANK = rises_of(
    [("t_ps", 1), ("qkv_ps", 3)] + GR * [("tile_ps", 2), ("score_ps", 1), ("pT_ps", 2), ("pv_ps", 1)]
    + [("t_ps", 1), ("proj_ps", 1), ("t_ps", 1)]
    + STEPS * [("a_ps", 1), ("r_ps", 1), ("z_ps", 1), ("hv_ps", 1), ("hn_ps", 1)]
    + [("t_ps", 1), ("gat_ps", 1), ("s2_ps", 1), ("eT_ps", 1), ("gp_ps", 1)]
    + [("t_ps", 1), ("tq_ps", 1), ("rv_ps", 1), ("ss_ps", 1), ("ov_ps", 1)])
BY_SCALAR = rises_of(
    [("t_hi", 1), ("qkv_hid", 3)] + GR * [("prob_done", 1), ("pT_hid", 2)]
    + [("t_hi", 1), ("norm_done", 2), ("h16_split", 1), ("t_hi", 1), ("hT_done", 1)]
    + [e for t in range(STEPS) for e in (("a_hid", 1), ("r_done", 1), ("rh_hid", 1), ("z_done", 1), ("hv_done", 1),
                                         ("hs_hid", int(t < STEPS - 1)), ("h16_hid", int(t < STEPS - 1)))]
    + [("norm_done", 1), ("t_hi", 1), ("gb_done", 1), ("s12_done", 1), ("eexp_done", 1), ("eT_hid", 1),
       ("elu_exp", 1), ("norm_done", 1)]
    + [("t_hi", 1), ("tq_hid", 1), ("vv_hid", 1), ("sq_done", 1), ("rel_hid", 1), ("norm_done", 1)])
BY_VECTOR = rises_of(
    [("t_lo", 1), ("qkv_lod", 3)] + GR * [("max_step", 2), ("pT_lod", 2), ("o_step", 2)]
    + [("t_lo", 1), ("proj_done", 1), ("moment", 3), ("nmr_done", 1), ("resid_done", 1),
       ("moment", 3), ("nmr_done", 1), ("h16_lod", 1), ("t_lo", 1)]
    + [e for t in range(STEPS) for e in ([("a_lod", 1), ("rh_done", 1), ("rh_lod", 1), ("h_step", 2)]
                                         + ([("hs_lod", 1), ("h16_lod", 1)] if t < STEPS - 1 else
                                            [("resid_done", 1), ("moment", 3)]))]
    + [("nmr_done", 1), ("t_lo", 1), ("s1_done", 1), ("gl_done", 1), ("edge_step", 4), ("einv_done", 1),
       ("eT_lod", 1), ("gp_done", 1), ("clip_done", 1), ("elu_done", 1), ("resid_done", 1), ("moment", 3),
       ("nmr_done", 1)]
    + [("t_lo", 1), ("tq_lod", 1), ("rel_done", 1), ("vv_lod", 1), ("rel_lod", 1), ("ss_done", 1),
       ("resid_done", 1), ("moment", 3), ("nmr_done", 1)])
BY_POOL = rises_of(
    [("xo_done", 1), ("xob_done", 1), ("rstd_done", 1), ("scaled_done", 1), ("rstd_done", 1), ("hd_done", STEPS),
     ("rstd_done", 2), ("rn_done", 1), ("rstd_done", 1)])


class Rises:

    def __init__(self, ctx, nc, name, order):
        self.sems = [ctx.enter_context(nc.semaphore(f"{name}_{g}")) for g in GROUPS]
        self.order = order

    def head_start(self, g):
        return 2 * g * len(self.order)

    def kind(self, name):
        return Kind(self, name)


class Kind:

    def __init__(self, rises, name):
        self.rises = rises
        self.places = [n + 1 for n, other in enumerate(rises.order) if other == name]

    def __getitem__(self, g):
        return self.rises.sems[g]

    def at(self, g, trip, k):
        per_trip = len(self.rises.order)
        place = self.places[k - 1] if k else self.places[-1] - per_trip
        return trip * per_trip + (place + self.rises.head_start(g))


def gnn_stack_kernel(nc, x, adj, w_qkv, w_proj, b_proj, ln_gamma, ln_beta, w3_w, w3_b, u3_w, u3_b, w4_w, w4_b,
                     w5_w, w5_b, u5_w, u5_b, gat_w, gat_a, gat_beta, wq, wk, wv, out):
    B, N, D = x.shape
    HD = D // HEADS
    SCALE = float(HD) ** -0.5
    KC = D // P
    TRIPS = B // (GR * len(GROUPS))
    COLS = GR * N
    HW = HD + 1
    assert N == P and COLS == 256 and KC == 2 and B % (GR * len(GROUPS)) == 0

    with ExitStack() as ctx:
        def sb(name, shape, dt):
            return ctx.enter_context(nc.sbuf_tensor(name, shape, dt))

        def sem(name):
            return ctx.enter_context(nc.semaphore(name))

        def per_group(name, shape, dt):
            return [sb(f"{name}_{g}", shape, dt) for g in GROUPS]

        ps = ctx.enter_context(nc.psum_tensor("ps", [P, 8, 512], F32))

        def bank(g, b):
            return ps[:, 2 * g + b, :]

        def both_banks(g):
            return ps[:, 2 * g:2 * g + 2, :]

        def chunked(t):
            return t.rearrange("p (c n) -> p c n", c=KC)

        def flat(t):
            return t.rearrange("p a b -> p (a b)")

        ident = sb("ident", [P, P], F32)
        ident16 = sb("ident16", [P, P], F16)
        ones = sb("ones", [P, 2], F32)
        gate_cell = sb("gate_cell", [P, 1], F32)
        start_cell = sb("start_cell", [P, 6, len(GROUPS)], F32)
        neg_half = sb("neg_half", [P, GR], F32)
        adj_sb = sb("adj_sb", [P, N], F32)
        adjT16 = sb("adjT16", [P, N], F16)
        far_id = sb("far_id", [P, P], F16)
        far16 = sb("far16", [P, 4, N], F16)
        qkv_hi = sb("qkv_hi", [P, KC, 3 * D], F32R)
        qkv_lo = sb("qkv_lo", [P, KC, 3 * D], F32R)
        proj_hi = sb("proj_hi", [P, KC, D], F32R)
        proj_lo = sb("proj_lo", [P, KC, D], F32R)
        wt_hi = sb("wt_hi", [P, 6, KC, D], F32R)
        wt_lo = sb("wt_lo", [P, 6, KC, D], F32R)
        gat_hi = sb("gat_hi", [P, KC, D + 2], F32R)
        gat_lo = sb("gat_lo", [P, KC, D + 2], F32R)
        wa2_hi = sb("wa2_hi", [P, KC, P], F32R)
        wa2_lo = sb("wa2_lo", [P, KC, P], F32R)
        beta_col = sb("beta_col", [P, 1], F32)
        bproj_row = sb("bproj_row", [P, D], F32)
        gamma_row = sb("gamma_row", [P, D], F32)
        lnbeta_row = sb("lnbeta_row", [P, D], F32)
        bias_raw = sb("bias_raw", [P, 5, KC], F32)
        bias_sum = sb("bias_sum", [P, 3, KC], F32)
        bias_act = sb("bias_act", [P, 3, KC], F32)

        x_in = per_group("x_in", [P, GR, D], F32)
        fT_hi = per_group("fT_hi", [P, KC, COLS], F32R)
        fT_lo = per_group("fT_lo", [P, KC, COLS], F32R)
        q_hi = per_group("q_hi", [P, KC, COLS], F16)
        q_lo = per_group("q_lo", [P, KC, COLS], F16)
        v_hi = per_group("v_hi", [P, GR, HEADS, HW], F16)
        v_lo = per_group("v_lo", [P, GR, HEADS, HW], F16)
        row_max = per_group("row_max", [P, HEADS], F32)
        neg_max = per_group("neg_max", [P, HEADS], F32)
        inv_sum = per_group("inv_sum", [P, HEADS], F32)
        feat = per_group("feat", [P, GR, D], F32)
        resid = per_group("resid", [P, GR, D], F32)
        stats = per_group("stats", [P, GR, 6], F32)
        mean_var = per_group("mean_var", [P, GR, 2], F32)
        var_eps = per_group("var_eps", [P, GR], F32)
        rstd = per_group("rstd", [P, GR], F32)
        neg_mr = per_group("neg_mr", [P, GR], F32)
        aT_hi = per_group("aT_hi", [P, KC, COLS], F32R)
        aT_lo = per_group("aT_lo", [P, KC, COLS], F32R)
        gates = per_group("gates", [P, 2, KC, COLS], F32)
        state = per_group("state", [P, 2, KC, COLS], F32)
        rh_hi = per_group("rh_hi", [P, KC, COLS], F32R)
        rh_lo = per_group("rh_lo", [P, KC, COLS], F32R)
        s1 = per_group("s1", [P, GR], F32)
        e_max = per_group("e_max", [P, GR], F32)
        e_sum = per_group("e_sum", [P, GR], F32)
        e_inv = per_group("e_inv", [P, GR], F32)
        sq_sum = per_group("sq_sum", [P, GR], F32)
        rel_norm = per_group("rel_norm", [P, GR], F32)
        mov_hi = per_group("mov_hi", [P, KC, 4, P], F32R)
        mov_lo = per_group("mov_lo", [P, KC, 4, P], F32R)

        tz, tr = ([t[:, n] for t in gates] for n in range(2))
        hT, rh = ([t[:, n] for t in state] for n in range(2))

        def as_rows(t):
            return t[:, :, :].rearrange("p a b -> p (a b)").rearrange("p (i d) -> p i d", d=D)

        def squares_of(t):
            return [t[:, n] for n in range(2)]

        def head_of(s):
            return 4 * (s % 2) + 2 * (s % 4 // 2) + s // 4

        def banked_relations(g):
            return both_banks(g).rearrange("p b n -> p (b n)").rearrange("p (q n) -> p q n", n=P)[:, 0:7:6, :]

        def banked_values(g):
            return both_banks(g).rearrange("p b n -> p (b n)")[:, P:P + 2 * 3 * P] \
                .rearrange("p (i d) -> p i d", d=3 * P)[:, :, 0:D]

        prob = [t[:, :, :, :].rearrange("p a b c -> p (a b c)").rearrange("p (s n) -> p s n", n=N) for t in gates]
        pT_hi, pT_lo = ([flat(t).bitcast(F16).rearrange("p (s m) -> p s m", m=N) for t in buf] for buf in (rh, hT))
        out_sb = [as_rows(t) for t in tz]
        temp = [as_rows(t) for t in hT]
        temp2 = [as_rows(t) for t in tr]
        k_hi_flat, k_lo_flat = ([t[:, n, :].bitcast(F16) for t in resid] for n in range(2))
        k_hi, k_lo = ([chunked(t) for t in part] for part in (k_hi_flat, k_lo_flat))
        h16_hi = [as_rows(t) for t in q_hi]
        h16_lo = [as_rows(t) for t in q_lo]
        g_hi = [as_rows(t) for t in aT_hi]
        g_lo = [as_rows(t) for t in aT_lo]
        edge = [t[:, 0, :].rearrange("p (i n) -> p i n", n=N) for t in rh]
        edge2 = [t[:, 1, :].rearrange("p (i n) -> p i n", n=N) for t in rh]
        eT_hi = [t[:, 0, :].rearrange("p (i n) -> p i n", n=N) for t in rh_hi]
        eT_lo = [t[:, 0, :].rearrange("p (i n) -> p i n", n=N) for t in rh_lo]
        pair_raw = [t[:, :, :, :].rearrange("p a b c -> p (a b c)").rearrange("p (c d) -> p c d", c=KC)
                    for t in gates[0:3]]
        square_raw = [m for t in state[1:4] for m in squares_of(t)]
        proj_raw = square_raw[5]
        summed = [feat[n][:, :, :] for n in range(4)]
        qkv_raw = [t[:, :, :, :].rearrange("p a b c -> p (a b c)")[:, 0:3 * D] for t in (gates[3], state[0])]
        wv_hi, wv_lo = aT_hi[0], aT_lo[0]
        a_row = resid[0][:, :, :].rearrange("p a b -> p (a b)")
        a_junk = resid[1][:, 0, :]
        gat_raw = [t[:, :, :].rearrange("p a b -> p (a b)")[:, 0:D + 2] for t in resid[2:4]]

        ld_weights = sem("ld_weights")
        ident_made = sem("ident_made")
        prep_v = sem("prep_v")
        prep_pe = sem("prep_pe")
        prep_done = sem("prep_done")

        in_bank = Rises(ctx, nc, "in_bank", IN_BANK)
        by_scalar = Rises(ctx, nc, "by_scalar", BY_SCALAR)
        by_vector = Rises(ctx, nc, "by_vector", BY_VECTOR)
        by_pool = Rises(ctx, nc, "by_pool", BY_POOL)
        x_loads = Rises(ctx, nc, "x_loads", ["x_loaded"] * 16)
        stores = Rises(ctx, nc, "stores", ["out_stored"] * 16)
        x_loaded = x_loads.kind("x_loaded")
        out_stored = stores.kind("out_stored")
        t_ps, t_hi, t_lo = in_bank.kind("t_ps"), by_scalar.kind("t_hi"), by_vector.kind("t_lo")
        qkv_ps, qkv_hid, qkv_lod = in_bank.kind("qkv_ps"), by_scalar.kind("qkv_hid"), by_vector.kind("qkv_lod")
        tile_ps = in_bank.kind("tile_ps")
        score_ps = in_bank.kind("score_ps")
        max_step = by_vector.kind("max_step")
        prob_done = by_scalar.kind("prob_done")
        pT_ps, pT_hid, pT_lod = in_bank.kind("pT_ps"), by_scalar.kind("pT_hid"), by_vector.kind("pT_lod")
        pv_ps = in_bank.kind("pv_ps")
        o_step = by_vector.kind("o_step")
        proj_ps, proj_done = in_bank.kind("proj_ps"), by_vector.kind("proj_done")
        xo_done = by_pool.kind("xo_done")
        xob_done = by_pool.kind("xob_done")
        scaled_done = by_pool.kind("scaled_done")
        resid_done = by_vector.kind("resid_done")
        moment = by_vector.kind("moment")
        rstd_done = by_pool.kind("rstd_done")
        nmr_done = by_vector.kind("nmr_done")
        norm_done = by_scalar.kind("norm_done")
        hT_done = by_scalar.kind("hT_done")
        h16_split = by_scalar.kind("h16_split")
        h16_hid, h16_lod = by_scalar.kind("h16_hid"), by_vector.kind("h16_lod")
        a_ps, a_hid, a_lod = in_bank.kind("a_ps"), by_scalar.kind("a_hid"), by_vector.kind("a_lod")
        r_ps, r_done = in_bank.kind("r_ps"), by_scalar.kind("r_done")
        z_ps, z_done = in_bank.kind("z_ps"), by_scalar.kind("z_done")
        rh_done, rh_hid, rh_lod = by_vector.kind("rh_done"), by_scalar.kind("rh_hid"), by_vector.kind("rh_lod")
        hv_ps, hv_done = in_bank.kind("hv_ps"), by_scalar.kind("hv_done")
        hd_done = by_pool.kind("hd_done")
        h_step = by_vector.kind("h_step")
        hs_hid, hs_lod = by_scalar.kind("hs_hid"), by_vector.kind("hs_lod")
        hn_ps = in_bank.kind("hn_ps")
        gat_ps, s1_done, gb_done, gl_done = (in_bank.kind("gat_ps"), by_vector.kind("s1_done"),
                                             by_scalar.kind("gb_done"), by_vector.kind("gl_done"))
        s2_ps, s12_done = in_bank.kind("s2_ps"), by_scalar.kind("s12_done")
        edge_step = by_vector.kind("edge_step")
        eexp_done, einv_done = by_scalar.kind("eexp_done"), by_vector.kind("einv_done")
        eT_ps, eT_hid, eT_lod = in_bank.kind("eT_ps"), by_scalar.kind("eT_hid"), by_vector.kind("eT_lod")
        gp_ps, gp_done = in_bank.kind("gp_ps"), by_vector.kind("gp_done")
        clip_done, elu_exp, elu_done = (by_vector.kind("clip_done"), by_scalar.kind("elu_exp"),
                                        by_vector.kind("elu_done"))
        tq_ps, tq_hid, tq_lod = in_bank.kind("tq_ps"), by_scalar.kind("tq_hid"), by_vector.kind("tq_lod")
        rv_ps = in_bank.kind("rv_ps")
        vv_hid, vv_lod = by_scalar.kind("vv_hid"), by_vector.kind("vv_lod")
        rel_done, sq_done = by_vector.kind("rel_done"), by_scalar.kind("sq_done")
        rel_hid, rel_lod = by_scalar.kind("rel_hid"), by_vector.kind("rel_lod")
        ss_ps, ss_done, rn_done = in_bank.kind("ss_ps"), by_vector.kind("ss_done"), by_pool.kind("rn_done")
        ov_ps = in_bank.kind("ov_ps")

        INNER, AFTER0, AFTER1, AFTER2, AFTER3 = range(5)

        x_rows = x.rearrange("b n d -> n b d")
        out_rows = out.rearrange("b n d -> n b d")

        def row_of(v):
            return v.rearrange("(a d) -> a d", a=1)

        ORDER = window()

        def issue(steps, trips, order, before=True, after=True):
            for name, n, g, behind in order:
                if name in steps and (before if behind else after):
                    steps[name](g, trips[g] - behind, n)

        def first(trip):
            return isinstance(trip, int) and trip == 0

        def program(eng, steps):
            issue(steps, [0] * len(GROUPS), ORDER, before=False)
            issue(steps, [1] * len(GROUPS), ORDER)
            with eng.Fori(2, TRIPS - 1) as trip:
                issue(steps, [eng.snap(trip) for _ in GROUPS], ORDER)
            issue(steps, [TRIPS - 1] * len(GROUPS), ORDER)
            issue(steps, [TRIPS] * len(GROUPS), ORDER, after=False)

        def adj_rows(n):
            return adj_sb[:, :].unsqueeze(1).to_broadcast([P, n, N])

        loads = [
            (adj_sb[:, :], adj),
            (qkv_raw[0], w_qkv[0:P, :]),
            (qkv_raw[1], w_qkv[P:2 * P, :]),
            (proj_raw, w_proj.rearrange("(c p) o -> p c o", p=P)),
            (pair_raw[0], w3_w.rearrange("(c p) i -> p c i", p=P)),
            (pair_raw[1], w4_w.rearrange("(c p) i -> p c i", p=P)),
            (pair_raw[2], w5_w.rearrange("(c p) i -> p c i", p=P)),
            (square_raw[0], u3_w.rearrange("(c p) i -> p c i", p=P)),
            (square_raw[1], u5_w.rearrange("(c p) i -> p c i", p=P)),
            (square_raw[2], wv.rearrange("(c p) i -> p c i", p=P)),
            (square_raw[3], wq.rearrange("(c p) i -> p c i", p=P)),
            (square_raw[4], wk.rearrange("(c p) i -> p c i", p=P)),
            (gat_raw[0][:, 0:D], gat_w[0:P, :]),
            (gat_raw[1][:, 0:D], gat_w[P:2 * P, :]),
            (a_row, gat_a.rearrange("k a -> a k").to_broadcast([P, 2 * D])),
            (beta_col[:, :], row_of(gat_beta).to_broadcast([P, 1])),
            (bproj_row[:, :], row_of(b_proj).to_broadcast([P, D])),
            (gamma_row[:, :], row_of(ln_gamma).to_broadcast([P, D])),
            (lnbeta_row[:, :], row_of(ln_beta).to_broadcast([P, D])),
        ] + [
            (bias_raw[:, n, c:c + 1], v[c * P:(c + 1) * P].rearrange("(p a) -> p a", a=1))
            for n, v in enumerate((w3_b, w4_b, w5_b, u3_b, u5_b)) for c in range(KC)
        ]

        block = ctx.enter_context(nc.Block())

        @block.sync
        def _(sp):
            def load(g, trip):
                sp.dma_start(x_in[g][:, :, :], x_rows[:, bass.ds(trip * (len(GROUPS) * GR) + g * GR, GR), :]) \
                    .then_inc(x_loaded[g], 16)

            def load_next(g, trip, _n):
                if isinstance(trip, int) and trip == TRIPS - 1:
                    return
                sp.wait_ge(xo_done[g], xo_done.at(g, trip, 1))
                load(g, trip + 1)

            def norm3(g, trip, _n):
                sp.wait_ge(norm_done[g], norm_done.at(g, trip, AFTER3 + 1))
                sp.dma_start(out_rows[:, bass.ds(trip * (len(GROUPS) * GR) + g * GR, GR), :], out_sb[g]) \
                    .then_inc(out_stored[g], 16)

            for g in GROUPS:
                load(g, 0)
            for dst, src in loads:
                sp.dma_start(dst, src).then_inc(ld_weights, 16)
            program(sp, {"load_next": load_next, "norm3": norm3})
            for g in GROUPS:
                sp.wait_ge(out_stored[g], out_stored.at(g, TRIPS, 0))

        @block.gpsimd
        def _(pool):
            nc.gpsimd.memset(ident[:, :], 0.0).then_inc(ident_made, 1)
            pool.wait_ge(ident_made, 1)
            nc.gpsimd.affine_select(out=ident[:, :], in_=ident[:, :], compare_op=ALU.not_equal, fill=1.0, base=0,
                                    pattern=[[-1, P]], channel_multiplier=1).then_inc(ident_made, 1)
            nc.gpsimd.memset(neg_half[:, :], -0.5).then_inc(ident_made, 1)
            nc.gpsimd.memset(ones[:, :], 1.0).then_inc(ident_made, 1)
            for g in GROUPS:
                nc.gpsimd.memset(v_hi[g][:, :, :, HD:HW], 1.0).then_inc(ident_made, 1)
                nc.gpsimd.memset(v_lo[g][:, :, :, HD:HW], 0.0).then_inc(ident_made, 1)
            for n, rises in enumerate((in_bank, by_scalar, by_vector, by_pool, x_loads, stores)):
                for g in GROUPS[1:]:
                    nc.gpsimd.memset(start_cell[:, n, g:g + 1], 0.0).then_inc(rises.sems[g], rises.head_start(g))

            def project(g, trip, _n):
                pool.wait_ge(proj_done[g], proj_done.at(g, trip, 1))
                nc.gpsimd.tensor_tensor(temp2[g], x_in[g][:, :, :], resid[g][:, :, :], ALU.add) \
                    .then_inc(xo_done[g], 1)
                pool.wait_ge(xo_done[g], xo_done.at(g, trip, 1))
                nc.gpsimd.tensor_tensor(temp2[g], temp2[g],
                                        lnbeta_row[:, :].unsqueeze(1).to_broadcast([P, GR, D]), ALU.add) \
                    .then_inc(xob_done[g], 1)

            def rescale(g, trip, _n):
                pool.wait_ge(norm_done[g], norm_done.at(g, trip, INNER + 1))
                nc.gpsimd.tensor_tensor(temp[g], temp[g], gamma_row[:, :].unsqueeze(1).to_broadcast([P, GR, D]),
                                        ALU.mult).then_inc(scaled_done[g], 1)

            def new_value(g, trip, t):
                pool.wait_ge(hv_done[g], hv_done.at(g, trip, t + 1))
                nc.gpsimd.tensor_tensor(flat(tr[g]), flat(rh[g]), flat(hT[g]), ALU.subtract).then_inc(hd_done[g], 1)

            def rsqrt_of(n):
                def step(g, trip, _n):
                    pool.wait_ge(moment[g], moment.at(g, trip, 3 * n + 3))
                    nc.gpsimd.tensor_tensor(rstd[g][:, :], var_eps[g][:, :], neg_half[:, :], ALU.pow) \
                        .then_inc(rstd_done[g], 1)
                return step

            def squares(g, trip, _n):
                pool.wait_ge(ss_done[g], ss_done.at(g, trip, 1))
                nc.gpsimd.tensor_tensor(rel_norm[g][:, :], sq_sum[g][:, :], neg_half[:, :], ALU.pow) \
                    .then_inc(rn_done[g], 1)

            program(pool, {"project": project, "inner_norm": rsqrt_of(INNER), "rescale": rescale,
                           "norm0": rsqrt_of(AFTER0), "new_value": new_value, "norm1": rsqrt_of(AFTER1), "norm2": rsqrt_of(AFTER2), "squares": squares,
                           "norm3": rsqrt_of(AFTER3)})

        @block.tensor
        def _(pe):
            def split_mm(dst, w_hi, w_lo, m_hi, m_lo, start=True, stop=True, shared=False):
                n = 0
                for c in range(KC):
                    for a, b in ((w_hi, m_hi), (w_hi, m_lo), (w_lo, m_hi)):
                        last = nc.tensor.matmul(dst, a(c), b(c), start=start and n == 0,
                                                stop=stop and n == 3 * KC - 1,
                                                skip_group_check=shared or not (start and stop))
                        n += 1
                return last

            def transposed(g, b, src):
                for c in range(KC):
                    for i in range(GR):
                        last = nc.tensor.transpose(chunked(bank(g, b))[:, c, i * P:(i + 1) * P],
                                                   src[:, i, c * P:(c + 1) * P], ident[:, :])
                last.then_inc(t_ps[g], 1)

            def maps(g, b, w_hi, w_lo, f_hi, f_lo, start=True, stop=True):
                for c in range(KC):
                    last = split_mm(chunked(bank(g, b))[:, c, :], lambda k: w_hi(k, c), lambda k: w_lo(k, c),
                                    lambda k: f_hi[:, k, :], lambda k: f_lo[:, k, :], start and c == 0, stop, True)
                return last

            def qkv_map(g, b, first_col):
                return maps(g, b, lambda k, c: qkv_hi[:, k, first_col + c * P:first_col + (c + 1) * P],
                            lambda k, c: qkv_lo[:, k, first_col + c * P:first_col + (c + 1) * P], fT_hi[g], fT_lo[g])

            def gate(g, b, w, f_hi, f_lo, start, stop):
                return maps(g, b, lambda k, c: wt_hi[:, w, k, c * P:(c + 1) * P],
                            lambda k, c: wt_lo[:, w, k, c * P:(c + 1) * P], f_hi[g], f_lo[g], start, stop)

            def rows_times(g, i, dst, w_hi, w_lo, start=True):
                return split_mm(dst, lambda k: fT_hi[g][:, k, i * P:(i + 1) * P],
                                lambda k: fT_lo[g][:, k, i * P:(i + 1) * P], w_hi, w_lo, start, True, True)

            def x_transpose(g, trip, _n):
                pe.wait_ge(x_loaded[g], x_loaded.at(g, trip, 16))
                if not first(trip):
                    pe.wait_ge(resid_done[g], resid_done.at(g, trip, 0))
                transposed(g, 0, x_in[g])

            def queries(g, trip, _n):
                pe.wait_ge(t_lo[g], t_lo.at(g, trip, 1))
                qkv_map(g, 1, 0).then_inc(qkv_ps[g], 1)

            def keys(g, trip, _n):
                qkv_map(g, 0, D).then_inc(qkv_ps[g], 1)

            def values(g, trip, _n):
                pe.wait_ge(qkv_lod[g], qkv_lod.at(g, trip, 1))
                for i in range(GR):
                    last = rows_times(g, i, bank(g, 1)[:, i * D:(i + 1) * D], lambda k: qkv_hi[:, k, 2 * D:3 * D],
                                      lambda k: qkv_lo[:, k, 2 * D:3 * D], i == 0)
                last.then_inc(qkv_ps[g], 1)

            def scores(g, trip, i):
                at = slice(i * N, (i + 1) * N)
                if i == 0:
                    pe.wait_ge(qkv_lod[g], qkv_lod.at(g, trip, 3))
                else:
                    pe.wait_ge(o_step[g], o_step.at(g, trip, 2 * i))
                for b in range(2):
                    nc.tensor.matmul(bank(g, b), far_id[:, :], far16[:, :, :], start=True, stop=False,
                                     skip_group_check=True)
                for j in range(4):
                    rows = slice(HD * j, HD * (j + 1))
                    if j >= 2:
                        pe.wait_ge(tile_ps[g], tile_ps.at(g, trip, 2 * i + j - 1))
                    for c in range(KC):
                        q = 2 * (j // 2) + c
                        for n, (a, b) in enumerate(((q_hi, k_hi), (q_hi, k_lo), (q_lo, k_hi))):
                            last = nc.tensor.matmul(bank(g, j % 2)[:, q * N:(q + 1) * N], a[g][rows, c, at],
                                                    b[g][rows, c, at], start=False, stop=(n == 2),
                                                    skip_group_check=True)
                    if j < 2:
                        last.then_inc(tile_ps[g], 1)
                last.then_inc(score_ps[g], 1)


            def weights(g, trip, i):
                pe.wait_ge(prob_done[g], prob_done.at(g, trip, i + 1))
                for b in range(2):
                    for s in range(4):
                        last = nc.tensor.transpose(bank(g, b)[:, s * N:(s + 1) * N],
                                                   prob[g][:, 4 * b + s, :], ident[:, :])
                    last.then_inc(pT_ps[g], 1)

            def mix(g, trip, i):
                for s in range(HEADS):
                    if s % 4 == 0:
                        pe.wait_ge(pT_lod[g], pT_lod.at(g, trip, 2 * i + s // 4 + 1))
                    h = head_of(s)
                    dst = bank(g, 0)[:, h * HW:(h + 1) * HW]
                    for n, (a, b) in enumerate(((pT_hi, v_hi), (pT_hi, v_lo), (pT_lo, v_hi))):
                        last = nc.tensor.matmul(dst, a[g][:, s, :], b[g][:, i, h, :], start=(n == 0), stop=(n == 2))
                last.then_inc(pv_ps[g], 1)

            def o_transpose(g, trip, _n):
                pe.wait_ge(o_step[g], o_step.at(g, trip, 2 * GR))
                transposed(g, 1, feat[g])

            def project(g, trip, _n):
                pe.wait_ge(t_lo[g], t_lo.at(g, trip, 2))
                for i in range(GR):
                    last = rows_times(g, i, bank(g, 0)[:, i * D:(i + 1) * D], lambda k: proj_hi[:, k, :],
                                      lambda k: proj_lo[:, k, :], i == 0)
                last.then_inc(proj_ps[g], 1)

            def state_transpose(g, trip, _n):
                pe.wait_ge(norm_done[g], norm_done.at(g, trip, AFTER0 + 1))
                transposed(g, 1, feat[g])

            def state_part(g, trip, t):
                if t == 0:
                    pe.wait_ge(t_lo[g], t_lo.at(g, trip, 3))
                else:
                    pe.wait_ge(z_done[g], z_done.at(g, trip, t))
                    pe.wait_ge(hs_lod[g], hs_lod.at(g, trip, t))
                gate(g, 0, U3, fT_hi, fT_lo, True, False)

            def neighbours(g, trip, t):
                if t == 0:
                    pe.wait_ge(hT_done[g], hT_done.at(g, trip, 1))
                else:
                    pe.wait_ge(h16_lod[g], h16_lod.at(g, trip, t + 1))
                for c in range(KC):
                    for i in range(GR):
                        for n, a in enumerate((h16_hi, h16_lo)):
                            last = nc.tensor.matmul(chunked(bank(g, 1))[:, c, i * N:(i + 1) * N],
                                                    a[g][:, i, c * P:(c + 1) * P], adjT16[:, :],
                                                    start=(n == 0), stop=(n == 1))
                last.then_inc(a_ps[g], 1)

            def reset_gate(g, trip, t):
                pe.wait_ge(a_lod[g], a_lod.at(g, trip, t + 1))
                gate(g, 0, W4, aT_hi, aT_lo, False, True).then_inc(r_ps[g], 1)

            def value_sums(g, trip, t):
                gate(g, 1, W5, aT_hi, aT_lo, True, False)

            def update_gate(g, trip, t):
                pe.wait_ge(r_done[g], r_done.at(g, trip, t + 1))
                gate(g, 0, W34, aT_hi, aT_lo, False, True).then_inc(z_ps[g], 1)

            def new_value(g, trip, t):
                pe.wait_ge(rh_lod[g], rh_lod.at(g, trip, t + 1))
                gate(g, 1, U5, rh_hi, rh_lo, False, True).then_inc(hv_ps[g], 1)

            def state_rows(g, trip, t):
                pe.wait_ge(h_step[g], h_step.at(g, trip, 2 * t + 2))
                for i in range(GR):
                    for c in range(KC):
                        last = nc.tensor.transpose(bank(g, 1)[:, i * D + c * P:i * D + (c + 1) * P],
                                                   hT[g][:, c, i * N:(i + 1) * N], ident[:, :])
                last.then_inc(hn_ps[g], 1)

            def f2_transpose(g, trip, _n):
                pe.wait_ge(norm_done[g], norm_done.at(g, trip, AFTER1 + 1))
                transposed(g, 1, feat[g])

            def features(g, trip, _n):
                pe.wait_ge(t_lo[g], t_lo.at(g, trip, 4))
                for i in range(GR):
                    last = rows_times(g, i, bank(g, i)[:, 0:D + 2], lambda k: gat_hi[:, k, :],
                                      lambda k: gat_lo[:, k, :])
                last.then_inc(gat_ps[g], 1)

            def edges(g, trip, _n):
                pe.wait_ge(gl_done[g], gl_done.at(g, trip, 1))
                split_mm(bank(g, 0)[:, 0:COLS], lambda k: wa2_hi[:, k, :], lambda k: wa2_lo[:, k, :],
                         lambda k: fT_hi[g][:, k, :], lambda k: fT_lo[g][:, k, :]).then_inc(s2_ps[g], 1)

            def edge_transpose(g, trip, _n):
                pe.wait_ge(eexp_done[g], eexp_done.at(g, trip, 1))
                for i in range(GR):
                    last = nc.tensor.transpose(bank(g, 1)[:, i * N:(i + 1) * N], edge2[g][:, i, :], ident[:, :])
                last.then_inc(eT_ps[g], 1)

            def mixed_rows(g, b, done):
                for i in range(GR):
                    for n, (a, m) in enumerate(((eT_hi, g_hi), (eT_hi, g_lo), (eT_lo, g_hi))):
                        last = nc.tensor.matmul(bank(g, b)[:, i * D:(i + 1) * D], a[g][:, i, :],
                                                m[g][:, i, :], start=(n == 0), stop=(n == 2))
                last.then_inc(done[g], 1)

            def edge_mix(g, trip, _n):
                pe.wait_ge(eT_lod[g], eT_lod.at(g, trip, 1))
                mixed_rows(g, 0, gp_ps)

            def f3_transpose(g, trip, _n):
                pe.wait_ge(norm_done[g], norm_done.at(g, trip, AFTER2 + 1))
                transposed(g, 1, feat[g])

            def fold(g, trip, _n):
                pe.wait_ge(t_lo[g], t_lo.at(g, trip, 5))
                gate(g, 0, WM, fT_hi, fT_lo, True, True).then_inc(tq_ps[g], 1)

            def relate(g, trip, _n):
                pe.wait_ge(tq_lod[g], tq_lod.at(g, trip, 1))
                for i in range(GR):
                    last = rows_times(g, i, bank(g, i)[:, 0:3 * P], lambda k: mov_hi[g][:, k, i:i + 3, :],
                                      lambda k: mov_lo[g][:, k, i:i + 3, :])
                last.then_inc(rv_ps[g], 1)

            def squares(g, trip, _n):
                pe.wait_ge(sq_done[g], sq_done.at(g, trip, 1))
                pe.wait_ge(vv_lod[g], vv_lod.at(g, trip, 1))
                for i in range(GR):
                    last = nc.tensor.matmul(bank(g, 0)[:, 2 * i:2 * i + 2], edge2[g][:, i, :], ones[:, :],
                                            start=True, stop=True)
                last.then_inc(ss_ps[g], 1)

            def relation_mix(g, trip, _n):
                pe.wait_ge(rel_lod[g], rel_lod.at(g, trip, 1))
                mixed_rows(g, 1, ov_ps)

            pe.wait_ge(ident_made, 4 + 2 * len(GROUPS))
            pe.wait_ge(prep_v, 5)
            srcs = [summed[0], summed[1], summed[2], square_raw[0], summed[3], square_raw[2]]
            for n, src in zip((W34, W4, W5, U3, U5, WV), srcs):
                for oc in range(KC):
                    for dc in range(KC):
                        nc.tensor.transpose(ps[:, n, dc * D + oc * P:dc * D + (oc + 1) * P],
                                            src[:, oc, dc * P:(dc + 1) * P], ident[:, :]).then_inc(prep_pe, 1)
            for dc in range(KC):
                for c in range(KC):
                    nc.tensor.matmul(ps[:, WM, dc * D:(dc + 1) * D], square_raw[3][:, c, dc * P:(dc + 1) * P],
                                     square_raw[4][:, c, :], start=(c == 0), stop=(c == KC - 1)).then_inc(prep_pe, 1)
            nc.tensor.transpose(ps[:, 7, 0:P], adj_sb[:, :], ident[:, :]).then_inc(prep_pe, 1)
            pe.wait_ge(prep_done, 1)

            program(pe, {"x_transpose": x_transpose, "queries": queries, "keys": keys, "values": values,
                         "scores": scores, "weights": weights, "mix": mix, "o_transpose": o_transpose,
                         "project": project, "state_transpose": state_transpose, "state_part": state_part,
                         "neighbours": neighbours, "reset_gate": reset_gate, "value_sums": value_sums,
                         "update_gate": update_gate, "new_value": new_value, "state_rows": state_rows,
                         "f2_transpose": f2_transpose, "features": features, "edges": edges,
                         "edge_transpose": edge_transpose, "edge_mix": edge_mix, "f3_transpose": f3_transpose,
                         "fold": fold, "relate": relate, "squares": squares, "relation_mix": relation_mix})

        @block.scalar
        def _(act):
            def whole(t):
                return t[:, :, :].rearrange("p a b -> p (a b)")

            def high_part(s, b):
                def step(g, trip, _n):
                    act.wait_ge(t_ps[g], t_ps.at(g, trip, s + 1))
                    nc.scalar.activation(whole(fT_hi[g]), bank(g, b), ACT.Copy).then_inc(t_hi[g], 1)
                return step

            def normalised(n, dst):
                def step(g, trip, _n):
                    act.wait_ge(nmr_done[g], nmr_done.at(g, trip, n + 1))
                    for i in range(GR):
                        last = nc.scalar.activation(dst[g][:, i, :], resid[g][:, i, :], ACT.Identity,
                                                    scale=rstd[g][:, i:i + 1], bias=neg_mr[g][:, i:i + 1])
                    last.then_inc(norm_done[g], 1)
                return step

            def queries(g, trip, _n):
                act.wait_ge(qkv_ps[g], qkv_ps.at(g, trip, 1))
                nc.scalar.activation(whole(q_hi[g]), bank(g, 1), ACT.Copy).then_inc(qkv_hid[g], 1)

            def keys(g, trip, _n):
                act.wait_ge(qkv_ps[g], qkv_ps.at(g, trip, 2))
                nc.scalar.activation(k_hi_flat[g], bank(g, 0), ACT.Copy).then_inc(qkv_hid[g], 1)

            def values(g, trip, _n):
                act.wait_ge(qkv_ps[g], qkv_ps.at(g, trip, 3))
                nc.scalar.activation(v_hi[g][:, :, :, 0:HD], bank(g, 1).rearrange("p (i h d) -> p i h d", i=GR, h=HEADS),
                                     ACT.Copy).then_inc(qkv_hid[g], 1)

            def scores(g, trip, i):
                act.wait_ge(max_step[g], max_step.at(g, trip, 2 * i + 2))
                if i == 0 and not first(trip):
                    act.wait_ge(out_stored[g], out_stored.at(g, trip, 0))
                for s in range(HEADS):
                    last = nc.scalar.activation(prob[g][:, s, :],
                                                bank(g, s // 4)[:, (s % 4) * N:(s % 4 + 1) * N], ACT.Exp,
                                                bias=neg_max[g][:, s:s + 1], scale=SCALE)
                last.then_inc(prob_done[g], 1)

            def weights(g, trip, i):
                for b in range(2):
                    act.wait_ge(pT_ps[g], pT_ps.at(g, trip, 2 * i + b + 1))
                    nc.scalar.activation(pT_hi[g][:, 4 * b:4 * b + 4, :], bank(g, b), ACT.Copy) \
                        .then_inc(pT_hid[g], 1)

            def state_transpose(g, trip, _n):
                act.wait_ge(norm_done[g], norm_done.at(g, trip, AFTER0 + 1))
                nc.scalar.activation(h16_hi[g], feat[g][:, :, :], ACT.Copy).then_inc(h16_split[g], 1)
                act.wait_ge(t_ps[g], t_ps.at(g, trip, 3))
                nc.scalar.activation(whole(fT_hi[g]), bank(g, 1), ACT.Copy).then_inc(t_hi[g], 1)
                nc.scalar.activation(flat(hT[g]), bank(g, 1), ACT.Copy).then_inc(hT_done[g], 1)

            def neighbours(g, trip, t):
                act.wait_ge(a_ps[g], a_ps.at(g, trip, t + 1))
                nc.scalar.activation(whole(aT_hi[g]), bank(g, 1), ACT.Copy).then_inc(a_hid[g], 1)

            def reset_gate(g, trip, t):
                act.wait_ge(r_ps[g], r_ps.at(g, trip, t + 1))
                for c in range(KC):
                    last = nc.scalar.activation(tr[g][:, c, :], chunked(bank(g, 0))[:, c, :], ACT.Tanh,
                                                bias=bias_act[:, 1, c:c + 1], scale=0.5)
                last.then_inc(r_done[g], 1)

            def reset_parts(g, trip, t):
                act.wait_ge(rh_done[g], rh_done.at(g, trip, t + 1))
                nc.scalar.activation(whole(rh_hi[g]), flat(rh[g]), ACT.Copy).then_inc(rh_hid[g], 1)

            def update_gate(g, trip, t):
                act.wait_ge(z_ps[g], z_ps.at(g, trip, t + 1))
                for c in range(KC):
                    last = nc.scalar.activation(tz[g][:, c, :], chunked(bank(g, 0))[:, c, :], ACT.Tanh,
                                                bias=bias_act[:, 0, c:c + 1], scale=0.5)
                last.then_inc(z_done[g], 1)

            def new_value(g, trip, t):
                act.wait_ge(hv_ps[g], hv_ps.at(g, trip, t + 1))
                for c in range(KC):
                    last = nc.scalar.activation(rh[g][:, c, :], chunked(bank(g, 1))[:, c, :], ACT.Tanh,
                                                bias=bias_act[:, 2, c:c + 1], scale=1.0)
                last.then_inc(hv_done[g], 1)

            def state_parts(g, trip, t):
                if t < STEPS - 1:
                    act.wait_ge(h_step[g], h_step.at(g, trip, 2 * t + 2))
                    nc.scalar.activation(whole(fT_hi[g]), flat(hT[g]), ACT.Copy).then_inc(hs_hid[g], 1)

            def state_rows(g, trip, t):
                if t < STEPS - 1:
                    act.wait_ge(hn_ps[g], hn_ps.at(g, trip, t + 1))
                    nc.scalar.activation(flat(h16_hi[g]), bank(g, 1), ACT.Copy).then_inc(h16_hid[g], 1)

            def features(g, trip, _n):
                act.wait_ge(gat_ps[g], gat_ps.at(g, trip, 1))
                nc.scalar.activation(g_hi[g], both_banks(g)[:, :, 0:D], ACT.Copy)
                nc.scalar.activation(temp[g], both_banks(g)[:, :, 0:D], ACT.Copy,
                                     scale=beta_col[:, 0:1]).then_inc(gb_done[g], 1)

            def edges(g, trip, _n):
                act.wait_ge(s1_done[g], s1_done.at(g, trip, 1))
                act.wait_ge(s2_ps[g], s2_ps.at(g, trip, 1))
                for i in range(GR):
                    last = nc.scalar.activation(edge[g][:, i, :], bank(g, 0)[:, i * N:(i + 1) * N],
                                                ACT.Identity, bias=s1[g][:, i:i + 1], scale=1.0)
                last.then_inc(s12_done[g], 1)

            def edge_exp(g, trip, _n):
                act.wait_ge(edge_step[g], edge_step.at(g, trip, 4))
                for i in range(GR):
                    last = nc.scalar.activation(edge2[g][:, i, :], edge2[g][:, i, :], ACT.Exp,
                                                bias=e_max[g][:, i:i + 1], scale=1.0, accum_out=e_sum[g][:, i:i + 1])
                last.then_inc(eexp_done[g], 1)

            def edge_transpose(g, trip, _n):
                act.wait_ge(eT_ps[g], eT_ps.at(g, trip, 1))
                nc.scalar.activation(eT_hi[g], bank(g, 1)[:, 0:COLS].rearrange("p (i n) -> p i n", i=GR), ACT.Copy) \
                    .then_inc(eT_hid[g], 1)

            def elu(g, trip, _n):
                act.wait_ge(clip_done[g], clip_done.at(g, trip, 1))
                nc.scalar.activation(temp2[g], temp2[g], ACT.Exp).then_inc(elu_exp[g], 1)

            def fold(g, trip, _n):
                act.wait_ge(tq_ps[g], tq_ps.at(g, trip, 1))
                nc.scalar.activation(mov_hi[g][:, :, 0:4:3, :],
                                     bank(g, 0).rearrange("p (c q n) -> p c q n", c=KC, q=GR), ACT.Copy) \
                    .then_inc(tq_hid[g], 1)

            def relate(g, trip, _n):
                act.wait_ge(rv_ps[g], rv_ps.at(g, trip, 1))
                nc.scalar.activation(g_hi[g], banked_values(g), ACT.Copy).then_inc(vv_hid[g], 1)

            def squares(g, trip, _n):
                act.wait_ge(rel_done[g], rel_done.at(g, trip, 1))
                nc.scalar.activation(edge2[g], edge[g], ACT.Square).then_inc(sq_done[g], 1)
                nc.scalar.activation(eT_hi[g], edge[g], ACT.Copy).then_inc(rel_hid[g], 1)

            act.wait_ge(prep_done, 1)
            program(act, {"x_transpose": high_part(0, 0), "queries": queries, "keys": keys, "values": values,
                          "scores": scores, "weights": weights, "o_transpose": high_part(1, 1),
                          "inner_norm": normalised(INNER, temp), "norm0": normalised(AFTER0, feat),
                          "state_transpose": state_transpose, "neighbours": neighbours, "reset_gate": reset_gate,
                          "reset_parts": reset_parts, "update_gate": update_gate, "new_value": new_value,
                          "state_parts": state_parts, "state_rows": state_rows, "norm1": normalised(AFTER1, feat), "f2_transpose": high_part(3, 1), "features": features,
                          "edges": edges, "edge_exp": edge_exp, "edge_transpose": edge_transpose, "elu": elu,
                          "norm2": normalised(AFTER2, feat), "f3_transpose": high_part(4, 1), "fold": fold,
                          "relate": relate, "squares": squares, "norm3": normalised(AFTER3, out_sb)})

        @block.vector
        def _(dve):
            v = nc.vector

            def f32(t):
                return t.bitcast(F32)

            def whole(t):
                return t[:, :, :].rearrange("p a b -> p (a b)")

            dve.wait_ge(ld_weights, 16 * len(loads))
            dve.wait_ge(ident_made, 4 + 2 * len(GROUPS))
            for n in range(3):
                v.tensor_tensor(summed[n], pair_raw[n][:, :, 0:D], pair_raw[n][:, :, D:2 * D], ALU.add) \
                    .then_inc(prep_v, 1)
            v.tensor_scalar(summed[3], square_raw[1], 0.5, None, ALU.mult).then_inc(prep_v, 1)
            dve.wait_ge(prep_v, 4)
            v.tensor_tensor(summed[0], summed[0], summed[1], ALU.subtract).then_inc(prep_v, 1)
            for c in range(KC):
                for n in range(2):
                    v.tensor_tensor_reduce(out=a_junk, in0=gat_raw[c][:, 0:D], in1=a_row[:, n * D:(n + 1) * D],
                                           scale=1.0, scalar=0.0, op0=ALU.mult, op1=ALU.add,
                                           accum_out=gat_raw[c][:, D + n:D + n + 1]).then_inc(prep_v, 1)
                    dve.wait_ge(prep_v, 5 + 2 * c + n + 1)
            v.tensor_tensor(bias_sum[:, 0:2, :], bias_raw[:, 0:2, :],
                            bias_raw[:, 3:4, :].to_broadcast([P, 2, KC]), ALU.add).then_inc(prep_v, 1)
            v.tensor_tensor(bias_sum[:, 2, :], bias_raw[:, 2, :], bias_raw[:, 4, :], ALU.add).then_inc(prep_v, 1)
            v.tensor_scalar(far_id[:, :], ident[:, :], FAR, None, ALU.mult).then_inc(prep_v, 1)
            v.tensor_scalar(far16[:, :, :], adj_rows(4), 0.0, -FAR, ALU.is_equal, ALU.mult).then_inc(prep_v, 1)
            for c in range(KC):
                v.tensor_copy(qkv_hi[:, c, :], qkv_raw[c]).then_inc(prep_v, 1)
            v.tensor_copy(proj_hi[:, :, :], proj_raw).then_inc(prep_v, 1)
            for c in range(KC):
                v.tensor_copy(gat_hi[:, c, :], gat_raw[c]).then_inc(prep_v, 1)
            dve.wait_ge(prep_v, 18)
            v.tensor_scalar(bias_act[:, 0:2, :], bias_sum[:, 0:2, :], 0.5, None, ALU.mult).then_inc(prep_v, 1)
            v.tensor_copy(bias_act[:, 2, :], bias_sum[:, 2, :]).then_inc(prep_v, 1)
            for c in range(KC):
                v.tensor_tensor(qkv_lo[:, c, :], qkv_raw[c], f32(qkv_hi[:, c, :]), ALU.subtract).then_inc(prep_v, 1)
            v.tensor_tensor(proj_lo[:, :, :], proj_raw, f32(proj_hi[:, :, :]), ALU.subtract) \
                .then_inc(prep_v, 1)
            for c in range(KC):
                v.tensor_tensor(gat_lo[:, c, :], gat_raw[c], f32(gat_hi[:, c, :]), ALU.subtract).then_inc(prep_v, 1)
            dve.wait_ge(prep_v, 25)
            for c in range(KC):
                v.tensor_copy(wa2_hi[:, c, :], f32(gat_hi[:, c, D + 1:D + 2]).to_broadcast([P, P])).then_inc(prep_v, 1)
                v.tensor_copy(wa2_lo[:, c, :], f32(gat_lo[:, c, D + 1:D + 2]).to_broadcast([P, P])).then_inc(prep_v, 1)
            dve.wait_ge(prep_pe, 29)
            for n in range(7):
                src = ps[:, n, :].rearrange("p (c o) -> p c o", c=KC)
                hi, lo = (wv_hi[:, :, :], wv_lo[:, :, :]) if n == WV else (wt_hi[:, n], wt_lo[:, n])
                v.tensor_copy(hi, src).then_inc(prep_v, 1)
                dve.wait_ge(prep_v, 29 + 2 * n + 1)
                v.tensor_tensor(lo, src, f32(hi), ALU.subtract).then_inc(prep_v, 1)
            v.tensor_copy(adjT16[:, :], ps[:, 7, 0:P]).then_inc(prep_v, 1)
            dve.wait_ge(prep_v, 44)
            for g in GROUPS:
                for c in range(KC):
                    v.tensor_copy(mov_hi[g][:, c, 1:3, :].rearrange("p q n -> p (q n)"),
                                  f32(wv_hi[:, c, :])).then_inc(prep_v, 1)
                    v.tensor_copy(mov_lo[g][:, c, 1:3, :].rearrange("p q n -> p (q n)"),
                                  f32(wv_lo[:, c, :])).then_inc(prep_v, 1)
            dve.wait_ge(prep_v, 44 + 2 * KC * len(GROUPS))
            v.memset(a_junk[:, 0:1], 0.0).then_inc(prep_done, 1)

            def low_part(s, b):
                def step(g, trip, _n):
                    dve.wait_ge(t_hi[g], t_hi.at(g, trip, s + 1))
                    v.tensor_tensor(whole(fT_lo[g]), bank(g, b), f32(whole(fT_hi[g])), ALU.subtract) \
                        .then_inc(t_lo[g], 1)
                return step

            def moments(g, n, trip):
                for i in range(GR):
                    last = v.bn_stats(stats[g][:, i, :], resid[g][:, i, :])
                last.then_inc(moment[g], 1)
                dve.wait_ge(moment[g], moment.at(g, trip, 3 * n + 1))
                v.memset(gate_cell[:, :], 0.0)
                for i in range(GR):
                    last = v.bn_aggr(mean_var[g][:, i, :], stats[g][:, i, :])
                last.then_inc(moment[g], 1)
                dve.wait_ge(moment[g], moment.at(g, trip, 3 * n + 2))
                v.tensor_scalar(var_eps[g][:, :], mean_var[g][:, :, 1], LN_EPS, None, ALU.add).then_inc(moment[g], 1)

            def shift(n):
                def step(g, trip, _n):
                    dve.wait_ge(rstd_done[g], rstd_done.at(g, trip, n + 1))
                    v.scalar_tensor_tensor(neg_mr[g][:, :], mean_var[g][:, :, 0], -1.0, rstd[g][:, :], ALU.mult,
                                           ALU.mult).then_inc(nmr_done[g], 1)
                return step

            def queries(g, trip, _n):
                dve.wait_ge(qkv_hid[g], qkv_hid.at(g, trip, 1))
                v.tensor_tensor(whole(q_lo[g]), bank(g, 1), whole(q_hi[g]), ALU.subtract).then_inc(qkv_lod[g], 1)

            def keys(g, trip, _n):
                dve.wait_ge(qkv_hid[g], qkv_hid.at(g, trip, 2))
                v.tensor_tensor(k_lo_flat[g], bank(g, 0), k_hi_flat[g], ALU.subtract).then_inc(qkv_lod[g], 1)

            def values(g, trip, _n):
                dve.wait_ge(qkv_hid[g], qkv_hid.at(g, trip, 3))
                v.tensor_tensor(v_lo[g][:, :, :, 0:HD], bank(g, 1).rearrange("p (i h d) -> p i h d", i=GR, h=HEADS),
                                v_hi[g][:, :, :, 0:HD], ALU.subtract).then_inc(qkv_lod[g], 1)

            def scores(g, trip, i):
                dve.wait_ge(score_ps[g], score_ps.at(g, trip, i + 1))
                v.tensor_reduce(row_max[g][:, :], both_banks(g).rearrange("p b (q m) -> p (b q) m", q=4),
                                AX_X, ALU.max).then_inc(max_step[g], 1)
                dve.wait_ge(max_step[g], max_step.at(g, trip, 2 * i + 1))
                v.tensor_scalar(neg_max[g][:, :], row_max[g][:, :], -SCALE, None, ALU.mult).then_inc(max_step[g], 1)

            def weights(g, trip, i):
                for b in range(2):
                    dve.wait_ge(pT_hid[g], pT_hid.at(g, trip, 2 * i + b + 1))
                    v.tensor_tensor(pT_lo[g][:, 4 * b:4 * b + 4, :], bank(g, b).rearrange("p (s m) -> p s m", s=4),
                                    pT_hi[g][:, 4 * b:4 * b + 4, :], ALU.subtract).then_inc(pT_lod[g], 1)

            def mix(g, trip, i):
                pv = bank(g, 0)[:, 0:HEADS * HW].rearrange("p (h d) -> p h d", h=HEADS)
                dve.wait_ge(pv_ps[g], pv_ps.at(g, trip, i + 1))
                v.reciprocal(inv_sum[g][:, :], pv[:, :, HD]).then_inc(o_step[g], 1)
                dve.wait_ge(o_step[g], o_step.at(g, trip, 2 * i + 1))
                v.tensor_tensor(feat[g][:, i, :].rearrange("p (h d) -> p h d", h=HEADS), pv[:, :, 0:HD],
                                inv_sum[g][:, :].unsqueeze(2).to_broadcast([P, HEADS, HD]), ALU.mult) \
                    .then_inc(o_step[g], 1)

            def project(g, trip, _n):
                dve.wait_ge(proj_ps[g], proj_ps.at(g, trip, 1))
                v.tensor_tensor(resid[g][:, :, :], bank(g, 0).rearrange("p (i d) -> p i d", i=GR),
                                bproj_row[:, :].unsqueeze(1).to_broadcast([P, GR, D]), ALU.add) \
                    .then_inc(proj_done[g], 1)
                dve.wait_ge(proj_done[g], proj_done.at(g, trip, 1))
                moments(g, INNER, trip)

            def add_norm(g, trip, _n):
                dve.wait_ge(scaled_done[g], scaled_done.at(g, trip, 1))
                v.tensor_tensor(resid[g][:, :, :], temp[g], temp2[g], ALU.add).then_inc(resid_done[g], 1)
                dve.wait_ge(resid_done[g], resid_done.at(g, trip, 1))
                moments(g, AFTER0, trip)

            def state_transpose(g, trip, _n):
                dve.wait_ge(h16_split[g], h16_split.at(g, trip, 1))
                v.tensor_tensor(h16_lo[g], feat[g][:, :, :], h16_hi[g], ALU.subtract).then_inc(h16_lod[g], 1)
                dve.wait_ge(hT_done[g], hT_done.at(g, trip, 1))
                v.tensor_tensor(whole(fT_lo[g]), flat(hT[g]), f32(whole(fT_hi[g])), ALU.subtract) \
                    .then_inc(t_lo[g], 1)

            def neighbours(g, trip, t):
                dve.wait_ge(a_hid[g], a_hid.at(g, trip, t + 1))
                v.tensor_tensor(whole(aT_lo[g]), bank(g, 1), f32(whole(aT_hi[g])), ALU.subtract) \
                    .then_inc(a_lod[g], 1)

            def reset_gate(g, trip, t):
                dve.wait_ge(r_done[g], r_done.at(g, trip, t + 1))
                v.scalar_tensor_tensor(flat(rh[g]), flat(tr[g]), 1.0, flat(hT[g]), ALU.add, ALU.mult) \
                    .then_inc(rh_done[g], 1)

            def reset_parts(g, trip, t):
                dve.wait_ge(rh_hid[g], rh_hid.at(g, trip, t + 1))
                v.tensor_tensor(whole(rh_lo[g]), flat(rh[g]), f32(whole(rh_hi[g])), ALU.subtract) \
                    .then_inc(rh_lod[g], 1)

            def blend(g, trip, t):
                dve.wait_ge(hd_done[g], hd_done.at(g, trip, t + 1))
                v.scalar_tensor_tensor(flat(tr[g]), flat(tz[g]), 1.0, flat(tr[g]), ALU.add, ALU.mult) \
                    .then_inc(h_step[g], 1)
                dve.wait_ge(h_step[g], h_step.at(g, trip, 2 * t + 1))
                v.scalar_tensor_tensor(flat(hT[g]), flat(tr[g]), 0.5, flat(hT[g]), ALU.mult, ALU.add) \
                    .then_inc(h_step[g], 1)

            def state_parts(g, trip, t):
                if t < STEPS - 1:
                    dve.wait_ge(hs_hid[g], hs_hid.at(g, trip, t + 1))
                    v.tensor_tensor(whole(fT_lo[g]), flat(hT[g]), f32(whole(fT_hi[g])), ALU.subtract) \
                        .then_inc(hs_lod[g], 1)

            def state_rows(g, trip, t):
                if t < STEPS - 1:
                    dve.wait_ge(h16_hid[g], h16_hid.at(g, trip, t + 1))
                    v.tensor_tensor(flat(h16_lo[g]), bank(g, 1), flat(h16_hi[g]), ALU.subtract) \
                        .then_inc(h16_lod[g], 1)
                else:
                    dve.wait_ge(hn_ps[g], hn_ps.at(g, trip, STEPS))
                    v.tensor_tensor(whole(resid[g]), bank(g, 1), whole(feat[g]), ALU.add).then_inc(resid_done[g], 1)
                    dve.wait_ge(resid_done[g], resid_done.at(g, trip, 2))
                    moments(g, AFTER1, trip)

            def features(g, trip, _n):
                dve.wait_ge(gb_done[g], gb_done.at(g, trip, 1))
                v.tensor_copy(s1[g][:, :], both_banks(g)[:, :, D]).then_inc(s1_done[g], 1)
                v.tensor_tensor(g_lo[g], both_banks(g)[:, :, 0:D], f32(g_hi[g]), ALU.subtract).then_inc(gl_done[g], 1)

            def edges(g, trip, _n):
                dve.wait_ge(s12_done[g], s12_done.at(g, trip, 1))
                v.scalar_tensor_tensor(edge2[g], edge[g], ALPHA, edge[g], ALU.mult, ALU.max).then_inc(edge_step[g], 1)
                dve.wait_ge(edge_step[g], edge_step.at(g, trip, 1))
                v.tensor_tensor(edge2[g], edge2[g], adj_rows(GR), ALU.mult).then_inc(edge_step[g], 1)
                dve.wait_ge(edge_step[g], edge_step.at(g, trip, 2))
                v.tensor_reduce(e_inv[g][:, :], edge2[g], AX_X, ALU.max).then_inc(edge_step[g], 1)
                dve.wait_ge(edge_step[g], edge_step.at(g, trip, 3))
                v.tensor_scalar(e_max[g][:, :], e_inv[g][:, :], -1.0, None, ALU.mult).then_inc(edge_step[g], 1)

            def edge_transpose(g, trip, _n):
                dve.wait_ge(eexp_done[g], eexp_done.at(g, trip, 1))
                v.reciprocal(e_inv[g][:, :], e_sum[g][:, :]).then_inc(einv_done[g], 1)
                dve.wait_ge(eT_hid[g], eT_hid.at(g, trip, 1))
                v.tensor_tensor(eT_lo[g], bank(g, 1)[:, 0:COLS].rearrange("p (i n) -> p i n", i=GR),
                                f32(eT_hi[g]), ALU.subtract).then_inc(eT_lod[g], 1)

            def edge_mix(g, trip, _n):
                dve.wait_ge(einv_done[g], einv_done.at(g, trip, 1))
                dve.wait_ge(gp_ps[g], gp_ps.at(g, trip, 1))
                for i in range(GR):
                    last = v.scalar_tensor_tensor(temp[g][:, i, :], bank(g, 0)[:, i * D:(i + 1) * D],
                                                  e_inv[g][:, i:i + 1], temp[g][:, i, :], ALU.mult, ALU.add)
                last.then_inc(gp_done[g], 1)
                dve.wait_ge(gp_done[g], gp_done.at(g, trip, 1))
                v.tensor_scalar(temp2[g], temp[g], 0.0, None, ALU.min).then_inc(clip_done[g], 1)

            def elu(g, trip, _n):
                dve.wait_ge(elu_exp[g], elu_exp.at(g, trip, 1))
                v.scalar_tensor_tensor(temp[g], temp[g], 0.0, temp2[g], ALU.max, ALU.add).then_inc(elu_done[g], 1)
                dve.wait_ge(elu_done[g], elu_done.at(g, trip, 1))
                v.scalar_tensor_tensor(resid[g][:, :, :], temp[g], -1.0, feat[g][:, :, :], ALU.add, ALU.add) \
                    .then_inc(resid_done[g], 1)
                dve.wait_ge(resid_done[g], resid_done.at(g, trip, 3))
                moments(g, AFTER2, trip)

            def fold(g, trip, _n):
                dve.wait_ge(tq_hid[g], tq_hid.at(g, trip, 1))
                v.tensor_tensor(mov_lo[g][:, :, 0:4:3, :], bank(g, 0).rearrange("p (c q n) -> p c q n", c=KC, q=GR),
                                f32(mov_hi[g][:, :, 0:4:3, :]), ALU.subtract).then_inc(tq_lod[g], 1)

            def relate(g, trip, _n):
                dve.wait_ge(vv_hid[g], vv_hid.at(g, trip, 1))
                v.tensor_tensor(edge[g], banked_relations(g), adj_rows(GR), ALU.mult).then_inc(rel_done[g], 1)
                v.tensor_tensor(g_lo[g], banked_values(g), f32(g_hi[g]), ALU.subtract).then_inc(vv_lod[g], 1)

            def squares(g, trip, _n):
                dve.wait_ge(rel_hid[g], rel_hid.at(g, trip, 1))
                v.tensor_tensor(eT_lo[g], edge[g], f32(eT_hi[g]), ALU.subtract).then_inc(rel_lod[g], 1)
                dve.wait_ge(ss_ps[g], ss_ps.at(g, trip, 1))
                v.tensor_copy(sq_sum[g][:, :], bank(g, 0)[:, 0:2 * GR:2]).then_inc(ss_done[g], 1)

            def relation_mix(g, trip, _n):
                dve.wait_ge(rn_done[g], rn_done.at(g, trip, 1))
                dve.wait_ge(ov_ps[g], ov_ps.at(g, trip, 1))
                for i in range(GR):
                    last = v.scalar_tensor_tensor(resid[g][:, i, :], bank(g, 1)[:, i * D:(i + 1) * D],
                                                  rel_norm[g][:, i:i + 1], feat[g][:, i, :], ALU.mult, ALU.add)
                last.then_inc(resid_done[g], 1)
                dve.wait_ge(resid_done[g], resid_done.at(g, trip, 4))
                moments(g, AFTER3, trip)

            program(dve, {"x_transpose": low_part(0, 0), "queries": queries, "keys": keys, "values": values,
                          "scores": scores, "weights": weights, "mix": mix, "o_transpose": low_part(1, 1),
                          "project": project, "inner_norm": shift(INNER), "add_norm": add_norm, "norm0": shift(AFTER0),
                          "state_transpose": state_transpose, "neighbours": neighbours, "reset_gate": reset_gate,
                          "reset_parts": reset_parts, "blend": blend, "state_parts": state_parts,
                          "state_rows": state_rows, "norm1": shift(AFTER1),
                          "f2_transpose": low_part(3, 1), "features": features, "edges": edges,
                          "edge_transpose": edge_transpose, "edge_mix": edge_mix, "elu": elu, "norm2": shift(AFTER2),
                          "f3_transpose": low_part(4, 1), "fold": fold, "relate": relate, "squares": squares,
                          "relation_mix": relation_mix, "norm3": shift(AFTER3)})


_INS = ['x', 'adj', 'L0_gnn_w_qkv', 'L0_gnn_w_proj', 'L0_gnn_b_proj', 'L0_gnn_ln_gamma', 'L0_gnn_ln_beta',
        'L1_gnn_w3_w', 'L1_gnn_w3_b', 'L1_gnn_u3_w', 'L1_gnn_u3_b', 'L1_gnn_w4_w', 'L1_gnn_w4_b', 'L1_gnn_w5_w',
        'L1_gnn_w5_b', 'L1_gnn_u5_w', 'L1_gnn_u5_b', 'L2_gnn_W', 'L2_gnn_a', 'L2_gnn_beta', 'L3_gnn_Wq', 'L3_gnn_Wk',
        'L3_gnn_Wv']
_OUTS = [((64, 128, 256), 'float32')]


def kernel(**inputs):
    import numpy as _np
    import concourse.bacc as _bacc
    from concourse import mybir as _mybir
    from concourse.bass_utils import run_bass_kernel_spmd as _run

    nc = _bacc.Bacc("TRN2", target_bir_lowering=False, num_devices=1)
    arrays, args = {}, []
    for name in _INS:
        a = _np.ascontiguousarray(inputs[name])
        arrays[f"in_{name}_dram"] = a
        args.append(nc.dram_tensor(f"in_{name}_dram", a.shape, _mybir.dt.from_np(a.dtype), kind="ExternalInput").ap())
    for i, (shape, dtype) in enumerate(_OUTS):
        dt = _mybir.dt.from_np(_np.dtype(dtype))
        args.append(nc.dram_tensor(f"out_{i}_dram", shape, dt, kind="ExternalOutput").ap())
    gnn_stack_kernel(nc, *args)
    r = _run(nc, [arrays], core_ids=[0])
    got = tuple(r.results[0][f"out_{i}_dram"] for i in range(len(_OUTS)))
    return got[0]
```

```python
from contextlib import ExitStack

import concourse.bass as bass
from concourse import mybir

F32 = mybir.dt.float32
F32R = mybir.dt.float32r
F16 = mybir.dt.float16
ALU = mybir.AluOpType
ACT = mybir.ActivationFunctionType
AX_X = mybir.AxisListType.X

P = 128
HEADS = 8
LN_EPS = 1e-5
ALPHA = 0.2
STEPS = 3
GR = 2
GROUPS = range(4)
FAR = -30000.0

W34, W4, W5, U3, U5, WM, WV = range(7)


TRIP = [
    ("x_transpose", 0, 40), ("queries", 0, 56), ("keys", 0, 29), ("values", 0, 131), ("scores", 0, 97),
    ("weights", 0, 70), ("mix", 0, 58), ("scores", 1, 41), ("weights", 1, 73), ("mix", 1, 89),
    ("o_transpose", 0, 124), ("project", 0, 112), ("inner_norm", 0, 26), ("rescale", 0, 24),
    ("add_norm", 0, 98), ("norm0", 0, 135), ("state_transpose", 0, 76), ("state_part", 0, 11),
    ("neighbours", 0, 58), ("reset_gate", 0, 42), ("value_sums", 0, 16), ("reset_parts", 0, 44),
    ("update_gate", 0, 9), ("new_value", 0, 54), ("blend", 0, 23), ("state_parts", 0, 97),
    ("state_rows", 0, 30), ("state_part", 1, 58), ("neighbours", 1, 67), ("reset_gate", 1, 33),
    ("value_sums", 1, 49), ("reset_parts", 1, 10), ("update_gate", 1, 58), ("new_value", 1, 80),
    ("blend", 1, 98), ("state_parts", 1, 41), ("state_rows", 1, 54), ("state_part", 2, 28),
    ("neighbours", 2, 54), ("reset_gate", 2, 27), ("value_sums", 2, 54), ("reset_parts", 2, 79),
    ("update_gate", 2, 47), ("new_value", 2, 31), ("blend", 2, 69), ("state_parts", 2, 76),
    ("state_rows", 2, 24), ("norm1", 0, 34), ("load_next", 0, 94), ("f2_transpose", 0, 29),
    ("features", 0, 57), ("edges", 0, 24), ("edge_exp", 0, 146), ("edge_transpose", 0, 80),
    ("edge_mix", 0, 79), ("elu", 0, 81), ("norm2", 0, 25), ("f3_transpose", 0, 48), ("fold", 0, 150),
    ("relate", 0, 62), ("squares", 0, 106), ("relation_mix", 0, 118), ("norm3", 0, 27)]
SHIFTS = (0.0, 1.0, 2.0, 3.0)


def window():
    whole = sum(w for _, _, w in TRIP)
    entries = []
    for g in GROUPS:
        at = SHIFTS[g] * whole / len(GROUPS)
        for name, n, w in TRIP:
            entries.append((at % whole, g, name, n, int(at >= whole)))
            at += w
    return [(name, n, g, behind) for _, g, name, n, behind in sorted(entries, key=lambda e: e[:2])]


def rises_of(events):
    return [name for name, n in events for _ in range(n)]


IN_BANK = rises_of(
    [("t_ps", 1), ("qkv_ps", 3)] + GR * [("tile_ps", 2), ("score_ps", 1), ("pT_ps", 2), ("pv_ps", 1)]
    + [("t_ps", 1), ("proj_ps", 1), ("t_ps", 1)]
    + STEPS * [("a_ps", 1), ("r_ps", 1), ("z_ps", 1), ("hv_ps", 1), ("hn_ps", 1)]
    + [("t_ps", 1), ("gat_ps", 1), ("s2_ps", 1), ("eT_ps", 1), ("gp_ps", 1)]
    + [("t_ps", 1), ("tq_ps", 1), ("rv_ps", 1), ("ss_ps", 1), ("ov_ps", 1)])
BY_SCALAR = rises_of(
    [("t_hi", 1), ("qkv_hid", 3)] + GR * [("prob_done", 1), ("pT_hid", 2)]
    + [("t_hi", 1), ("norm_done", 2), ("h16_split", 1), ("t_hi", 1), ("hT_done", 1)]
    + [e for t in range(STEPS) for e in (("a_hid", 1), ("r_done", 1), ("rh_hid", 1), ("z_done", 1), ("hv_done", 1),
                                         ("hs_hid", int(t < STEPS - 1)), ("h16_hid", int(t < STEPS - 1)))]
    + [("norm_done", 1), ("t_hi", 1), ("gb_done", 1), ("s12_done", 1), ("eexp_done", 1), ("eT_hid", 1),
       ("elu_exp", 1), ("norm_done", 1)]
    + [("t_hi", 1), ("tq_hid", 1), ("vv_hid", 1), ("sq_done", 1), ("rel_hid", 1), ("norm_done", 1)])
BY_VECTOR = rises_of(
    [("t_lo", 1), ("qkv_lod", 3)] + GR * [("max_step", 2), ("pT_lod", 2), ("o_step", 2)]
    + [("t_lo", 1), ("proj_done", 1), ("moment", 4)]
    + [e for t in range(STEPS) for e in (("a_lod", 1), ("rh_done", 1), ("rh_lod", 1), ("h_step", 2),
                                         ("h16_lod", int(t < STEPS - 1)))]
    + [("resid_done", 1), ("moment", 2)]
    + [("t_lo", 1), ("s1_done", 1), ("gl_done", 1), ("edge_step", 4), ("einv_done", 1), ("eT_lod", 1),
       ("gp_done", 1), ("clip_done", 1), ("elu_done", 1), ("resid_done", 1), ("moment", 2)]
    + [("t_lo", 1), ("tq_lod", 1), ("rel_done", 1), ("vv_lod", 1), ("ss_done", 1), ("resid_done", 1), ("moment", 2)])
BY_POOL = rises_of(
    [("xo_done", 1), ("xob_done", 1), ("eps_done", 1), ("rstd_done", 1), ("nmr_done", 1), ("scaled_done", 1),
     ("inner_done", 1), ("eps_done", 1), ("rstd_done", 1), ("nmr_done", 1), ("first_lod", 1), ("hT_lod", 1)]
    + [e for t in range(STEPS) for e in (("hd_done", 1), ("hs_lod", int(t < STEPS - 1)))]
    + 2 * [("eps_done", 1), ("rstd_done", 1), ("nmr_done", 1)] 
    + [("rel_lod", 1), ("rn_done", 1), ("eps_done", 1), ("rstd_done", 1), ("nmr_done", 1)])


class Rises:

    def __init__(self, ctx, nc, name, order):
        self.sems = [ctx.enter_context(nc.semaphore(f"{name}_{g}")) for g in GROUPS]
        self.order = order

    def head_start(self, g):
        return 2 * g * len(self.order)

    def kind(self, name):
        return Kind(self, name)


class Kind:

    def __init__(self, rises, name):
        self.rises = rises
        self.places = [n + 1 for n, other in enumerate(rises.order) if other == name]

    def __getitem__(self, g):
        return self.rises.sems[g]

    def at(self, g, trip, k):
        per_trip = len(self.rises.order)
        place = self.places[k - 1] if k else self.places[-1] - per_trip
        return trip * per_trip + (place + self.rises.head_start(g))


def gnn_stack_kernel(nc, x, adj, w_qkv, w_proj, b_proj, ln_gamma, ln_beta, w3_w, w3_b, u3_w, u3_b, w4_w, w4_b,
                     w5_w, w5_b, u5_w, u5_b, gat_w, gat_a, gat_beta, wq, wk, wv, out):
    B, N, D = x.shape
    HD = D // HEADS
    SCALE = float(HD) ** -0.5
    KC = D // P
    TRIPS = B // (GR * len(GROUPS))
    COLS = GR * N
    HW = HD + 1
    assert N == P and COLS == 256 and KC == 2 and B % (GR * len(GROUPS)) == 0

    with ExitStack() as ctx:
        def sb(name, shape, dt):
            return ctx.enter_context(nc.sbuf_tensor(name, shape, dt))

        def sem(name):
            return ctx.enter_context(nc.semaphore(name))

        def per_group(name, shape, dt):
            return [sb(f"{name}_{g}", shape, dt) for g in GROUPS]

        ps = ctx.enter_context(nc.psum_tensor("ps", [P, 8, 512], F32))

        def bank(g, b):
            return ps[:, 2 * g + b, :]

        def both_banks(g):
            return ps[:, 2 * g:2 * g + 2, :]

        def chunked(t):
            return t.rearrange("p (c n) -> p c n", c=KC)

        def flat(t):
            return t.rearrange("p a b -> p (a b)")

        ident = sb("ident", [P, P], F32)
        ident16 = sb("ident16", [P, P], F16)
        zeros = sb("zeros", [P, GR], F32)
        eps = sb("eps", [P, GR], F32)
        ones = sb("ones", [P, 2], F32)
        gate_cell = sb("gate_cell", [P, 1], F32)
        start_cell = sb("start_cell", [P, 6, len(GROUPS)], F32)
        neg_half = sb("neg_half", [P, GR], F32)
        adj_sb = sb("adj_sb", [P, N], F32)
        adjT16 = sb("adjT16", [P, N], F16)
        far_id = sb("far_id", [P, P], F16)
        far16 = sb("far16", [P, 4, N], F16)
        qkv_hi = sb("qkv_hi", [P, KC, 3 * D], F32R)
        qkv_lo = sb("qkv_lo", [P, KC, 3 * D], F32R)
        proj_hi = sb("proj_hi", [P, KC, D], F32R)
        proj_lo = sb("proj_lo", [P, KC, D], F32R)
        wt_hi = sb("wt_hi", [P, 6, KC, D], F32R)
        wt_lo = sb("wt_lo", [P, 6, KC, D], F32R)
        gat_hi = sb("gat_hi", [P, KC, D + 2], F32R)
        gat_lo = sb("gat_lo", [P, KC, D + 2], F32R)
        wa2_hi = sb("wa2_hi", [P, KC, P], F32R)
        wa2_lo = sb("wa2_lo", [P, KC, P], F32R)
        beta_col = sb("beta_col", [P, 1], F32)
        bproj_row = sb("bproj_row", [P, D], F32)
        gamma_row = sb("gamma_row", [P, D], F32)
        lnbeta_row = sb("lnbeta_row", [P, D], F32)
        bias_raw = sb("bias_raw", [P, 5, KC], F32)
        bias_sum = sb("bias_sum", [P, 3, KC], F32)
        bias_act = sb("bias_act", [P, 3, KC], F32)

        x_in = per_group("x_in", [P, GR, D], F32)
        fT_hi = per_group("fT_hi", [P, KC, COLS], F32R)
        fT_lo = per_group("fT_lo", [P, KC, COLS], F32R)
        q_hi = per_group("q_hi", [P, KC, COLS], F16)
        q_lo = per_group("q_lo", [P, KC, COLS], F16)
        v_hi = per_group("v_hi", [P, GR, HEADS, HW], F16)
        v_lo = per_group("v_lo", [P, GR, HEADS, HW], F16)
        row_max = per_group("row_max", [P, HEADS], F32)
        neg_max = per_group("neg_max", [P, HEADS], F32)
        inv_sum = per_group("inv_sum", [P, HEADS], F32)
        feat = per_group("feat", [P, GR, D], F32)
        resid = per_group("resid", [P, GR, D], F32)
        stats = per_group("stats", [P, GR, 6], F32)
        mean_var = per_group("mean_var", [P, GR, 2], F32)
        var_eps = per_group("var_eps", [P, GR], F32)
        neg_mean = per_group("neg_mean", [P, GR], F32)
        rstd = per_group("rstd", [P, GR], F32)
        neg_mr = per_group("neg_mr", [P, GR], F32)
        aT_hi = per_group("aT_hi", [P, KC, COLS], F32R)
        aT_lo = per_group("aT_lo", [P, KC, COLS], F32R)
        gates = per_group("gates", [P, 2, KC, COLS], F32)
        state = per_group("state", [P, 2, KC, COLS], F32)
        rh_hi = per_group("rh_hi", [P, KC, COLS], F32R)
        rh_lo = per_group("rh_lo", [P, KC, COLS], F32R)
        s1 = per_group("s1", [P, GR], F32)
        e_max = per_group("e_max", [P, GR], F32)
        e_sum = per_group("e_sum", [P, GR], F32)
        e_inv = per_group("e_inv", [P, GR], F32)
        sq_sum = per_group("sq_sum", [P, GR], F32)
        rel_norm = per_group("rel_norm", [P, GR], F32)
        mov_hi = per_group("mov_hi", [P, KC, 4, P], F32R)
        mov_lo = per_group("mov_lo", [P, KC, 4, P], F32R)

        tz, tr = ([t[:, n] for t in gates] for n in range(2))
        hT, rh = ([t[:, n] for t in state] for n in range(2))

        def as_rows(t):
            return t[:, :, :].rearrange("p a b -> p (a b)").rearrange("p (i d) -> p i d", d=D)

        def squares_of(t):
            return [t[:, n] for n in range(2)]

        def head_of(s):
            return 4 * (s % 2) + 2 * (s % 4 // 2) + s // 4

        def banked_relations(g):
            return both_banks(g).rearrange("p b n -> p (b n)").rearrange("p (q n) -> p q n", n=P)[:, 0:7:6, :]

        def banked_values(g):
            return both_banks(g).rearrange("p b n -> p (b n)")[:, P:P + 2 * 3 * P] \
                .rearrange("p (i d) -> p i d", d=3 * P)[:, :, 0:D]

        prob = [t[:, :, :, :].rearrange("p a b c -> p (a b c)").rearrange("p (s n) -> p s n", n=N) for t in gates]
        pT_hi, pT_lo = ([flat(t).bitcast(F16).rearrange("p (s m) -> p s m", m=N) for t in buf] for buf in (rh, hT))
        out_sb = [as_rows(t) for t in tz]
        temp = [as_rows(t) for t in hT]
        temp2 = [as_rows(t) for t in tr]
        k_hi_flat, k_lo_flat = ([t[:, n, :].bitcast(F16) for t in resid] for n in range(2))
        k_hi, k_lo = ([chunked(t) for t in part] for part in (k_hi_flat, k_lo_flat))
        h16_hi = [as_rows(t) for t in q_hi]
        h16_lo = [as_rows(t) for t in q_lo]
        g_hi = [as_rows(t) for t in aT_hi]
        g_lo = [as_rows(t) for t in aT_lo]
        edge = [t[:, 0, :].rearrange("p (i n) -> p i n", n=N) for t in rh]
        edge2 = [t[:, 1, :].rearrange("p (i n) -> p i n", n=N) for t in rh]
        eT_hi = [t[:, 0, :].rearrange("p (i n) -> p i n", n=N) for t in rh_hi]
        eT_lo = [t[:, 0, :].rearrange("p (i n) -> p i n", n=N) for t in rh_lo]
        pair_raw = [t[:, :, :, :].rearrange("p a b c -> p (a b c)").rearrange("p (c d) -> p c d", c=KC)
                    for t in gates[0:3]]
        square_raw = [m for t in state[1:4] for m in squares_of(t)]
        proj_raw = square_raw[5]
        summed = [feat[n][:, :, :] for n in range(4)]
        qkv_raw = [t[:, :, :, :].rearrange("p a b c -> p (a b c)")[:, 0:3 * D] for t in (gates[3], state[0])]
        wv_hi, wv_lo = aT_hi[0], aT_lo[0]
        a_row = resid[0][:, :, :].rearrange("p a b -> p (a b)")
        a_junk = resid[1][:, 0, :]
        gat_raw = [t[:, :, :].rearrange("p a b -> p (a b)")[:, 0:D + 2] for t in resid[2:4]]

        ld_squares = sem("ld_squares")
        ld_rows = sem("ld_rows")
        ident_made = sem("ident_made")
        prep_v = sem("prep_v")
        prep_pe = sem("prep_pe")
        prep_a = sem("prep_a")
        prep_done = sem("prep_done")

        in_bank = Rises(ctx, nc, "in_bank", IN_BANK)
        by_scalar = Rises(ctx, nc, "by_scalar", BY_SCALAR)
        by_vector = Rises(ctx, nc, "by_vector", BY_VECTOR)
        by_pool = Rises(ctx, nc, "by_pool", BY_POOL)
        x_loads = Rises(ctx, nc, "x_loads", ["x_loaded"] * 16)
        stores = Rises(ctx, nc, "stores", ["out_stored"] * 16)
        x_loaded = x_loads.kind("x_loaded")
        out_stored = stores.kind("out_stored")
        t_ps, t_hi, t_lo = in_bank.kind("t_ps"), by_scalar.kind("t_hi"), by_vector.kind("t_lo")
        qkv_ps, qkv_hid, qkv_lod = in_bank.kind("qkv_ps"), by_scalar.kind("qkv_hid"), by_vector.kind("qkv_lod")
        tile_ps = in_bank.kind("tile_ps")
        score_ps = in_bank.kind("score_ps")
        max_step = by_vector.kind("max_step")
        prob_done = by_scalar.kind("prob_done")
        pT_ps, pT_hid, pT_lod = in_bank.kind("pT_ps"), by_scalar.kind("pT_hid"), by_vector.kind("pT_lod")
        pv_ps = in_bank.kind("pv_ps")
        o_step = by_vector.kind("o_step")
        proj_ps, proj_done = in_bank.kind("proj_ps"), by_vector.kind("proj_done")
        xo_done = by_pool.kind("xo_done")
        xob_done = by_pool.kind("xob_done")
        scaled_done = by_pool.kind("scaled_done")
        resid_done = by_vector.kind("resid_done")
        moment = by_vector.kind("moment")
        rstd_done = by_pool.kind("rstd_done")
        eps_done = by_pool.kind("eps_done")
        nmr_done = by_pool.kind("nmr_done")
        norm_done = by_scalar.kind("norm_done")
        hT_done = by_scalar.kind("hT_done")
        inner_done = by_pool.kind("inner_done")
        h16_split, first_lod, hT_lod = by_scalar.kind("h16_split"), by_pool.kind("first_lod"), by_pool.kind("hT_lod")
        h16_hid, h16_lod = by_scalar.kind("h16_hid"), by_vector.kind("h16_lod")
        a_ps, a_hid, a_lod = in_bank.kind("a_ps"), by_scalar.kind("a_hid"), by_vector.kind("a_lod")
        r_ps, r_done = in_bank.kind("r_ps"), by_scalar.kind("r_done")
        z_ps, z_done = in_bank.kind("z_ps"), by_scalar.kind("z_done")
        rh_done, rh_hid, rh_lod = by_vector.kind("rh_done"), by_scalar.kind("rh_hid"), by_vector.kind("rh_lod")
        hv_ps, hv_done = in_bank.kind("hv_ps"), by_scalar.kind("hv_done")
        hd_done = by_pool.kind("hd_done")
        h_step = by_vector.kind("h_step")
        hs_hid, hs_lod = by_scalar.kind("hs_hid"), by_pool.kind("hs_lod")
        hn_ps = in_bank.kind("hn_ps")
        gat_ps, s1_done, gb_done, gl_done = (in_bank.kind("gat_ps"), by_vector.kind("s1_done"),
                                             by_scalar.kind("gb_done"), by_vector.kind("gl_done"))
        s2_ps, s12_done = in_bank.kind("s2_ps"), by_scalar.kind("s12_done")
        edge_step = by_vector.kind("edge_step")
        eexp_done, einv_done = by_scalar.kind("eexp_done"), by_vector.kind("einv_done")
        eT_ps, eT_hid, eT_lod = in_bank.kind("eT_ps"), by_scalar.kind("eT_hid"), by_vector.kind("eT_lod")
        gp_ps, gp_done = in_bank.kind("gp_ps"), by_vector.kind("gp_done")
        clip_done, elu_exp, elu_done = (by_vector.kind("clip_done"), by_scalar.kind("elu_exp"),
                                        by_vector.kind("elu_done"))
        tq_ps, tq_hid, tq_lod = in_bank.kind("tq_ps"), by_scalar.kind("tq_hid"), by_vector.kind("tq_lod")
        rv_ps = in_bank.kind("rv_ps")
        vv_hid, vv_lod = by_scalar.kind("vv_hid"), by_vector.kind("vv_lod")
        rel_done, sq_done = by_vector.kind("rel_done"), by_scalar.kind("sq_done")
        rel_hid, rel_lod = by_scalar.kind("rel_hid"), by_pool.kind("rel_lod")
        ss_ps, ss_done, rn_done = in_bank.kind("ss_ps"), by_vector.kind("ss_done"), by_pool.kind("rn_done")
        ov_ps = in_bank.kind("ov_ps")

        INNER, AFTER0, AFTER1, AFTER2, AFTER3 = range(5)

        x_rows = x.rearrange("b n d -> n b d")
        out_rows = out.rearrange("b n d -> n b d")

        def row_of(v):
            return v.rearrange("(a d) -> a d", a=1)

        ORDER = window()

        def issue(steps, trip, order, before=True, after=True):
            for name, n, g, behind in order:
                if name in steps and (before if behind else after):
                    steps[name](g, trip - behind, n)

        def first(trip):
            return isinstance(trip, int) and trip == 0

        def program(eng, steps, peel_last=False):
            issue(steps, 0, ORDER, before=False)
            with eng.Fori(1, TRIPS - peel_last) as trip:
                issue(steps, trip, ORDER)
            if peel_last:
                issue(steps, TRIPS - 1, ORDER)
            issue(steps, TRIPS, ORDER, after=False)

        def adj_rows(n):
            return adj_sb[:, :].unsqueeze(1).to_broadcast([P, n, N])

        WEIGHTS = (W34, W4, W5, U3, U5, WV, WM)

        def parts_of(n):
            return (wv_hi[:, :, :], wv_lo[:, :, :]) if n == WV else (wt_hi[:, n], wt_lo[:, n])

        square_loads = [
            (pair_raw[0], w3_w.rearrange("(c p) i -> p c i", p=P)),
            (pair_raw[1], w4_w.rearrange("(c p) i -> p c i", p=P)),
            (pair_raw[2], w5_w.rearrange("(c p) i -> p c i", p=P)),
            (square_raw[1], u5_w.rearrange("(c p) i -> p c i", p=P)),
            (square_raw[0], u3_w.rearrange("(c p) i -> p c i", p=P)),
            (square_raw[2], wv.rearrange("(c p) i -> p c i", p=P)),
            (square_raw[3], wq.rearrange("(c p) i -> p c i", p=P)),
            (square_raw[4], wk.rearrange("(c p) i -> p c i", p=P)),
            (adj_sb[:, :], adj),
        ]
        row_loads = [
            (gat_raw[0][:, 0:D], gat_w[0:P, :]),
            (gat_raw[1][:, 0:D], gat_w[P:2 * P, :]),
            (a_row, gat_a.rearrange("k a -> a k").to_broadcast([P, 2 * D])),
            (qkv_raw[0], w_qkv[0:P, :]),
            (qkv_raw[1], w_qkv[P:2 * P, :]),
            (proj_raw, w_proj.rearrange("(c p) o -> p c o", p=P)),
            (beta_col[:, :], row_of(gat_beta).to_broadcast([P, 1])),
            (bproj_row[:, :], row_of(b_proj).to_broadcast([P, D])),
            (gamma_row[:, :], row_of(ln_gamma).to_broadcast([P, D])),
            (lnbeta_row[:, :], row_of(ln_beta).to_broadcast([P, D])),
        ] + [
            (bias_raw[:, n, c:c + 1], v[c * P:(c + 1) * P].rearrange("(p a) -> p a", a=1))
            for n, v in enumerate((w3_b, w4_b, w5_b, u3_b, u5_b)) for c in range(KC)
        ]

        block = ctx.enter_context(nc.Block())

        @block.sync
        def _(sp):
            def load(g, trip):
                sp.dma_start(x_in[g][:, :, :], x_rows[:, bass.ds(trip * (len(GROUPS) * GR) + g * GR, GR), :]) \
                    .then_inc(x_loaded[g], 16)

            def load_next(g, trip, _n):
                if isinstance(trip, int) and trip == TRIPS - 1:
                    return
                sp.wait_ge(xo_done[g], xo_done.at(g, trip, 1))
                load(g, trip + 1)

            def norm3(g, trip, _n):
                sp.wait_ge(norm_done[g], norm_done.at(g, trip, AFTER3 + 1))
                sp.dma_start(out_rows[:, bass.ds(trip * (len(GROUPS) * GR) + g * GR, GR), :], out_sb[g]) \
                    .then_inc(out_stored[g], 16)

            for dst, src in square_loads:
                sp.dma_start(dst, src).then_inc(ld_squares, 16)
            for dst, src in row_loads:
                sp.dma_start(dst, src).then_inc(ld_rows, 16)
            for g in sorted(GROUPS, key=lambda g: SHIFTS[g]):
                load(g, 0)
            program(sp, {"load_next": load_next, "norm3": norm3}, peel_last=True)
            for g in GROUPS:
                sp.wait_ge(out_stored[g], out_stored.at(g, TRIPS, 0))

        @block.gpsimd
        def _(pool):
            nc.gpsimd.memset(ident[:, :], 0.0).then_inc(ident_made, 1)
            pool.wait_ge(ident_made, 1)
            nc.gpsimd.affine_select(out=ident[:, :], in_=ident[:, :], compare_op=ALU.not_equal, fill=1.0, base=0,
                                    pattern=[[-1, P]], channel_multiplier=1).then_inc(ident_made, 1)
            nc.gpsimd.memset(neg_half[:, :], -0.5).then_inc(ident_made, 1)
            nc.gpsimd.memset(ones[:, :], 1.0).then_inc(ident_made, 1)
            nc.gpsimd.memset(zeros[:, :], 0.0).then_inc(ident_made, 1)
            nc.gpsimd.memset(eps[:, :], LN_EPS).then_inc(ident_made, 1)
            for g in GROUPS:
                nc.gpsimd.memset(v_hi[g][:, :, :, HD:HW], 1.0).then_inc(ident_made, 1)
                nc.gpsimd.memset(v_lo[g][:, :, :, HD:HW], 0.0).then_inc(ident_made, 1)
            for n, rises in enumerate((in_bank, by_scalar, by_vector, by_pool, x_loads, stores)):
                for g in GROUPS[1:]:
                    nc.gpsimd.memset(start_cell[:, n, g:g + 1], 0.0).then_inc(rises.sems[g], rises.head_start(g))

            pool.wait_ge(ident_made, 6 + 2 * len(GROUPS))

            def project(g, trip, _n):
                pool.wait_ge(proj_done[g], proj_done.at(g, trip, 1))
                nc.gpsimd.tensor_tensor(temp2[g], x_in[g][:, :, :], resid[g][:, :, :], ALU.add) \
                    .then_inc(xo_done[g], 1)
                pool.wait_ge(xo_done[g], xo_done.at(g, trip, 1))
                nc.gpsimd.tensor_tensor(temp2[g], temp2[g],
                                        lnbeta_row[:, :].unsqueeze(1).to_broadcast([P, GR, D]), ALU.add) \
                    .then_inc(xob_done[g], 1)

            def rescale(g, trip, _n):
                pool.wait_ge(norm_done[g], norm_done.at(g, trip, INNER + 1))
                nc.gpsimd.tensor_tensor(temp[g], temp[g], gamma_row[:, :].unsqueeze(1).to_broadcast([P, GR, D]),
                                        ALU.mult).then_inc(scaled_done[g], 1)
                pool.wait_ge(scaled_done[g], scaled_done.at(g, trip, 1))
                nc.gpsimd.tensor_tensor(resid[g][:, :, :], temp[g], temp2[g], ALU.add).then_inc(inner_done[g], 1)

            def state_transpose(g, trip, _n):
                pool.wait_ge(h16_split[g], h16_split.at(g, trip, 1))
                nc.gpsimd.tensor_tensor(h16_lo[g], feat[g][:, :, :], h16_hi[g], ALU.subtract).then_inc(first_lod[g], 1)
                pool.wait_ge(hT_done[g], hT_done.at(g, trip, 1))
                nc.gpsimd.tensor_tensor(fT_lo[g][:, :, :], hT[g], fT_hi[g][:, :, :].bitcast(F32), ALU.subtract) \
                    .then_inc(hT_lod[g], 1)

            def state_parts(g, trip, t):
                if t < STEPS - 1:
                    pool.wait_ge(hs_hid[g], hs_hid.at(g, trip, t + 1))
                    nc.gpsimd.tensor_tensor(fT_lo[g][:, :, :], hT[g], fT_hi[g][:, :, :].bitcast(F32), ALU.subtract) \
                        .then_inc(hs_lod[g], 1)

            def new_value(g, trip, t):
                pool.wait_ge(hv_done[g], hv_done.at(g, trip, t + 1))
                nc.gpsimd.tensor_tensor(flat(tr[g]), flat(rh[g]), flat(hT[g]), ALU.subtract).then_inc(hd_done[g], 1)

            def rsqrt_of(n):
                def step(g, trip, _n):
                    pool.wait_ge(moment[g], moment.at(g, trip, 2 * n + 2))
                    nc.gpsimd.tensor_tensor(neg_mean[g][:, :], zeros[:, :], mean_var[g][:, :, 0], ALU.subtract)
                    nc.gpsimd.tensor_tensor(var_eps[g][:, :], mean_var[g][:, :, 1], eps[:, :], ALU.add) \
                        .then_inc(eps_done[g], 1)
                    pool.wait_ge(eps_done[g], eps_done.at(g, trip, n + 1))
                    nc.gpsimd.tensor_tensor(rstd[g][:, :], var_eps[g][:, :], neg_half[:, :], ALU.pow) \
                        .then_inc(rstd_done[g], 1)
                    pool.wait_ge(rstd_done[g], rstd_done.at(g, trip, n + 1))
                    nc.gpsimd.tensor_tensor(neg_mr[g][:, :], neg_mean[g][:, :], rstd[g][:, :], ALU.mult) \
                        .then_inc(nmr_done[g], 1)
                return step

            def squares(g, trip, _n):
                pool.wait_ge(rel_hid[g], rel_hid.at(g, trip, 1))
                nc.gpsimd.tensor_tensor(eT_lo[g], edge[g], eT_hi[g].bitcast(F32), ALU.subtract).then_inc(rel_lod[g], 1)
                pool.wait_ge(ss_done[g], ss_done.at(g, trip, 1))
                nc.gpsimd.tensor_tensor(rel_norm[g][:, :], sq_sum[g][:, :], neg_half[:, :], ALU.pow) \
                    .then_inc(rn_done[g], 1)

            program(pool, {"project": project, "inner_norm": rsqrt_of(INNER), "rescale": rescale,
                           "norm0": rsqrt_of(AFTER0), "state_transpose": state_transpose, "new_value": new_value,
                           "state_parts": state_parts, "norm1": rsqrt_of(AFTER1), "norm2": rsqrt_of(AFTER2), "squares": squares,
                           "norm3": rsqrt_of(AFTER3)})

        @block.tensor
        def _(pe):
            def split_mm(dst, w_hi, w_lo, m_hi, m_lo, start=True, stop=True, shared=False):
                n = 0
                for c in range(KC):
                    for a, b in ((w_hi, m_hi), (w_hi, m_lo), (w_lo, m_hi)):
                        last = nc.tensor.matmul(dst, a(c), b(c), start=start and n == 0,
                                                stop=stop and n == 3 * KC - 1,
                                                skip_group_check=shared or not (start and stop))
                        n += 1
                return last

            def transposed(g, b, src):
                for c in range(KC):
                    for i in range(GR):
                        last = nc.tensor.transpose(chunked(bank(g, b))[:, c, i * P:(i + 1) * P],
                                                   src[:, i, c * P:(c + 1) * P], ident[:, :])
                last.then_inc(t_ps[g], 1)

            def maps(g, b, w_hi, w_lo, f_hi, f_lo, start=True, stop=True):
                for c in range(KC):
                    last = split_mm(chunked(bank(g, b))[:, c, :], lambda k: w_hi(k, c), lambda k: w_lo(k, c),
                                    lambda k: f_hi[:, k, :], lambda k: f_lo[:, k, :], start and c == 0, stop, True)
                return last

            def qkv_map(g, b, first_col):
                return maps(g, b, lambda k, c: qkv_hi[:, k, first_col + c * P:first_col + (c + 1) * P],
                            lambda k, c: qkv_lo[:, k, first_col + c * P:first_col + (c + 1) * P], fT_hi[g], fT_lo[g])

            def gate(g, b, w, f_hi, f_lo, start, stop):
                return maps(g, b, lambda k, c: wt_hi[:, w, k, c * P:(c + 1) * P],
                            lambda k, c: wt_lo[:, w, k, c * P:(c + 1) * P], f_hi[g], f_lo[g], start, stop)

            def rows_times(g, i, dst, w_hi, w_lo, start=True):
                return split_mm(dst, lambda k: fT_hi[g][:, k, i * P:(i + 1) * P],
                                lambda k: fT_lo[g][:, k, i * P:(i + 1) * P], w_hi, w_lo, start, True, True)

            def x_transpose(g, trip, _n):
                pe.wait_ge(x_loaded[g], x_loaded.at(g, trip, 16))
                if not first(trip):
                    pe.wait_ge(resid_done[g], resid_done.at(g, trip, 0))
                transposed(g, 0, x_in[g])

            def queries(g, trip, _n):
                pe.wait_ge(t_lo[g], t_lo.at(g, trip, 1))
                qkv_map(g, 1, 0).then_inc(qkv_ps[g], 1)

            def keys(g, trip, _n):
                qkv_map(g, 0, D).then_inc(qkv_ps[g], 1)

            def values(g, trip, _n):
                pe.wait_ge(qkv_lod[g], qkv_lod.at(g, trip, 1))
                for i in range(GR):
                    last = rows_times(g, i, bank(g, 1)[:, i * D:(i + 1) * D], lambda k: qkv_hi[:, k, 2 * D:3 * D],
                                      lambda k: qkv_lo[:, k, 2 * D:3 * D], i == 0)
                last.then_inc(qkv_ps[g], 1)

            def scores(g, trip, i):
                at = slice(i * N, (i + 1) * N)
                if i == 0:
                    pe.wait_ge(qkv_lod[g], qkv_lod.at(g, trip, 3))
                else:
                    pe.wait_ge(o_step[g], o_step.at(g, trip, 2 * i))
                for b in range(2):
                    nc.tensor.matmul(bank(g, b), far_id[:, :], far16[:, :, :], start=True, stop=False,
                                     skip_group_check=True)
                for j in range(4):
                    rows = slice(HD * j, HD * (j + 1))
                    if j >= 2:
                        pe.wait_ge(tile_ps[g], tile_ps.at(g, trip, 2 * i + j - 1))
                    for c in range(KC):
                        q = 2 * (j // 2) + c
                        for n, (a, b) in enumerate(((q_hi, k_hi), (q_hi, k_lo), (q_lo, k_hi))):
                            last = nc.tensor.matmul(bank(g, j % 2)[:, q * N:(q + 1) * N], a[g][rows, c, at],
                                                    b[g][rows, c, at], start=False, stop=(n == 2),
                                                    skip_group_check=True)
                    if j < 2:
                        last.then_inc(tile_ps[g], 1)
                last.then_inc(score_ps[g], 1)


            def weights(g, trip, i):
                pe.wait_ge(prob_done[g], prob_done.at(g, trip, i + 1))
                for b in range(2):
                    for s in range(4):
                        last = nc.tensor.transpose(bank(g, b)[:, s * N:(s + 1) * N],
                                                   prob[g][:, 4 * b + s, :], ident[:, :])
                    last.then_inc(pT_ps[g], 1)

            def mix(g, trip, i):
                for s in range(HEADS):
                    if s % 4 == 0:
                        pe.wait_ge(pT_lod[g], pT_lod.at(g, trip, 2 * i + s // 4 + 1))
                    h = head_of(s)
                    dst = bank(g, 0)[:, h * HW:(h + 1) * HW]
                    for n, (a, b) in enumerate(((pT_hi, v_hi), (pT_hi, v_lo), (pT_lo, v_hi))):
                        last = nc.tensor.matmul(dst, a[g][:, s, :], b[g][:, i, h, :], start=(n == 0), stop=(n == 2))
                last.then_inc(pv_ps[g], 1)

            def o_transpose(g, trip, _n):
                pe.wait_ge(o_step[g], o_step.at(g, trip, 2 * GR))
                transposed(g, 1, feat[g])

            def project(g, trip, _n):
                pe.wait_ge(t_lo[g], t_lo.at(g, trip, 2))
                for i in range(GR):
                    last = rows_times(g, i, bank(g, 0)[:, i * D:(i + 1) * D], lambda k: proj_hi[:, k, :],
                                      lambda k: proj_lo[:, k, :], i == 0)
                last.then_inc(proj_ps[g], 1)

            def state_transpose(g, trip, _n):
                pe.wait_ge(norm_done[g], norm_done.at(g, trip, AFTER0 + 1))
                transposed(g, 1, feat[g])

            def state_part(g, trip, t):
                if t == 0:
                    pe.wait_ge(hT_lod[g], hT_lod.at(g, trip, 1))
                else:
                    pe.wait_ge(z_done[g], z_done.at(g, trip, t))
                    pe.wait_ge(hs_lod[g], hs_lod.at(g, trip, t))
                gate(g, 0, U3, fT_hi, fT_lo, True, False)

            def neighbours(g, trip, t):
                if t == 0:
                    pe.wait_ge(hT_done[g], hT_done.at(g, trip, 1))
                else:
                    pe.wait_ge(h16_lod[g], h16_lod.at(g, trip, t))
                for c in range(KC):
                    for i in range(GR):
                        for n, a in enumerate((h16_hi, h16_lo)):
                            last = nc.tensor.matmul(chunked(bank(g, 1))[:, c, i * N:(i + 1) * N],
                                                    a[g][:, i, c * P:(c + 1) * P], adjT16[:, :],
                                                    start=(n == 0), stop=(n == 1))
                last.then_inc(a_ps[g], 1)

            def reset_gate(g, trip, t):
                pe.wait_ge(a_lod[g], a_lod.at(g, trip, t + 1))
                gate(g, 0, W4, aT_hi, aT_lo, False, True).then_inc(r_ps[g], 1)

            def value_sums(g, trip, t):
                gate(g, 1, W5, aT_hi, aT_lo, True, False)

            def update_gate(g, trip, t):
                pe.wait_ge(r_done[g], r_done.at(g, trip, t + 1))
                gate(g, 0, W34, aT_hi, aT_lo, False, True).then_inc(z_ps[g], 1)

            def new_value(g, trip, t):
                pe.wait_ge(rh_lod[g], rh_lod.at(g, trip, t + 1))
                gate(g, 1, U5, rh_hi, rh_lo, False, True).then_inc(hv_ps[g], 1)

            def state_rows(g, trip, t):
                pe.wait_ge(h_step[g], h_step.at(g, trip, 2 * t + 2))
                for i in range(GR):
                    for c in range(KC):
                        last = nc.tensor.transpose(bank(g, 1)[:, i * D + c * P:i * D + (c + 1) * P],
                                                   hT[g][:, c, i * N:(i + 1) * N], ident[:, :])
                last.then_inc(hn_ps[g], 1)

            def f2_transpose(g, trip, _n):
                pe.wait_ge(norm_done[g], norm_done.at(g, trip, AFTER1 + 1))
                transposed(g, 1, feat[g])

            def features(g, trip, _n):
                pe.wait_ge(t_lo[g], t_lo.at(g, trip, 3))
                for i in range(GR):
                    last = rows_times(g, i, bank(g, i)[:, 0:D + 2], lambda k: gat_hi[:, k, :],
                                      lambda k: gat_lo[:, k, :])
                last.then_inc(gat_ps[g], 1)

            def edges(g, trip, _n):
                pe.wait_ge(gl_done[g], gl_done.at(g, trip, 1))
                split_mm(bank(g, 0)[:, 0:COLS], lambda k: wa2_hi[:, k, :], lambda k: wa2_lo[:, k, :],
                         lambda k: fT_hi[g][:, k, :], lambda k: fT_lo[g][:, k, :]).then_inc(s2_ps[g], 1)

            def edge_transpose(g, trip, _n):
                pe.wait_ge(eexp_done[g], eexp_done.at(g, trip, 1))
                for i in range(GR):
                    last = nc.tensor.transpose(bank(g, 1)[:, i * N:(i + 1) * N], edge2[g][:, i, :], ident[:, :])
                last.then_inc(eT_ps[g], 1)

            def mixed_rows(g, b, done):
                for i in range(GR):
                    for n, (a, m) in enumerate(((eT_hi, g_hi), (eT_hi, g_lo), (eT_lo, g_hi))):
                        last = nc.tensor.matmul(bank(g, b)[:, i * D:(i + 1) * D], a[g][:, i, :],
                                                m[g][:, i, :], start=(n == 0), stop=(n == 2))
                last.then_inc(done[g], 1)

            def edge_mix(g, trip, _n):
                pe.wait_ge(eT_lod[g], eT_lod.at(g, trip, 1))
                mixed_rows(g, 0, gp_ps)

            def f3_transpose(g, trip, _n):
                pe.wait_ge(norm_done[g], norm_done.at(g, trip, AFTER2 + 1))
                transposed(g, 1, feat[g])

            def fold(g, trip, _n):
                pe.wait_ge(t_lo[g], t_lo.at(g, trip, 4))
                gate(g, 0, WM, fT_hi, fT_lo, True, True).then_inc(tq_ps[g], 1)

            def relate(g, trip, _n):
                pe.wait_ge(tq_lod[g], tq_lod.at(g, trip, 1))
                for i in range(GR):
                    last = rows_times(g, i, bank(g, i)[:, 0:3 * P], lambda k: mov_hi[g][:, k, i:i + 3, :],
                                      lambda k: mov_lo[g][:, k, i:i + 3, :])
                last.then_inc(rv_ps[g], 1)

            def squares(g, trip, _n):
                pe.wait_ge(sq_done[g], sq_done.at(g, trip, 1))
                pe.wait_ge(vv_lod[g], vv_lod.at(g, trip, 1))
                for i in range(GR):
                    last = nc.tensor.matmul(bank(g, 0)[:, 2 * i:2 * i + 2], edge2[g][:, i, :], ones[:, :],
                                            start=True, stop=True)
                last.then_inc(ss_ps[g], 1)

            def relation_mix(g, trip, _n):
                pe.wait_ge(rel_lod[g], rel_lod.at(g, trip, 1))
                mixed_rows(g, 1, ov_ps)

            pe.wait_ge(ident_made, 6 + 2 * len(GROUPS))
            pe.wait_ge(prep_v, 5)
            srcs = [summed[0], summed[1], summed[2], square_raw[0], summed[3], square_raw[2]]
            for n, src in zip(WEIGHTS, srcs):
                for oc in range(KC):
                    for dc in range(KC):
                        nc.tensor.transpose(ps[:, n, dc * D + oc * P:dc * D + (oc + 1) * P],
                                            src[:, oc, dc * P:(dc + 1) * P], ident[:, :]).then_inc(prep_pe, 1)
            for dc in range(KC):
                for c in range(KC):
                    nc.tensor.matmul(ps[:, WM, dc * D:(dc + 1) * D], square_raw[3][:, c, dc * P:(dc + 1) * P],
                                     square_raw[4][:, c, :], start=(c == 0), stop=(c == KC - 1)).then_inc(prep_pe, 1)
            nc.tensor.transpose(ps[:, 7, 0:P], adj_sb[:, :], ident[:, :]).then_inc(prep_pe, 1)
            pe.wait_ge(prep_done, 1)

            program(pe, {"x_transpose": x_transpose, "queries": queries, "keys": keys, "values": values,
                         "scores": scores, "weights": weights, "mix": mix, "o_transpose": o_transpose,
                         "project": project, "state_transpose": state_transpose, "state_part": state_part,
                         "neighbours": neighbours, "reset_gate": reset_gate, "value_sums": value_sums,
                         "update_gate": update_gate, "new_value": new_value, "state_rows": state_rows,
                         "f2_transpose": f2_transpose, "features": features, "edges": edges,
                         "edge_transpose": edge_transpose, "edge_mix": edge_mix, "f3_transpose": f3_transpose,
                         "fold": fold, "relate": relate, "squares": squares, "relation_mix": relation_mix})

        @block.scalar
        def _(act):
            def whole(t):
                return t[:, :, :].rearrange("p a b -> p (a b)")

            def high_part(s, b):
                def step(g, trip, _n):
                    act.wait_ge(t_ps[g], t_ps.at(g, trip, s + 1))
                    nc.scalar.activation(whole(fT_hi[g]), bank(g, b), ACT.Copy).then_inc(t_hi[g], 1)
                return step

            def normalised(n, dst):
                def step(g, trip, _n):
                    act.wait_ge(nmr_done[g], nmr_done.at(g, trip, n + 1))
                    for i in range(GR):
                        last = nc.scalar.activation(dst[g][:, i, :], resid[g][:, i, :], ACT.Identity,
                                                    scale=rstd[g][:, i:i + 1], bias=neg_mr[g][:, i:i + 1])
                    last.then_inc(norm_done[g], 1)
                return step

            def queries(g, trip, _n):
                act.wait_ge(qkv_ps[g], qkv_ps.at(g, trip, 1))
                nc.scalar.activation(whole(q_hi[g]), bank(g, 1), ACT.Copy).then_inc(qkv_hid[g], 1)

            def keys(g, trip, _n):
                act.wait_ge(qkv_ps[g], qkv_ps.at(g, trip, 2))
                nc.scalar.activation(k_hi_flat[g], bank(g, 0), ACT.Copy).then_inc(qkv_hid[g], 1)

            def values(g, trip, _n):
                act.wait_ge(qkv_ps[g], qkv_ps.at(g, trip, 3))
                nc.scalar.activation(v_hi[g][:, :, :, 0:HD], bank(g, 1).rearrange("p (i h d) -> p i h d", i=GR, h=HEADS),
                                     ACT.Copy).then_inc(qkv_hid[g], 1)

            def scores(g, trip, i):
                act.wait_ge(max_step[g], max_step.at(g, trip, 2 * i + 2))
                if i == 0 and not first(trip):
                    act.wait_ge(out_stored[g], out_stored.at(g, trip, 0))
                for s in range(HEADS):
                    last = nc.scalar.activation(prob[g][:, s, :],
                                                bank(g, s // 4)[:, (s % 4) * N:(s % 4 + 1) * N], ACT.Exp,
                                                bias=neg_max[g][:, s:s + 1], scale=SCALE)
                last.then_inc(prob_done[g], 1)

            def weights(g, trip, i):
                for b in range(2):
                    act.wait_ge(pT_ps[g], pT_ps.at(g, trip, 2 * i + b + 1))
                    nc.scalar.activation(pT_hi[g][:, 4 * b:4 * b + 4, :], bank(g, b), ACT.Copy) \
                        .then_inc(pT_hid[g], 1)

            def state_transpose(g, trip, _n):
                act.wait_ge(norm_done[g], norm_done.at(g, trip, AFTER0 + 1))
                nc.scalar.activation(h16_hi[g], feat[g][:, :, :], ACT.Copy).then_inc(h16_split[g], 1)
                act.wait_ge(t_ps[g], t_ps.at(g, trip, 3))
                nc.scalar.activation(whole(fT_hi[g]), bank(g, 1), ACT.Copy).then_inc(t_hi[g], 1)
                nc.scalar.activation(flat(hT[g]), bank(g, 1), ACT.Copy).then_inc(hT_done[g], 1)

            def neighbours(g, trip, t):
                act.wait_ge(a_ps[g], a_ps.at(g, trip, t + 1))
                nc.scalar.activation(whole(aT_hi[g]), bank(g, 1), ACT.Copy).then_inc(a_hid[g], 1)

            def reset_gate(g, trip, t):
                act.wait_ge(r_ps[g], r_ps.at(g, trip, t + 1))
                for c in range(KC):
                    last = nc.scalar.activation(tr[g][:, c, :], chunked(bank(g, 0))[:, c, :], ACT.Tanh,
                                                bias=bias_act[:, 1, c:c + 1], scale=0.5)
                last.then_inc(r_done[g], 1)

            def reset_parts(g, trip, t):
                act.wait_ge(rh_done[g], rh_done.at(g, trip, t + 1))
                nc.scalar.activation(whole(rh_hi[g]), flat(rh[g]), ACT.Copy).then_inc(rh_hid[g], 1)

            def update_gate(g, trip, t):
                act.wait_ge(z_ps[g], z_ps.at(g, trip, t + 1))
                for c in range(KC):
                    last = nc.scalar.activation(tz[g][:, c, :], chunked(bank(g, 0))[:, c, :], ACT.Tanh,
                                                bias=bias_act[:, 0, c:c + 1], scale=0.5)
                last.then_inc(z_done[g], 1)

            def new_value(g, trip, t):
                act.wait_ge(hv_ps[g], hv_ps.at(g, trip, t + 1))
                for c in range(KC):
                    last = nc.scalar.activation(rh[g][:, c, :], chunked(bank(g, 1))[:, c, :], ACT.Tanh,
                                                bias=bias_act[:, 2, c:c + 1], scale=1.0)
                last.then_inc(hv_done[g], 1)

            def state_parts(g, trip, t):
                if t < STEPS - 1:
                    act.wait_ge(h_step[g], h_step.at(g, trip, 2 * t + 2))
                    nc.scalar.activation(whole(fT_hi[g]), flat(hT[g]), ACT.Copy).then_inc(hs_hid[g], 1)

            def state_rows(g, trip, t):
                if t < STEPS - 1:
                    act.wait_ge(hn_ps[g], hn_ps.at(g, trip, t + 1))
                    nc.scalar.activation(flat(h16_hi[g]), bank(g, 1), ACT.Copy).then_inc(h16_hid[g], 1)

            def features(g, trip, _n):
                act.wait_ge(gat_ps[g], gat_ps.at(g, trip, 1))
                nc.scalar.activation(g_hi[g], both_banks(g)[:, :, 0:D], ACT.Copy)
                nc.scalar.activation(temp[g], both_banks(g)[:, :, 0:D], ACT.Copy,
                                     scale=beta_col[:, 0:1]).then_inc(gb_done[g], 1)

            def edges(g, trip, _n):
                act.wait_ge(s1_done[g], s1_done.at(g, trip, 1))
                act.wait_ge(s2_ps[g], s2_ps.at(g, trip, 1))
                for i in range(GR):
                    last = nc.scalar.activation(edge[g][:, i, :], bank(g, 0)[:, i * N:(i + 1) * N],
                                                ACT.Identity, bias=s1[g][:, i:i + 1], scale=1.0)
                last.then_inc(s12_done[g], 1)

            def edge_exp(g, trip, _n):
                act.wait_ge(edge_step[g], edge_step.at(g, trip, 4))
                for i in range(GR):
                    last = nc.scalar.activation(edge2[g][:, i, :], edge2[g][:, i, :], ACT.Exp,
                                                bias=e_max[g][:, i:i + 1], scale=1.0, accum_out=e_sum[g][:, i:i + 1])
                last.then_inc(eexp_done[g], 1)

            def edge_transpose(g, trip, _n):
                act.wait_ge(eT_ps[g], eT_ps.at(g, trip, 1))
                nc.scalar.activation(eT_hi[g], bank(g, 1)[:, 0:COLS].rearrange("p (i n) -> p i n", i=GR), ACT.Copy) \
                    .then_inc(eT_hid[g], 1)

            def elu(g, trip, _n):
                act.wait_ge(clip_done[g], clip_done.at(g, trip, 1))
                nc.scalar.activation(temp2[g], temp2[g], ACT.Exp).then_inc(elu_exp[g], 1)

            def fold(g, trip, _n):
                act.wait_ge(tq_ps[g], tq_ps.at(g, trip, 1))
                nc.scalar.activation(mov_hi[g][:, :, 0:4:3, :],
                                     bank(g, 0).rearrange("p (c q n) -> p c q n", c=KC, q=GR), ACT.Copy) \
                    .then_inc(tq_hid[g], 1)

            def relate(g, trip, _n):
                act.wait_ge(rv_ps[g], rv_ps.at(g, trip, 1))
                nc.scalar.activation(g_hi[g], banked_values(g), ACT.Copy).then_inc(vv_hid[g], 1)

            def squares(g, trip, _n):
                act.wait_ge(rel_done[g], rel_done.at(g, trip, 1))
                nc.scalar.activation(edge2[g], edge[g], ACT.Square).then_inc(sq_done[g], 1)
                nc.scalar.activation(eT_hi[g], edge[g], ACT.Copy).then_inc(rel_hid[g], 1)

            act.wait_ge(ld_rows, 16 * len(row_loads))
            for c in range(KC):
                nc.scalar.activation(qkv_hi[:, c, :], qkv_raw[c], ACT.Copy).then_inc(prep_a, 1)
            nc.scalar.activation(proj_hi[:, :, :], proj_raw, ACT.Copy).then_inc(prep_a, 1)
            act.wait_ge(prep_v, 9)
            for c in range(KC):
                nc.scalar.activation(gat_hi[:, c, :], gat_raw[c], ACT.Copy).then_inc(prep_a, 1)
            act.wait_ge(prep_pe, 29)
            for n in WEIGHTS:
                nc.scalar.activation(parts_of(n)[0], ps[:, n, :].rearrange("p (c o) -> p c o", c=KC), ACT.Copy) \
                    .then_inc(prep_a, 1)
            act.wait_ge(prep_a, 12)
            for g in GROUPS:
                for c in range(KC):
                    nc.scalar.activation(mov_hi[g][:, c, 1:3, :].rearrange("p q n -> p (q n)"),
                                         wv_hi[:, c, :].bitcast(F32), ACT.Copy).then_inc(prep_a, 1)
            act.wait_ge(prep_done, 1)
            program(act, {"x_transpose": high_part(0, 0), "queries": queries, "keys": keys, "values": values,
                          "scores": scores, "weights": weights, "o_transpose": high_part(1, 1),
                          "inner_norm": normalised(INNER, temp), "norm0": normalised(AFTER0, feat),
                          "state_transpose": state_transpose, "neighbours": neighbours, "reset_gate": reset_gate,
                          "reset_parts": reset_parts, "update_gate": update_gate, "new_value": new_value,
                          "state_parts": state_parts, "state_rows": state_rows, "norm1": normalised(AFTER1, feat), "f2_transpose": high_part(3, 1), "features": features,
                          "edges": edges, "edge_exp": edge_exp, "edge_transpose": edge_transpose, "elu": elu,
                          "norm2": normalised(AFTER2, feat), "f3_transpose": high_part(4, 1), "fold": fold,
                          "relate": relate, "squares": squares, "norm3": normalised(AFTER3, out_sb)})

        @block.vector
        def _(dve):
            v = nc.vector

            def f32(t):
                return t.bitcast(F32)

            def whole(t):
                return t[:, :, :].rearrange("p a b -> p (a b)")

            dve.wait_ge(ld_squares, 16 * len(square_loads))
            dve.wait_ge(ident_made, 6 + 2 * len(GROUPS))
            for n in range(3):
                v.tensor_tensor(summed[n], pair_raw[n][:, :, 0:D], pair_raw[n][:, :, D:2 * D], ALU.add) \
                    .then_inc(prep_v, 1)
            v.tensor_scalar(summed[3], square_raw[1], 0.5, None, ALU.mult).then_inc(prep_v, 1)
            dve.wait_ge(prep_v, 4)
            v.tensor_tensor(summed[0], summed[0], summed[1], ALU.subtract).then_inc(prep_v, 1)
            dve.wait_ge(ld_rows, 16 * len(row_loads))
            for c in range(KC):
                for n in range(2):
                    v.tensor_tensor_reduce(out=a_junk, in0=gat_raw[c][:, 0:D], in1=a_row[:, n * D:(n + 1) * D],
                                           scale=1.0, scalar=0.0, op0=ALU.mult, op1=ALU.add,
                                           accum_out=gat_raw[c][:, D + n:D + n + 1]).then_inc(prep_v, 1)
                    dve.wait_ge(prep_v, 5 + 2 * c + n + 1)
            v.tensor_tensor(bias_sum[:, 0:2, :], bias_raw[:, 0:2, :],
                            bias_raw[:, 3:4, :].to_broadcast([P, 2, KC]), ALU.add).then_inc(prep_v, 1)
            v.tensor_tensor(bias_sum[:, 2, :], bias_raw[:, 2, :], bias_raw[:, 4, :], ALU.add).then_inc(prep_v, 1)
            v.tensor_scalar(far_id[:, :], ident[:, :], FAR, None, ALU.mult).then_inc(prep_v, 1)
            v.tensor_scalar(far16[:, :, :], adj_rows(4), 0.0, -FAR, ALU.is_equal, ALU.mult).then_inc(prep_v, 1)
            dve.wait_ge(prep_v, 13)
            v.tensor_scalar(bias_act[:, 0:2, :], bias_sum[:, 0:2, :], 0.5, None, ALU.mult).then_inc(prep_v, 1)
            v.tensor_copy(bias_act[:, 2, :], bias_sum[:, 2, :]).then_inc(prep_v, 1)
            dve.wait_ge(prep_a, 5)
            for c in range(KC):
                v.tensor_tensor(qkv_lo[:, c, :], qkv_raw[c], f32(qkv_hi[:, c, :]), ALU.subtract).then_inc(prep_v, 1)
            v.tensor_tensor(proj_lo[:, :, :], proj_raw, f32(proj_hi[:, :, :]), ALU.subtract) \
                .then_inc(prep_v, 1)
            for c in range(KC):
                v.tensor_tensor(gat_lo[:, c, :], gat_raw[c], f32(gat_hi[:, c, :]), ALU.subtract).then_inc(prep_v, 1)
            dve.wait_ge(prep_v, 20)
            for c in range(KC):
                v.tensor_copy(wa2_hi[:, c, :], f32(gat_hi[:, c, D + 1:D + 2]).to_broadcast([P, P])).then_inc(prep_v, 1)
                v.tensor_copy(wa2_lo[:, c, :], f32(gat_lo[:, c, D + 1:D + 2]).to_broadcast([P, P])).then_inc(prep_v, 1)
            dve.wait_ge(prep_pe, 29)
            v.tensor_copy(adjT16[:, :], ps[:, 7, 0:P]).then_inc(prep_v, 1)
            for place, n in enumerate(WEIGHTS):
                hi, lo = parts_of(n)
                dve.wait_ge(prep_a, 5 + place + 1)
                v.tensor_tensor(lo, ps[:, n, :].rearrange("p (c o) -> p c o", c=KC), f32(hi), ALU.subtract) \
                    .then_inc(prep_v, 1)
            dve.wait_ge(prep_v, 32)
            for g in GROUPS:
                for c in range(KC):
                    v.tensor_copy(mov_lo[g][:, c, 1:3, :].rearrange("p q n -> p (q n)"),
                                  f32(wv_lo[:, c, :])).then_inc(prep_v, 1)
            dve.wait_ge(prep_v, 32 + KC * len(GROUPS))
            dve.wait_ge(prep_a, 12 + KC * len(GROUPS))
            v.memset(a_junk[:, 0:1], 0.0).then_inc(prep_done, 1)

            def low_part(s, b):
                def step(g, trip, _n):
                    dve.wait_ge(t_hi[g], t_hi.at(g, trip, s + 1))
                    v.tensor_tensor(whole(fT_lo[g]), bank(g, b), f32(whole(fT_hi[g])), ALU.subtract) \
                        .then_inc(t_lo[g], 1)
                return step

            def moments(g, n, trip):
                for i in range(GR):
                    last = v.bn_stats(stats[g][:, i, :], resid[g][:, i, :])
                last.then_inc(moment[g], 1)
                dve.wait_ge(moment[g], moment.at(g, trip, 2 * n + 1))
                v.memset(gate_cell[:, :], 0.0)
                for i in range(GR):
                    last = v.bn_aggr(mean_var[g][:, i, :], stats[g][:, i, :])
                last.then_inc(moment[g], 1)

            def queries(g, trip, _n):
                dve.wait_ge(qkv_hid[g], qkv_hid.at(g, trip, 1))
                v.tensor_tensor(whole(q_lo[g]), bank(g, 1), whole(q_hi[g]), ALU.subtract).then_inc(qkv_lod[g], 1)

            def keys(g, trip, _n):
                dve.wait_ge(qkv_hid[g], qkv_hid.at(g, trip, 2))
                v.tensor_tensor(k_lo_flat[g], bank(g, 0), k_hi_flat[g], ALU.subtract).then_inc(qkv_lod[g], 1)

            def values(g, trip, _n):
                dve.wait_ge(qkv_hid[g], qkv_hid.at(g, trip, 3))
                v.tensor_tensor(v_lo[g][:, :, :, 0:HD], bank(g, 1).rearrange("p (i h d) -> p i h d", i=GR, h=HEADS),
                                v_hi[g][:, :, :, 0:HD], ALU.subtract).then_inc(qkv_lod[g], 1)

            def scores(g, trip, i):
                dve.wait_ge(score_ps[g], score_ps.at(g, trip, i + 1))
                v.tensor_reduce(row_max[g][:, :], both_banks(g).rearrange("p b (q m) -> p (b q) m", q=4),
                                AX_X, ALU.max).then_inc(max_step[g], 1)
                dve.wait_ge(max_step[g], max_step.at(g, trip, 2 * i + 1))
                v.tensor_scalar(neg_max[g][:, :], row_max[g][:, :], -SCALE, None, ALU.mult).then_inc(max_step[g], 1)

            def weights(g, trip, i):
                for b in range(2):
                    dve.wait_ge(pT_hid[g], pT_hid.at(g, trip, 2 * i + b + 1))
                    v.tensor_tensor(pT_lo[g][:, 4 * b:4 * b + 4, :], bank(g, b).rearrange("p (s m) -> p s m", s=4),
                                    pT_hi[g][:, 4 * b:4 * b + 4, :], ALU.subtract).then_inc(pT_lod[g], 1)

            def mix(g, trip, i):
                pv = bank(g, 0)[:, 0:HEADS * HW].rearrange("p (h d) -> p h d", h=HEADS)
                dve.wait_ge(pv_ps[g], pv_ps.at(g, trip, i + 1))
                v.reciprocal(inv_sum[g][:, :], pv[:, :, HD]).then_inc(o_step[g], 1)
                dve.wait_ge(o_step[g], o_step.at(g, trip, 2 * i + 1))
                v.tensor_tensor(feat[g][:, i, :].rearrange("p (h d) -> p h d", h=HEADS), pv[:, :, 0:HD],
                                inv_sum[g][:, :].unsqueeze(2).to_broadcast([P, HEADS, HD]), ALU.mult) \
                    .then_inc(o_step[g], 1)

            def project(g, trip, _n):
                dve.wait_ge(proj_ps[g], proj_ps.at(g, trip, 1))
                v.tensor_tensor(resid[g][:, :, :], bank(g, 0).rearrange("p (i d) -> p i d", i=GR),
                                bproj_row[:, :].unsqueeze(1).to_broadcast([P, GR, D]), ALU.add) \
                    .then_inc(proj_done[g], 1)
                dve.wait_ge(proj_done[g], proj_done.at(g, trip, 1))
                moments(g, INNER, trip)

            def add_norm(g, trip, _n):
                dve.wait_ge(inner_done[g], inner_done.at(g, trip, 1))
                moments(g, AFTER0, trip)

            def neighbours(g, trip, t):
                dve.wait_ge(a_hid[g], a_hid.at(g, trip, t + 1))
                v.tensor_tensor(whole(aT_lo[g]), bank(g, 1), f32(whole(aT_hi[g])), ALU.subtract) \
                    .then_inc(a_lod[g], 1)

            def reset_gate(g, trip, t):
                dve.wait_ge(r_done[g], r_done.at(g, trip, t + 1))
                v.scalar_tensor_tensor(flat(rh[g]), flat(tr[g]), 1.0, flat(hT[g]), ALU.add, ALU.mult) \
                    .then_inc(rh_done[g], 1)

            def reset_parts(g, trip, t):
                dve.wait_ge(rh_hid[g], rh_hid.at(g, trip, t + 1))
                v.tensor_tensor(whole(rh_lo[g]), flat(rh[g]), f32(whole(rh_hi[g])), ALU.subtract) \
                    .then_inc(rh_lod[g], 1)

            def blend(g, trip, t):
                dve.wait_ge(hd_done[g], hd_done.at(g, trip, t + 1))
                v.scalar_tensor_tensor(flat(tr[g]), flat(tz[g]), 1.0, flat(tr[g]), ALU.add, ALU.mult) \
                    .then_inc(h_step[g], 1)
                dve.wait_ge(h_step[g], h_step.at(g, trip, 2 * t + 1))
                v.scalar_tensor_tensor(flat(hT[g]), flat(tr[g]), 0.5, flat(hT[g]), ALU.mult, ALU.add) \
                    .then_inc(h_step[g], 1)

            def state_rows(g, trip, t):
                if t < STEPS - 1:
                    dve.wait_ge(h16_hid[g], h16_hid.at(g, trip, t + 1))
                    v.tensor_tensor(flat(h16_lo[g]), bank(g, 1), flat(h16_hi[g]), ALU.subtract) \
                        .then_inc(h16_lod[g], 1)
                else:
                    dve.wait_ge(hn_ps[g], hn_ps.at(g, trip, STEPS))
                    v.tensor_tensor(whole(resid[g]), bank(g, 1), whole(feat[g]), ALU.add).then_inc(resid_done[g], 1)
                    dve.wait_ge(resid_done[g], resid_done.at(g, trip, 1))
                    moments(g, AFTER1, trip)

            def features(g, trip, _n):
                dve.wait_ge(gb_done[g], gb_done.at(g, trip, 1))
                v.tensor_copy(s1[g][:, :], both_banks(g)[:, :, D]).then_inc(s1_done[g], 1)
                v.tensor_tensor(g_lo[g], both_banks(g)[:, :, 0:D], f32(g_hi[g]), ALU.subtract).then_inc(gl_done[g], 1)

            def edges(g, trip, _n):
                dve.wait_ge(s12_done[g], s12_done.at(g, trip, 1))
                v.scalar_tensor_tensor(edge2[g], edge[g], ALPHA, edge[g], ALU.mult, ALU.max).then_inc(edge_step[g], 1)
                dve.wait_ge(edge_step[g], edge_step.at(g, trip, 1))
                v.tensor_tensor(edge2[g], edge2[g], adj_rows(GR), ALU.mult).then_inc(edge_step[g], 1)
                dve.wait_ge(edge_step[g], edge_step.at(g, trip, 2))
                v.tensor_reduce(e_inv[g][:, :], edge2[g], AX_X, ALU.max).then_inc(edge_step[g], 1)
                dve.wait_ge(edge_step[g], edge_step.at(g, trip, 3))
                v.tensor_scalar(e_max[g][:, :], e_inv[g][:, :], -1.0, None, ALU.mult).then_inc(edge_step[g], 1)

            def edge_transpose(g, trip, _n):
                dve.wait_ge(eexp_done[g], eexp_done.at(g, trip, 1))
                v.reciprocal(e_inv[g][:, :], e_sum[g][:, :]).then_inc(einv_done[g], 1)
                dve.wait_ge(eT_hid[g], eT_hid.at(g, trip, 1))
                v.tensor_tensor(eT_lo[g], bank(g, 1)[:, 0:COLS].rearrange("p (i n) -> p i n", i=GR),
                                f32(eT_hi[g]), ALU.subtract).then_inc(eT_lod[g], 1)

            def edge_mix(g, trip, _n):
                dve.wait_ge(einv_done[g], einv_done.at(g, trip, 1))
                dve.wait_ge(gp_ps[g], gp_ps.at(g, trip, 1))
                for i in range(GR):
                    last = v.scalar_tensor_tensor(temp[g][:, i, :], bank(g, 0)[:, i * D:(i + 1) * D],
                                                  e_inv[g][:, i:i + 1], temp[g][:, i, :], ALU.mult, ALU.add)
                last.then_inc(gp_done[g], 1)
                dve.wait_ge(gp_done[g], gp_done.at(g, trip, 1))
                v.tensor_scalar(temp2[g], temp[g], 0.0, None, ALU.min).then_inc(clip_done[g], 1)

            def elu(g, trip, _n):
                dve.wait_ge(elu_exp[g], elu_exp.at(g, trip, 1))
                v.scalar_tensor_tensor(temp[g], temp[g], 0.0, temp2[g], ALU.max, ALU.add).then_inc(elu_done[g], 1)
                dve.wait_ge(elu_done[g], elu_done.at(g, trip, 1))
                v.scalar_tensor_tensor(resid[g][:, :, :], temp[g], -1.0, feat[g][:, :, :], ALU.add, ALU.add) \
                    .then_inc(resid_done[g], 1)
                dve.wait_ge(resid_done[g], resid_done.at(g, trip, 2))
                moments(g, AFTER2, trip)

            def fold(g, trip, _n):
                dve.wait_ge(tq_hid[g], tq_hid.at(g, trip, 1))
                v.tensor_tensor(mov_lo[g][:, :, 0:4:3, :], bank(g, 0).rearrange("p (c q n) -> p c q n", c=KC, q=GR),
                                f32(mov_hi[g][:, :, 0:4:3, :]), ALU.subtract).then_inc(tq_lod[g], 1)

            def relate(g, trip, _n):
                dve.wait_ge(vv_hid[g], vv_hid.at(g, trip, 1))
                v.tensor_tensor(edge[g], banked_relations(g), adj_rows(GR), ALU.mult).then_inc(rel_done[g], 1)
                v.tensor_tensor(g_lo[g], banked_values(g), f32(g_hi[g]), ALU.subtract).then_inc(vv_lod[g], 1)

            def squares(g, trip, _n):
                dve.wait_ge(ss_ps[g], ss_ps.at(g, trip, 1))
                v.tensor_copy(sq_sum[g][:, :], bank(g, 0)[:, 0:2 * GR:2]).then_inc(ss_done[g], 1)

            def relation_mix(g, trip, _n):
                dve.wait_ge(rn_done[g], rn_done.at(g, trip, 1))
                dve.wait_ge(ov_ps[g], ov_ps.at(g, trip, 1))
                for i in range(GR):
                    last = v.scalar_tensor_tensor(resid[g][:, i, :], bank(g, 1)[:, i * D:(i + 1) * D],
                                                  rel_norm[g][:, i:i + 1], feat[g][:, i, :], ALU.mult, ALU.add)
                last.then_inc(resid_done[g], 1)
                dve.wait_ge(resid_done[g], resid_done.at(g, trip, 3))
                moments(g, AFTER3, trip)

            program(dve, {"x_transpose": low_part(0, 0), "queries": queries, "keys": keys, "values": values,
                          "scores": scores, "weights": weights, "mix": mix, "o_transpose": low_part(1, 1),
                          "project": project, "add_norm": add_norm, "neighbours": neighbours, "reset_gate": reset_gate,
                          "reset_parts": reset_parts, "blend": blend, "state_rows": state_rows, 
                          "f2_transpose": low_part(3, 1), "features": features, "edges": edges,
                          "edge_transpose": edge_transpose, "edge_mix": edge_mix, "elu": elu, 
                          "f3_transpose": low_part(4, 1), "fold": fold, "relate": relate, "squares": squares,
                          "relation_mix": relation_mix})


_INS = ['x', 'adj', 'L0_gnn_w_qkv', 'L0_gnn_w_proj', 'L0_gnn_b_proj', 'L0_gnn_ln_gamma', 'L0_gnn_ln_beta',
        'L1_gnn_w3_w', 'L1_gnn_w3_b', 'L1_gnn_u3_w', 'L1_gnn_u3_b', 'L1_gnn_w4_w', 'L1_gnn_w4_b', 'L1_gnn_w5_w',
        'L1_gnn_w5_b', 'L1_gnn_u5_w', 'L1_gnn_u5_b', 'L2_gnn_W', 'L2_gnn_a', 'L2_gnn_beta', 'L3_gnn_Wq', 'L3_gnn_Wk',
        'L3_gnn_Wv']
_OUTS = [((64, 128, 256), 'float32')]


def kernel(**inputs):
    import numpy as _np
    import concourse.bacc as _bacc
    from concourse import mybir as _mybir
    from concourse.bass_utils import run_bass_kernel_spmd as _run

    nc = _bacc.Bacc("TRN2", target_bir_lowering=False, num_devices=1)
    arrays, args = {}, []
    for name in _INS:
        a = _np.ascontiguousarray(inputs[name])
        arrays[f"in_{name}_dram"] = a
        args.append(nc.dram_tensor(f"in_{name}_dram", a.shape, _mybir.dt.from_np(a.dtype), kind="ExternalInput").ap())
    for i, (shape, dtype) in enumerate(_OUTS):
        dt = _mybir.dt.from_np(_np.dtype(dtype))
        args.append(nc.dram_tensor(f"out_{i}_dram", shape, dt, kind="ExternalOutput").ap())
    gnn_stack_kernel(nc, *args)
    r = _run(nc, [arrays], core_ids=[0])
    got = tuple(r.results[0][f"out_{i}_dram"] for i in range(len(_OUTS)))
    return got[0]
```
